# Optimizing a Trainium2 kernel written in Bass

```python
import numpy as np
import jax
import jax.numpy as jnp

def _softmax(x, axis=-1):
    return jax.nn.softmax(x, axis=axis)

def _gelu(x):
    return jax.nn.gelu(x, approximate=True)

def _silu(x):
    return jax.nn.silu(x)

def _sigmoid(x):
    return jax.nn.sigmoid(x)

def _layernorm(x, axis=-1, eps=1e-05):
    m = jnp.mean(x, axis=axis, keepdims=True)
    v = jnp.var(x, axis=axis, keepdims=True)
    return (x - m) / jnp.sqrt(v + eps)

def _scatter_add(tgt, idx, src, axis=0):
    return tgt.at[idx].add(src)

def _segment_sum(src, seg, n):
    return jax.ops.segment_sum(src, seg, n)
kernel_name = 'mk_vit_tower_d1_tok_img256_r4_4c53b4'

def setup_inputs(seed: int=0):
    np.random.seed(seed)
    _w = jnp.asarray

    def _rec_inputs():
        import jax
        import jax.numpy as jnp
        _rk = jax.random.key(seed)
        x = -7.10856e-05 + 0.999911 * jax.random.normal(jax.random.fold_in(_rk, 1), (4, 64, 128, 64), jnp.float32)
        return x
    x = _rec_inputs()

    def _L0_tok_setup():
        import jax, jax.numpy as jnp
        import numpy as np
        PATCH_LEN = 16
        STRIDE = 8
        PAD = 8
        key = jax.random.key(seed)
        k1, k2 = jax.random.split(key)
        x = jax.random.normal(k1, (32, 64, 128, 64), dtype=jnp.float32)
        in_feat = 64 * (PATCH_LEN // 2 + 1) * 2
        W = jax.random.normal(k2, (64, in_feat), dtype=jnp.float32) * 0.02
        return {'x': x, 'W': W}
    _L0_tok_all = _L0_tok_setup()
    _L0_tok_in = {k: v for k, v in _L0_tok_all.items() if k in ('W',)}
    del _L0_tok_all

    def _L0_attn_setup():
        import jax, jax.numpy as jnp
        import numpy as np
        BSZ, L, D, S, K = (8, 1024, 64, 16, 4)
        key = jax.random.key(seed)
        ks = jax.random.split(key, 8)
        sc = 0.02
        return {'x': jax.random.normal(ks[0], (BSZ, L, D), jnp.float32), 'dt': jax.random.normal(ks[1], (D, S), jnp.float32) * 0.01, 'B_w': jax.random.normal(ks[2], (S, D), jnp.float32) * sc, 'C_w': jax.random.normal(ks[3], (D, S), jnp.float32) * sc, 'conv_w': jax.random.normal(ks[4], (D, 1, K), jnp.float32) * sc, 'conv_b': jnp.zeros((D,), jnp.float32), 'in_w': jax.random.normal(ks[5], (2 * D, D), jnp.float32) * sc, 'in_b': jnp.zeros((2 * D,), jnp.float32), 'out_w': jax.random.normal(ks[6], (D, D), jnp.float32) * sc, 'out_b': jnp.zeros((D,), jnp.float32), 'gamma': jnp.ones((D,), jnp.float32), 'beta': jnp.zeros((D,), jnp.float32)}
    _L0_attn_all = _L0_attn_setup()
    _L0_attn_in = {k: v for k, v in _L0_attn_all.items() if k in ('dt', 'B_w', 'C_w', 'conv_w', 'conv_b', 'in_w', 'in_b', 'out_w', 'out_b', 'gamma', 'beta')}
    del _L0_attn_all

    def _L0_ffn_setup():
        import jax, jax.numpy as jnp
        import numpy as np
        B, T, C = (64, 96, 64)
        NH, NKV = (4, 2)
        HD = C // NH
        NREP = NH // NKV
        NE, TOPK = (8, 2)
        HID = int(8 / 3 * C)
        EPS_RMS = 1e-06

        def _rope_tables(t_len):
            inv_freq = 1.0 / 10000.0 ** (np.arange(0, HD, 2, dtype=np.float32) / HD)
            t = np.arange(t_len, dtype=np.float32)
            freqs = np.outer(t, inv_freq)
            emb = np.concatenate([freqs, freqs], axis=-1)
            return (jnp.asarray(np.cos(emb)), jnp.asarray(np.sin(emb)))

        def _rotate_half(x):
            h = x.shape[-1] // 2
            return jnp.concatenate([-x[..., h:], x[..., :h]], axis=-1)

        def _rmsnorm(v, w):
            return v * jax.lax.rsqrt(jnp.mean(v * v, axis=-1, keepdims=True) + EPS_RMS) * w
        key = jax.random.key(seed)
        ks = jax.random.split(key, 10)
        s = lambda k, shape: jax.random.normal(k, shape, jnp.float32) * 0.02
        return {'x': jax.random.normal(ks[0], (B, T, C), jnp.float32), 'ln1_w': jnp.ones((C,), jnp.float32), 'ln2_w': jnp.ones((C,), jnp.float32), 'wq': s(ks[1], (NH * HD, C)), 'wk': s(ks[2], (NKV * HD, C)), 'wv': s(ks[3], (NKV * HD, C)), 'wo': s(ks[4], (C, C)), 'router_w': s(ks[5], (NE, C)), 'w1': s(ks[6], (NE, HID, C)), 'w2': s(ks[7], (NE, C, HID)), 'w3': s(ks[8], (NE, HID, C))}
    _L0_ffn_all = _L0_ffn_setup()
    _L0_ffn_in = {k: v for k, v in _L0_ffn_all.items() if k in ('ln1_w', 'ln2_w', 'wq', 'wk', 'wv', 'wo', 'router_w', 'w1', 'w2', 'w3')}
    del _L0_ffn_all
    return {'x': x, 'L0_tok_W': _L0_tok_in['W'], 'L0_attn_dt': _L0_attn_in['dt'], 'L0_attn_B_w': _L0_attn_in['B_w'], 'L0_attn_C_w': _L0_attn_in['C_w'], 'L0_attn_conv_w': _L0_attn_in['conv_w'], 'L0_attn_conv_b': _L0_attn_in['conv_b'], 'L0_attn_in_w': _L0_attn_in['in_w'], 'L0_attn_in_b': _L0_attn_in['in_b'], 'L0_attn_out_w': _L0_attn_in['out_w'], 'L0_attn_out_b': _L0_attn_in['out_b'], 'L0_attn_gamma': _L0_attn_in['gamma'], 'L0_attn_beta': _L0_attn_in['beta'], 'L0_ffn_ln1_w': _L0_ffn_in['ln1_w'], 'L0_ffn_ln2_w': _L0_ffn_in['ln2_w'], 'L0_ffn_wq': _L0_ffn_in['wq'], 'L0_ffn_wk': _L0_ffn_in['wk'], 'L0_ffn_wv': _L0_ffn_in['wv'], 'L0_ffn_wo': _L0_ffn_in['wo'], 'L0_ffn_router_w': _L0_ffn_in['router_w'], 'L0_ffn_w1': _L0_ffn_in['w1'], 'L0_ffn_w2': _L0_ffn_in['w2'], 'L0_ffn_w3': _L0_ffn_in['w3']}

def reference(x, L0_tok_W, L0_attn_dt, L0_attn_B_w, L0_attn_C_w, L0_attn_conv_w, L0_attn_conv_b, L0_attn_in_w, L0_attn_in_b, L0_attn_out_w, L0_attn_out_b, L0_attn_gamma, L0_attn_beta, L0_ffn_ln1_w, L0_ffn_ln2_w, L0_ffn_wq, L0_ffn_wk, L0_ffn_wv, L0_ffn_wo, L0_ffn_router_w, L0_ffn_w1, L0_ffn_w2, L0_ffn_w3):
    import jax
    import jax.numpy as jnp

    def _L0_tok_ref(x, W):
        import jax, jax.numpy as jnp
        import numpy as np
        PATCH_LEN = 16
        STRIDE = 8
        PAD = 8
        B, C, T, V = x.shape
        xp = jnp.pad(x, ((0, 0), (0, 0), (0, PAD), (0, 0)), mode='edge')
        Tp = T + PAD
        N = (Tp - PATCH_LEN) // STRIDE + 1
        idx = jnp.arange(N)[:, None] * STRIDE + jnp.arange(PATCH_LEN)[None, :]
        patches = xp[:, :, idx, :]
        patches = jnp.transpose(patches, (0, 4, 2, 3, 1))
        xf = jnp.fft.rfft(patches, axis=-2, norm='ortho')
        F = xf.shape[-2]
        x_real = xf.real.reshape(B, V, N, F * C)
        x_imag = xf.imag.reshape(B, V, N, F * C)
        x_emb = jnp.concatenate([x_real, x_imag], axis=-1)
        x_emb = x_emb @ W.T
        return x_emb.reshape(B, V * N, -1)

    def _L0_attn_ref(x, dt, B_w, C_w, conv_w, conv_b, in_w, in_b, out_w, out_b, gamma, beta):
        import jax, jax.numpy as jnp
        import numpy as np
        BSZ, L, D, S, K = (8, 1024, 64, 16, 4)
        d_model = x.shape[-1]
        k = conv_w.shape[-1]
        xr = x @ in_w.T + in_b
        xp, res = jnp.split(xr, 2, axis=-1)
        xc = jnp.transpose(xp, (0, 2, 1))
        xc = jax.lax.conv_general_dilated(xc, conv_w, window_strides=(1,), padding=[(k - 1, 0)], feature_group_count=d_model, dimension_numbers=('NCH', 'OIH', 'NCH'))
        xc = xc + conv_b[None, :, None]
        xconv = jnp.transpose(xc, (0, 2, 1))
        dA = jnp.exp(jnp.einsum('bld,ds->bls', xconv, dt))
        dB = xconv @ B_w.T
        dA_cp = jnp.cumprod(dA, axis=1)
        yc = jnp.cumsum(dA_cp * dB, axis=1)
        y = jnp.concatenate([dB[:, :1], yc[:, 1:] - yc[:, :-1] * dA[:, 1:]], axis=1)
        y = y @ C_w.T
        out = y * jax.nn.silu(res) @ out_w.T + out_b
        out = out + xconv
        mean = out.mean(axis=(0, 1))
        var = jnp.mean((out - mean) ** 2, axis=(0, 1))
        out = (out - mean) * jax.lax.rsqrt(var + 1e-05) * gamma + beta
        return out

    def _L0_ffn_ref(x, ln1_w, ln2_w, wq, wk, wv, wo, router_w, w1, w2, w3):
        import jax, jax.numpy as jnp
        import numpy as np
        B, T, C = (64, 96, 64)
        NH, NKV = (4, 2)
        HD = C // NH
        NREP = NH // NKV
        NE, TOPK = (8, 2)
        HID = int(8 / 3 * C)
        EPS_RMS = 1e-06

        def _rope_tables(t_len):
            inv_freq = 1.0 / 10000.0 ** (np.arange(0, HD, 2, dtype=np.float32) / HD)
            t = np.arange(t_len, dtype=np.float32)
            freqs = np.outer(t, inv_freq)
            emb = np.concatenate([freqs, freqs], axis=-1)
            return (jnp.asarray(np.cos(emb)), jnp.asarray(np.sin(emb)))

        def _rotate_half(x):
            h = x.shape[-1] // 2
            return jnp.concatenate([-x[..., h:], x[..., :h]], axis=-1)

        def _rmsnorm(v, w):
            return v * jax.lax.rsqrt(jnp.mean(v * v, axis=-1, keepdims=True) + EPS_RMS) * w
        Bx, Tx, Cx = x.shape
        h = _rmsnorm(x, ln1_w)
        q = (h @ wq.T).reshape(Bx, Tx, NH, HD).transpose(0, 2, 1, 3)
        k = (h @ wk.T).reshape(Bx, Tx, NKV, HD).transpose(0, 2, 1, 3)
        v = (h @ wv.T).reshape(Bx, Tx, NKV, HD).transpose(0, 2, 1, 3)
        cos, sin = _rope_tables(Tx)
        cos, sin = (cos[None, None], sin[None, None])
        q = q * cos + _rotate_half(q) * sin
        k = k * cos + _rotate_half(k) * sin
        k = jnp.repeat(k, NREP, axis=1)
        v = jnp.repeat(v, NREP, axis=1)
        scores = jnp.einsum('bhtd,bhsd->bhts', q, k) / jnp.sqrt(jnp.float32(HD))
        causal = jnp.tril(jnp.ones((Tx, Tx), dtype=bool))
        scores = jnp.where(causal[None, None], scores, jnp.float32(-1e+30))
        att = jax.nn.softmax(scores, axis=-1)
        y = jnp.einsum('bhts,bhsd->bhtd', att, v).transpose(0, 2, 1, 3).reshape(Bx, Tx, Cx)
        x = x + y @ wo.T
        flat = _rmsnorm(x, ln2_w).reshape(-1, Cx)
        probs = jax.nn.softmax(flat @ router_w.T, axis=-1)
        tp, ti = jax.lax.top_k(probs, TOPK)
        tp = tp / (jnp.sum(tp, axis=-1, keepdims=True) + 1e-09)
        weights = jnp.sum(tp[..., None] * jax.nn.one_hot(ti, NE, dtype=flat.dtype), axis=1)
        out = jnp.zeros_like(flat)
        for e in range(NE):
            hh = jax.nn.silu(flat @ w1[e].T) * (flat @ w3[e].T)
            out = out + weights[:, e:e + 1] * (hh @ w2[e].T)
        return x + out.reshape(Bx, Tx, Cx)
    h = _L0_tok_ref(x, L0_tok_W)
    h = h + _L0_attn_ref(_layernorm(h, axis=-1), L0_attn_dt, L0_attn_B_w, L0_attn_C_w, L0_attn_conv_w, L0_attn_conv_b, L0_attn_in_w, L0_attn_in_b, L0_attn_out_w, L0_attn_out_b, L0_attn_gamma, L0_attn_beta)
    h = h + _L0_ffn_ref(_layernorm(h, axis=-1), L0_ffn_ln1_w, L0_ffn_ln2_w, L0_ffn_wq, L0_ffn_wk, L0_ffn_wv, L0_ffn_wo, L0_ffn_router_w, L0_ffn_w1, L0_ffn_w2, L0_ffn_w3)
    return h

_drawn_inputs = setup_inputs


def setup_inputs(seed=0):
    import zlib

    import numpy as np

    out = dict(_drawn_inputs(seed))
    spreads = {'L0_attn_conv_b': (0.0, 0.1),
     'L0_attn_in_b': (0.0, 0.1),
     'L0_attn_out_b': (0.0, 0.8),
     'L0_attn_gamma': (1.0, 0.2),
     'L0_attn_beta': (0.0, 0.1),
     'L0_ffn_ln1_w': (1.0, 0.6),
     'L0_ffn_ln2_w': (1.0, 0.6)}
    factors = {'L0_ffn_wq': 8.0,
     'L0_ffn_wk': 8.0,
     'L0_ffn_wv': 8.0,
     'L0_ffn_wo': 8.0,
     'L0_ffn_router_w': 8.0,
     'L0_ffn_w1': 8.0,
     'L0_ffn_w2': 8.0,
     'L0_ffn_w3': 8.0}
    for name, (base, spread) in spreads.items():
        noise = np.random.default_rng([zlib.crc32(name.encode()), seed]).standard_normal(out[name].shape)
        drawn = base * np.exp(spread * noise) if base else spread * noise
        out[name] = jnp.asarray(drawn.astype(out[name].dtype))
    for name, factor in factors.items():
        out[name] = (out[name] * factor).astype(out[name].dtype)
    return out
```

```python
from contextlib import ExitStack

import numpy as np

import concourse.bass as bass
from concourse import mybir

ALU = mybir.AluOpType
ACT = mybir.ActivationFunctionType
AX = mybir.AxisListType
F32 = mybir.dt.float32
F32R = mybir.dt.float32r
BF16 = mybir.dt.bfloat16

P = 128
BATCH, CHAN, TIME, VARS = 4, 64, 128, 64
PATCH, STRIDE = 16, 8
NPATCH = TIME // STRIDE
TOK = VARS * NPATCH
PAIRS = BATCH // 2
HALF = TOK // 2
NM = NPATCH // 2
NFREQ = PATCH // 2 + 1
STATE = 16
TAPS = 4
HEADS, KV, HD = 4, 2, 16
SBLK = TOK // P
EXPERTS, HID = 8, 170
EPAIRS = EXPERTS // 2
HTILES = 3
REST = HID - P
CHUNKS = BATCH * 2
NEG = -1e30

PARAMS = [("in_x", 128), ("in_r", 128), ("ssm_dt", 32), ("ssm_B", 32), ("ssm_C", 128), ("out_w", 128),
          ("wq", 128), ("wq_rot", 128), ("wk", 64), ("wk_rot", 64), ("wv", 32), ("wo", 64), ("router", 8),
          ("conv_w", 4), ("conv_b", 1), ("in_b_x", 1), ("in_b_r", 1), ("out_b", 1), ("gamma", 1), ("beta", 1),
          ("ln1", 1), ("ln2", 1),
          ("center", 128), ("chan_mean", 128), ("bn_mean", 128), ("den_sel", 128), ("ident", 128),
          ("ident2", 64), ("expert_id", 8), ("eps5", 1), ("eps6", 1)]


def param_columns():
    at, out = 0, {}
    for name, width in PARAMS:
        out[name] = (at, width)
        at += width
    return out, at


def score_units():
    units = [(0, 0, 4), (1, 0, 4)]
    for tb in (2, 3):
        units += [(tb, 0, 2), (tb, 2, 2)]
    for tb in range(4, SBLK):
        units += [(tb, h, 1) for h in range(HEADS)]
    return units


def prob_chunks(j):
    t = P * j
    return [(t, HALF), (HALF, TOK)] if t < HALF else [(t, TOK)]


def vit_tower(nc, x, tok_W, params_d, dft_d, rope_d, masks_d, w1_d, w3_d, w2_d, out):
    cols, NPARAM = param_columns()
    units = score_units()
    NU = len(units)
    NCH = sum(len(prob_chunks(j)) for j in range(SBLK)) * HEADS

    with ExitStack() as ctx:
        def sb(name, shape, dt=F32):
            return ctx.enter_context(nc.sbuf_tensor(name, shape, dt))

        def sem(name):
            return ctx.enter_context(nc.semaphore(name))

        ps = ctx.enter_context(nc.psum_tensor("ps", [P, 8, 512], F32))
        psf = ps[:].rearrange("p a b -> p (a b)")

        XSLOT = (NM + 1) * STRIDE * VARS
        early = sb("early", [P, 3 * XSLOT])
        work = sb("work", [P, 12 * TOK])
        params = sb("params", [P, NPARAM])
        masks = sb("masks", [P, 3, P], BF16)
        spec = sb("spec", [P, 3, STRIDE, CHAN])
        H = sb("H", [P, PAIRS, TOK])
        mix = sb("mix", [P, PAIRS, TOK])
        high = sb("high", [P, PAIRS, TOK], F32R)
        low = sb("low", [P, PAIRS, TOK], F32R)
        khigh = sb("khigh", [P, TOK], F32R)
        klow = sb("klow", [P, TOK], F32R)
        QT = sb("QT", [P, 2, KV, TOK], F32R)
        KT = sb("KT", [P, 2, HEADS, TOK], F32R)
        small = sb("small", [P, 64])
        negmax = sb("negmax", [32, 2, P], F32R)
        w_dram = nc.dram_tensor("routing_weights", [EXPERTS, BATCH * TOK], F32, kind="Internal").ap()

        def par(name, rows=slice(0, P)):
            a, w = cols[name]
            return params[rows, a:a + w]

        xs = [early[:, XSLOT * i:XSLOT * (i + 1)].rearrange("p (m r v) -> p m r v", r=STRIDE, v=VARS) for i in range(3)]
        normed = early[:, 0:2 * TOK].rearrange("p (a t) -> p a t", a=PAIRS)
        V = early[:, 2 * TOK:4 * TOK].rearrange("p (b j g d) -> p b j g d", b=BATCH, j=SBLK, g=KV)
        PT = early[:, 4 * TOK:12 * TOK].rearrange("p (i h t) -> p i h t", i=2, h=HEADS)
        gates = early[:, 4 * TOK:12 * TOK].rearrange("p (i q t) -> p i q t", i=2, q=EPAIRS)
        w2 = early[:, 12 * TOK:13 * TOK].rearrange("p (q s o) -> p q s o", q=EPAIRS, s=4)

        def wk_tile(i):
            return work[:, i * TOK:(i + 1) * TOK]

        sq, rstd, hn = wk_tile(0), wk_tile(1), wk_tile(2)
        xpad = work[:, 3 * TOK:4 * TOK + TAPS - 1]
        sres, xconv, cprod, csum, zeros = wk_tile(5), wk_tile(6), wk_tile(7), wk_tile(8), wk_tile(9)
        gated, shifted, dA = sq, rstd, hn
        tokW = work[0:2 * NFREQ, 5 * TOK:9 * TOK].rearrange("k (o c) -> k o c", o=CHAN)
        dft = work[0:2 * NFREQ, 4 * TOK + 64:4 * TOK + 64 + PATCH]
        cos_t, sin_t = wk_tile(10), wk_tile(11)
        attn_o, rden, attn_n = wk_tile(0), wk_tile(1), wk_tile(2)
        w1_raw = work[:, 6 * TOK:6 * TOK + 1536]
        w3_raw = work[:, 6 * TOK + 1536:9 * TOK]
        flat = work[:, 0:2 * TOK].rearrange("p (a t) -> p a t", a=PAIRS)
        silu1 = work[:, 2 * TOK:3 * TOK].rearrange("p (i t) -> p i t", i=2)
        hid = work[:, 3 * TOK:4 * TOK].rearrange("p (i t) -> p i t", i=2)
        gated_y = work[:, 4 * TOK:5 * TOK].rearrange("p (i t) -> p i t", i=2)
        final = work[:, 5 * TOK:5 * TOK + 512].rearrange("p (i b o) -> p i b o", i=2, b=4)
        wT = work[0:32, 5 * TOK + 512:6 * TOK].rearrange("p (k s) -> p k s", k=4)
        sq3, inv3 = wk_tile(9), wk_tile(10)
        rt = [work[:, 11 * TOK + P * i:11 * TOK + P * (i + 1)].rearrange("p (b e) -> p b e", e=EXPERTS)
              for i in range(7)]
        kt_flat = KT[:].rearrange("p i h t -> p (i h t)")
        w_parts = [kt_flat[:, 1536 * i:1536 * (i + 1)].rearrange("p (q i c) -> p q i c", q=EPAIRS, i=HTILES)
                   for i in range(4)]
        tok_parts = QT[:].rearrange("p i g t -> p (i g t)")

        sums, sqs, tot, vtot = small[:, 0:2], small[:, 2:4], small[:, 4:5], small[:, 5:6]
        negmean, bnscale = small[:, 6:7], small[:, 7:8]
        maxima = small[:, 8:40].rearrange("p (h b) -> p h b", h=HEADS)
        r_m, r_min, r_m2, r_den = (work[:, 11 * TOK + 7 * P + 16 * i:11 * TOK + 7 * P + 16 * (i + 1)] for i in range(4))

        params_in = sem("params_in"); tokw_in = sem("tokw_in"); rope_in = sem("rope_in"); masks_in = sem("masks_in")
        x_in = [sem(f"x_in{b}") for b in range(BATCH)]
        weff_ready = sem("weff_ready"); weff_placed = sem("weff_placed")
        patches_ready = sem("patches_ready"); h_ready = sem("h_ready")
        centered = sem("centered"); sq_ready = sem("sq_ready"); var_ready = sem("var_ready")
        rstd_ready = sem("rstd_ready"); hn_ready = sem("hn_ready"); xp_ready = sem("xp_ready")
        res_ready = sem("res_ready"); sres_ready = sem("sres_ready"); xconv_ready = sem("xconv_ready")
        ssm_ready = sem("ssm_ready"); dA_ready = sem("dA_ready"); y_ready = sem("y_ready")
        cy_ready = sem("cy_ready"); g_ready = sem("g_ready"); outw_ready = sem("outw_ready"); o_ready = sem("o_ready")
        tot_ready = sem("tot_ready"); bnmean_ready = sem("bnmean_ready"); negmean_ready = sem("negmean_ready")
        sqs_ready = sem("sqs_ready"); vtot_ready = sem("vtot_ready"); bnvar_ready = sem("bnvar_ready")
        bnrstd_ready = sem("bnrstd_ready"); h2_ready = sem("h2_ready")
        centered2 = sem("centered2"); sq2_ready = sem("sq2_ready"); var2_ready = sem("var2_ready")
        s2_ready = sem("s2_ready"); ms_ready = sem("ms_ready"); r_ready = sem("r_ready"); hr_ready = sem("hr_ready")
        q_ready = sem("q_ready"); q_taken = sem("q_taken"); q_split = sem("q_split")
        k_ready = sem("k_ready"); k_taken = sem("k_taken"); k_split = sem("k_split")
        v_ready = sem("v_ready"); v_placed = sem("v_placed"); v_blank = sem("v_blank"); kt_blank = sem("kt_blank")
        qk_in = [sem(f"qk_in{i}") for i in range(2)]; m_in = [sem(f"m_in{i}") for i in range(2)]
        scores_ready = sem("scores_ready"); maxed = sem("maxed")
        max_turned = sem("max_turned"); negmax_ready = sem("negmax_ready")
        logits_t = sem("logits_t"); probs_ready = sem("probs_ready"); pv_done = sem("pv_done")
        o_out = sem("o_out"); den_ready = sem("den_ready"); rden_ready = sem("rden_ready")
        attn_ready = sem("attn_ready"); wo_ready = sem("wo_ready"); x1_ready = sem("x1_ready")
        moe_w_in = sem("moe_w_in"); w2_in = sem("w2_in"); w_high = sem("w_high"); w_low = sem("w_low")
        sq3_ready = sem("sq3_ready"); var3_ready = sem("var3_ready"); inv3_ready = sem("inv3_ready")
        flat_ready = sem("flat_ready"); split3 = sem("split3"); tok_in = [sem(f"tok_in{b}") for b in range(BATCH)]; base_ready = sem("base_ready")
        logit_ready = sem("logit_ready"); rdiff = sem("rdiff"); rexp = sem("rexp"); rw_ready = sem("rw_ready")
        wT_ready = sem("wT_ready"); wT_out = sem("wT_out"); w_stored = sem("w_stored")
        gates_in = [sem(f"gates_in{i}") for i in range(2)]
        h1_ready = sem("h1_ready"); h3_ready = sem("h3_ready"); silu_ready = sem("silu_ready"); hid_ready = sem("hid_ready")
        y2_ready = sem("y2_ready"); gy_ready = sem("gy_ready"); fin_ready = sem("fin_ready"); fin_out = sem("fin_out")
        hid_used = sem("hid_used"); gy_used = sem("gy_used")
        stored = [sem(f"stored{i}") for i in range(2)]
        dve_step = sem("dve_step"); act_step = sem("act_step"); pool_step = sem("pool_step")

        block = ctx.enter_context(nc.Block())

        @block.sync
        def _(sp):
            def load_x(b):
                v = x[b].rearrange("c (m s r) v -> s c m (r v)", s=2, r=STRIDE)
                for s in range(2):
                    rows = slice(CHAN * s, CHAN * (s + 1))
                    sp.dma_start(xs[b % 3][rows, 0:NM].rearrange("p m r v -> p m (r v)"), v[s]).then_inc(x_in[b], 16)
                    sp.dma_start(xs[b % 3][rows, NM],
                                 x[b, :, TIME - 1:TIME, :].broadcast_to([CHAN, STRIDE, VARS])).then_inc(x_in[b], 16)

            load_x(0)
            load_x(1)
            load_x(2)
            sp.wait_ge(patches_ready, 1)
            load_x(3)
            for b in range(BATCH):
                p, h0, buf = b // 2, CHAN * (b % 2), b % 2
                sp.wait_ge(q_split, p + 1)
                sp.wait_ge(k_split, p + 1)
                if b == 0:
                    sp.wait_ge(kt_blank, 1)
                if b >= 2:
                    sp.wait_ge(logits_t, NCH * (b - 1))
                for g in range(KV):
                    src = slice(h0 + 32 * g, h0 + 32 * (g + 1))
                    for grp, part in enumerate((high, high, low)):
                        sp.dma_start(QT[32 * grp:32 * grp + 32, buf, g, :].bitcast(F32), part[src, p, :].bitcast(F32)).then_inc(qk_in[buf], 16)
                for h in range(HEADS):
                    row = 64 * p + 32 * (b % 2) + HD * (h // 2)
                    for grp, part in enumerate((khigh, klow, khigh)):
                        at = 32 * grp + HD * (h % 2)
                        sp.dma_start(KT[at:at + HD, buf, h, :].bitcast(F32), part[row:row + HD, :].bitcast(F32)).then_inc(qk_in[buf], 16)
            for b in range(BATCH):
                p, rows = b // 2, slice(CHAN * (b % 2), CHAN * (b % 2) + CHAN)
                if b % 2 == 0:
                    sp.wait_ge(split3, p + 1)
                    if b == 0:
                        sp.wait_ge(logits_t, NCH * BATCH)
                sp.dma_start(tok_parts[0:CHAN, TOK * b:TOK * (b + 1)].bitcast(F32), high[rows, p, :].bitcast(F32)).then_inc(tok_in[b], 16)
                sp.dma_start(tok_parts[CHAN:P, TOK * b:TOK * (b + 1)].bitcast(F32), low[rows, p, :].bitcast(F32)).then_inc(tok_in[b], 16)
            for k in range(CHUNKS):
                sp.wait_ge(fin_out, k + 1)
                sp.dma_start(out[k // 2, HALF * (k % 2):HALF * (k % 2 + 1), :].rearrange("(b s) o -> s b o", b=4),
                             final[:, k % 2]).then_inc(stored[k % 2], 16)
            for i in range(2):
                sp.wait_ge(stored[i], 8 * CHUNKS)

        @block.gpsimd
        def _(pool):
            pool.memset(zeros, 0.0).then_inc(pool_step, 1)
            pool.memset(xpad[:, 0:TAPS - 1], 0.0).then_inc(pool_step, 1)
            pool.memset(kt_flat.bitcast(F32), 0.0).then_inc(pool_step, 1)
            pool.wait_ge(pool_step, 3)
            for h in range(HEADS):
                kh = KT[:, :, h, :].bitcast(F32)
                if h % 2 == 0:
                    pool.memset(kh[96:98], 1.0).then_inc(pool_step, 1)
                else:
                    pool.memset(kh[96:100], 1.0).then_inc(pool_step, 1)
            pool.wait_ge(pool_step, 3 + HEADS)
            for h in (1, 3):
                pool.memset(KT[96:98, :, h, :].bitcast(F32), 0.0).then_inc(pool_step, 1)
            pool.wait_ge(pool_step, 5 + HEADS)
            pool.memset(small[:, 60:61], 0.0).then_inc(kt_blank, 1)
            pool.wait_ge(patches_ready, BATCH)
            pool.memset(V.rearrange("p b j g d -> p (b j g) d")[:, :, HD:32], 0.0).then_inc(pool_step, 1)
            pool.wait_ge(pool_step, 6 + HEADS)
            pool.memset(V.rearrange("p b j g d -> p (b j g) d")[:, :, HD:HD + 1], 1.0).then_inc(v_blank, 1)
            for b in range(BATCH):
                pool.wait_ge(negmax_ready, 2 * (b + 1))
                if b >= 2:
                    pool.wait_ge(logits_t, NCH * (b - 1))
                for h in range(HEADS):
                    for part in range(2):
                        at = 96 + 2 * (h % 2) + part
                        pool.dma_start(QT[at:at + 1, b % 2, h // 2, :].rearrange("p (b s) -> p b s", s=P).bitcast(F32),
                                       negmax[SBLK * h:SBLK * (h + 1), part, :].bitcast(F32)).then_inc(m_in[b % 2], 16)
            for p in range(PAIRS):
                pool.wait_ge(wT_out, p + 1)
                for blk in range(4):
                    pool.dma_start(
                        w_dram[:, 2 * TOK * p:2 * TOK * (p + 1)].rearrange("e (k b s) -> b e k s", k=4, b=4)[blk],
                        wT[EXPERTS * blk:EXPERTS * (blk + 1)]).then_inc(w_stored, 16)
                pool.wait_ge(w_stored, 64 * (p + 1))
                for b in (2 * p, 2 * p + 1):
                    if b == 0:
                        pool.wait_ge(pv_done, SBLK * BATCH)
                    if b >= 2:
                        pool.wait_ge(gy_ready, 2 * EPAIRS * (b - 1))
                    for e in range(EXPERTS):
                        pool.dma_start(gates[CHAN * (e % 2):CHAN * (e % 2 + 1), b % 2, e // 2, :],
                                       w_dram[e:e + 1, TOK * b:TOK * (b + 1)].broadcast_to([CHAN, TOK])
                                       ).then_inc(gates_in[b % 2], 16)

        @block.scalar
        def _(act):
            done = [0]

            def settle(ins):
                done[0] += 1
                ins.then_inc(act_step, 1)
                act.wait_ge(act_step, done[0])

            act.dma_start(tokW, tok_W.rearrange("o (k c) -> k o c", c=CHAN)).then_inc(tokw_in, 16)
            act.dma_start(dft, dft_d).then_inc(tokw_in, 16)
            act.dma_start(params[:], params_d).then_inc(params_in, 16)
            act.dma_start(masks[:], masks_d.rearrange("m p s -> p m s")).then_inc(masks_in, 16)
            act.dma_start(cos_t, rope_d[0]).then_inc(rope_in, 16)
            act.dma_start(sin_t, rope_d[1]).then_inc(rope_in, 16)
            act.preload_act_table_set("natural_log_exp_and_others")
            act.wait_ge(params_in, 16)

            def patches_out(b):
                act.wait_ge(patches_ready, b + 1)
                dst = H[CHAN * (b % 2):CHAN * (b % 2 + 1), b // 2, :].rearrange("c (v m two) -> c two m v", m=NM, two=2)
                for two in range(2):
                    act.activation(dst[:, two], ps[CHAN * two:CHAN * (two + 1), b, :].rearrange("c (m v) -> c m v", v=VARS),
                                   ACT.Copy).then_inc(h_ready, 1)

            def inv_sqrt(dst, src, eps):
                settle(act.activation(dst, src, ACT.Ln, bias=par(eps)))
                return act.activation(dst, dst, ACT.Exp, scale=-0.5)

            def mixer(p):
                rows = slice(32 * p, 32 * p + 32)
                act.wait_ge(centered, p + 1)
                if p:
                    act.wait_ge(outw_ready, p)
                act.activation(sq, psf[:, 4 * 512:6 * 512], ACT.Square).then_inc(sq_ready, 1)
                act.wait_ge(var_ready, p + 1)
                if p:
                    act.wait_ge(y_ready, p)
                inv_sqrt(rstd, psf[:, 6 * 512:8 * 512], "eps5").then_inc(rstd_ready, 1)
                act.wait_ge(res_ready, p + 1)
                act.wait_ge(weff_ready, 1)
                act.activation(sres, psf[:, 6 * 512:8 * 512], ACT.Silu, bias=par("in_b_r")).then_inc(sres_ready, 1)
                act.preload_act_table_set("natural_log_exp_and_others")
                act.wait_ge(ssm_ready, p + 1)
                act.activation(dA[rows], psf[rows, 4 * 512:6 * 512], ACT.Exp).then_inc(dA_ready, 1)

            patches_out(0)
            patches_out(1)
            mixer(0)
            patches_out(2)
            patches_out(3)
            mixer(1)

            act.wait_ge(negmean_ready, 1)
            for p in range(PAIRS):
                act.activation(wk_tile(p), mix[:, p, :], ACT.Square, bias=negmean,
                               accum_out=sqs[:, p:p + 1]).then_inc(sqs_ready, 1)
            act.wait_ge(bnvar_ready, 1)
            inv_sqrt(bnscale, ps[:, 5, 0:1], "eps5").then_inc(bnrstd_ready, 1)

            for p in range(PAIRS):
                b0 = 4 * p * 512
                act.wait_ge(centered2, p + 1)
                if p == 0:
                    act.wait_ge(sqs_ready, 2)
                act.activation(wk_tile(4 * p), psf[:, b0:b0 + 1024], ACT.Square).then_inc(sq2_ready, 1)
                act.wait_ge(var2_ready, p + 1)
                inv_sqrt(wk_tile(4 * p + 1), psf[:, b0 + 1024:b0 + 2048], "eps5").then_inc(s2_ready, 1)
                act.wait_ge(ms_ready, p + 1)
                inv_sqrt(wk_tile(4 * p + 2), wk_tile(4 * p + 2), "eps6").then_inc(r_ready, 1)
            for p in range(PAIRS):
                act.wait_ge(v_ready, p + 1)
                act.wait_ge(v_blank, 1)
                act.activation(V[:, 2 * p:2 * p + 2, :, :, 0:HD].rearrange("p b j g d -> p b (j g) d"),
                               ps[:, 4 * p:4 * p + 2, 0:256].rearrange("p b (n d) -> p b n d", d=HD), ACT.Copy).then_inc(v_placed, 1)

            act.wait_ge(k_split, PAIRS)
            act.wait_ge(v_ready, PAIRS)
            for rows in (slice(0, CHAN), slice(CHAN, P)):
                act.dma_start(w1_raw[rows], w1_d).then_inc(moe_w_in, 16)
                act.dma_start(w3_raw[rows], w3_d).then_inc(moe_w_in, 16)
            act.wait_ge(patches_ready, BATCH)
            act.dma_start(w2.rearrange("p q s o -> p (q s o)"), w2_d).then_inc(w2_in, 16)
            n = 0
            for b in range(BATCH):
                for j in range(SBLK):
                    for h in range(HEADS):
                        if h == 0 and SBLK * b + j >= 2:
                            act.wait_ge(pv_done, SBLK * b + j - 1)
                        for t0, t1 in prob_chunks(j):
                            act.wait_ge(logits_t, n + 1)
                            act.activation(PT[:, j % 2, h, t0:t1], ps[:, 4 + n % 2, 0:t1 - t0], ACT.Exp,
                                           scale=float(HD) ** -0.5).then_inc(probs_ready, 1)
                            n += 1
                    if j == 0 and b:
                        act.wait_ge(den_ready, b)
                        if b >= 2:
                            act.wait_ge(attn_ready, b - 1)
                        settle(act.activation(rden, psf[:, 6 * 512:8 * 512], ACT.Ln))
                        act.activation(rden, rden, ACT.Exp, scale=-1.0).then_inc(rden_ready, 1)
                act.wait_ge(pv_done, SBLK * (b + 1))
                if b:
                    act.wait_ge(attn_ready, b)
                act.activation(attn_o, psf[:, 6 * 512:8 * 512], ACT.Copy).then_inc(o_out, 1)
            act.wait_ge(den_ready, BATCH)
            settle(act.activation(rden, psf[:, 6 * 512:8 * 512], ACT.Ln))
            act.activation(rden, rden, ACT.Exp, scale=-1.0).then_inc(rden_ready, 1)

            act.wait_ge(moe_w_in, 64)
            act.wait_ge(logits_t, NCH * BATCH)
            for i, raw in enumerate((w1_raw, w3_raw)):
                act.activation(kt_flat[:, 3072 * i:3072 * i + 1536], raw, ACT.Copy).then_inc(w_high, 1)

            for p in range(PAIRS):
                act.wait_ge(x1_ready, 2 * (p + 1))
                if p:
                    act.wait_ge(var3_ready, p)
                act.activation(sq3, mix[:, p, :], ACT.Square).then_inc(sq3_ready, 1)
                act.wait_ge(var3_ready, p + 1)
                if p:
                    act.wait_ge(flat_ready, p)
                inv_sqrt(inv3, psf[:, 0:1024], "eps6").then_inc(inv3_ready, 1)
                act.wait_ge(rdiff, p + 1)
                act.activation(rt[1], rt[1], ACT.Exp).then_inc(rexp, 1)
                act.wait_ge(wT_ready, p + 1)
                if p:
                    act.wait_ge(w_stored, 64 * p)
                act.activation(wT, ps[0:32, 4, :].rearrange("p (k s) -> p k s", k=4), ACT.Copy).then_inc(wT_out, 1)

            def rows_out(k):
                act.wait_ge(fin_ready, k + 1)
                if k >= 2:
                    act.wait_ge(stored[k % 2], 16 * (k // 2))
                act.activation(final[:, k % 2], ps[:, 6 + k % 2, 0:256].rearrange("p (b o) -> p b o", b=4),
                               ACT.Copy).then_inc(fin_out, 1)

            per_chunk = EPAIRS * HTILES
            for n in range(CHUNKS * per_chunk):
                act.wait_ge(h1_ready, n + 1)
                if n >= 2:
                    act.wait_ge(hid_ready, n - 1)
                act.activation(silu1[:, n % 2, :], ps[:, n % 2, :], ACT.Silu).then_inc(silu_ready, 1)
                if n > per_chunk and n % per_chunk == 4:
                    rows_out(n // per_chunk - 1)
            rows_out(CHUNKS - 1)

        @block.vector
        def _(dve):
            done = [0]

            def settle(ins):
                done[0] += 1
                ins.then_inc(dve_step, 1)
                dve.wait_ge(dve_step, done[0])

            settle(dve.memset(spec[:], 0.0))
            dve.wait_ge(weff_ready, 1)
            for bank in range(2):
                src = ps[:, 6 + bank, :].rearrange("p (o r) -> p r o", r=PATCH)
                osl = slice(32 * bank, 32 * bank + 32)
                lo, hi = slice(0, CHAN), slice(CHAN, P)
                dve.tensor_copy(spec[lo, 0, :, osl], src[lo, 0:STRIDE]).then_inc(weff_placed, 1)
                dve.tensor_copy(spec[hi, 0, :, osl], src[hi, STRIDE:PATCH]).then_inc(weff_placed, 1)
                dve.tensor_copy(spec[hi, 1, :, osl], src[hi, 0:STRIDE]).then_inc(weff_placed, 1)
                dve.tensor_copy(spec[lo, 2, :, osl], src[lo, STRIDE:PATCH]).then_inc(weff_placed, 1)
            dve.wait_ge(params_in, 16)

            def mixer(p):
                rows = slice(32 * p, 32 * p + 32)
                lo4, lo6 = psf[:, 4 * 512:6 * 512], psf[:, 6 * 512:8 * 512]
                dve.wait_ge(rstd_ready, p + 1)
                dve.tensor_tensor(hn, lo4, rstd, ALU.mult).then_inc(hn_ready, 1)
                dve.wait_ge(xp_ready, p + 1)
                dve.wait_ge(pool_step, 2)
                settle(dve.tensor_scalar(xpad[:, TAPS - 1:], lo4, par("in_b_x"), None, ALU.add))
                cw = par("conv_w")
                dve.wait_ge(weff_placed, 8)
                settle(dve.tensor_scalar(xconv, xpad[:, 0:TOK], cw[:, 0:1], par("conv_b"), ALU.mult, ALU.add))
                for k in range(1, TAPS):
                    ins = dve.scalar_tensor_tensor(xconv, xpad[:, k:k + TOK], cw[:, k:k + 1], xconv, ALU.mult, ALU.add)
                    if k < TAPS - 1:
                        settle(ins)
                ins.then_inc(xconv_ready, 1)
                dve.wait_ge(dA_ready, p + 1)
                settle(dve.tensor_tensor_scan(cprod[rows], dA[rows], zeros[rows], 1.0, ALU.mult, ALU.add))
                settle(dve.tensor_tensor(cprod[rows], cprod[rows], lo6[rows], ALU.mult))
                settle(dve.tensor_tensor_scan(csum[rows], cprod[rows], zeros[rows], 0.0, ALU.add, ALU.add))
                settle(dve.tensor_tensor(shifted[rows, 1:], csum[rows, 0:TOK - 1], dA[rows, 1:], ALU.mult))
                settle(dve.tensor_copy(cprod[rows, 0:1], lo6[rows, 0:1]))
                dve.tensor_tensor(cprod[rows, 1:], csum[rows, 1:], shifted[rows, 1:], ALU.subtract).then_inc(y_ready, 1)
                dve.wait_ge(cy_ready, p + 1)
                dve.wait_ge(sres_ready, p + 1)
                dve.tensor_tensor(gated, lo4, sres, ALU.mult).then_inc(g_ready, 1)
                dve.wait_ge(outw_ready, p + 1)
                dve.wait_ge(xconv_ready, p + 1)
                dve.scalar_tensor_tensor(mix[:, p, :], lo6, par("out_b"), xconv, ALU.add, ALU.add,
                                         accum_out=sums[:, p:p + 1]).then_inc(o_ready, 1)

            mixer(0)
            mixer(1)

            dve.wait_ge(o_ready, 2)
            dve.tensor_tensor(tot, sums[:, 0:1], sums[:, 1:2], ALU.add).then_inc(tot_ready, 1)
            dve.wait_ge(bnmean_ready, 1)
            dve.tensor_scalar(negmean, ps[:, 4, 0:1], -1.0, None, ALU.mult).then_inc(negmean_ready, 1)
            dve.wait_ge(sqs_ready, 2)
            dve.tensor_tensor(vtot, sqs[:, 0:1], sqs[:, 1:2], ALU.add).then_inc(vtot_ready, 1)
            dve.wait_ge(bnrstd_ready, 1)
            dve.wait_ge(negmean_ready, 1)
            settle(dve.tensor_tensor(bnscale, bnscale, par("gamma"), ALU.mult))
            for p in range(PAIRS):
                settle(dve.tensor_scalar(mix[:, p, :], mix[:, p, :], negmean, bnscale, ALU.add, ALU.mult))
                dve.scalar_tensor_tensor(H[:, p, :], mix[:, p, :], par("beta"), H[:, p, :], ALU.add,
                                         ALU.add).then_inc(h2_ready, 1)

            def norm2(p):
                b0 = 4 * p * 512
                s2, ms = wk_tile(4 * p + 1), wk_tile(4 * p + 2)
                dve.wait_ge(s2_ready, p + 1)
                settle(dve.tensor_tensor(ms, s2, s2, ALU.mult))
                dve.tensor_tensor(ms, ms, psf[:, b0 + 1024:b0 + 2048], ALU.mult).then_inc(ms_ready, 1)
                dve.wait_ge(patches_ready, BATCH)
                settle(dve.tensor_tensor(normed[:, p, :], psf[:, b0:b0 + 1024], s2, ALU.mult))
                dve.wait_ge(r_ready, p + 1)
                dve.scalar_tensor_tensor(wk_tile(4 * p + 3), normed[:, p, :], par("ln1"), ms, ALU.mult,
                                         ALU.mult).then_inc(hr_ready, 1)

            def rotate(ready, taken, n, rows, b0, hi, lo, split):
                t1, t2 = wk_tile(8)[rows], wk_tile(9)[rows]
                dve.wait_ge(ready, n)
                dve.wait_ge(rope_in, 32)
                settle(dve.tensor_tensor(t1, psf[rows, b0:b0 + 1024], cos_t[rows], ALU.mult))
                dve.tensor_tensor(t2, psf[rows, b0 + 1024:b0 + 2048], sin_t[rows], ALU.mult).then_inc(taken, 1)
                dve.wait_ge(taken, n)
                settle(dve.tensor_tensor(t1, t1, t2, ALU.add))
                settle(dve.tensor_copy(hi, t1))
                dve.tensor_tensor(lo, t1, hi.bitcast(F32), ALU.subtract).then_inc(split, 1)
                dve.wait_ge(split, n)

            for p in range(PAIRS):
                norm2(p)
                b0 = 4 * p * 512
                rotate(q_ready, q_taken, p + 1, slice(0, P), b0, high[:, p, :], low[:, p, :], q_split)
                krows = slice(64 * p, 64 * p + 64)
                rotate(k_ready, k_taken, p + 1, krows, b0, khigh[krows], klow[krows], k_split)

            def normalize(b):
                dve.wait_ge(rden_ready, b + 1)
                dve.wait_ge(o_out, b + 1)
                dve.tensor_tensor(attn_n, attn_o, rden, ALU.mult).then_inc(attn_ready, 1)

            def residual(b):
                rows = slice(CHAN * (b % 2), CHAN * (b % 2) + CHAN)
                dve.wait_ge(wo_ready, b + 1)
                dve.tensor_tensor(mix[rows, b // 2, :], psf[rows, 6 * 512:8 * 512], normed[rows, b // 2, :],
                                  ALU.add).then_inc(x1_ready, 1)

            for b in range(BATCH):
                for i, (tb, h, nh) in enumerate(units):
                    W = P * (tb + 1)
                    bank = 2 * ((b * (NU + 1) + i) % 2)
                    dve.wait_ge(scores_ready, b * NU + i + 1)
                    if b and i == 0:
                        dve.wait_ge(max_turned, b)
                    if tb < 2:
                        src = psf[:, bank * 512:bank * 512 + nh * W].rearrange("p (h s) -> p h s", h=nh)
                    elif tb < 4:
                        src = ps[:, bank:bank + nh, 0:W]
                    else:
                        src = psf[:, bank * 512:bank * 512 + W]
                    dve.tensor_reduce(maxima[:, h:h + nh, tb], src, AX.X, ALU.max).then_inc(maxed, 1)
                    if b >= 2 and i == 3:
                        normalize(b - 2)
                    if b >= 2 and i == 4:
                        residual(b - 2)
                bank = 2 * ((b * (NU + 1) + NU) % 2)
                dve.wait_ge(max_turned, b + 1)
                if b:
                    dve.wait_ge(m_in[(b - 1) % 2], 16 * 8 * ((b - 1) // 2 + 1))
                dve.tensor_scalar(negmax[:, 0, :], ps[0:32, bank, 0:P], -1.0, None, ALU.mult).then_inc(negmax_ready, 1)
                dve.wait_ge(negmax_ready, 2 * b + 1)
                dve.scalar_tensor_tensor(negmax[:, 1, :], ps[0:32, bank, 0:P], -1.0, negmax[:, 0, :].bitcast(F32),
                                         ALU.mult, ALU.subtract).then_inc(negmax_ready, 1)
            for b in range(BATCH - 2, BATCH):
                normalize(b)
                residual(b)

            dve.wait_ge(moe_w_in, 64)
            for i, raw in enumerate((w1_raw, w3_raw)):
                dve.wait_ge(w_high, i + 1)
                dve.tensor_tensor(kt_flat[:, 3072 * i + 1536:3072 * (i + 1)], raw,
                                  kt_flat[:, 3072 * i:3072 * i + 1536].bitcast(F32), ALU.subtract).then_inc(w_low, 1)

            def bcast(col):
                return col.rearrange("p (b e) -> p b e", e=1).broadcast_to([P, 2 * SBLK, EXPERTS])

            ident8 = par("expert_id").rearrange("p (b e) -> p b e", b=1).broadcast_to([P, 2 * SBLK, EXPERTS])
            for p in range(PAIRS):
                dve.wait_ge(inv3_ready, p + 1)
                dve.wait_ge(x1_ready, 2 * (p + 1))
                dve.scalar_tensor_tensor(flat[:, p, :], mix[:, p, :], par("ln2"), inv3, ALU.mult,
                                         ALU.mult).then_inc(flat_ready, 1)
                dve.wait_ge(flat_ready, p + 1)
                settle(dve.tensor_copy(high[:, p, :], flat[:, p, :]))
                dve.tensor_tensor(low[:, p, :], flat[:, p, :], high[:, p, :].bitcast(F32), ALU.subtract).then_inc(split3, 1)
                dve.tensor_tensor(H[:, p, :], H[:, p, :], mix[:, p, :], ALU.add).then_inc(base_ready, 1)
                lg = ps[:, 2:4, 0:SBLK * EXPERTS].rearrange("p h (b e) -> p h b e", e=EXPERTS)
                halves = "p (h b) e -> p h b e"
                dve.wait_ge(logit_ready, p + 1)
                if p:
                    dve.wait_ge(wT_ready, p)
                settle(dve.tensor_reduce(r_m.rearrange("p (h b) -> p h b", h=2), lg, AX.X, ALU.max))
                dve.tensor_tensor(rt[1].rearrange(halves, h=2), lg, bcast(r_m).rearrange(halves, h=2), ALU.subtract).then_inc(rdiff, 1)
                dve.wait_ge(rexp, p + 1)
                settle(dve.tensor_reduce(r_den, rt[1], AX.X, ALU.add))
                settle(dve.reciprocal(r_den, r_den))
                settle(dve.tensor_tensor(rt[0], rt[1], bcast(r_den), ALU.mult))
                settle(dve.tensor_reduce(r_m, rt[0], AX.X, ALU.max))
                settle(dve.tensor_tensor(rt[2], rt[0], bcast(r_m), ALU.is_equal))
                settle(dve.tensor_tensor(rt[2], rt[2], ident8, ALU.mult))
                settle(dve.tensor_reduce(r_min, rt[2], AX.X, ALU.min))
                settle(dve.tensor_tensor(rt[3], ident8, bcast(r_min), ALU.is_equal))
                settle(dve.scalar_tensor_tensor(rt[4], rt[3], -2.0, rt[0], ALU.mult, ALU.add))
                settle(dve.tensor_reduce(r_m2, rt[4], AX.X, ALU.max))
                settle(dve.tensor_tensor(rt[5], rt[4], bcast(r_m2), ALU.is_equal))
                settle(dve.tensor_tensor(rt[5], rt[5], ident8, ALU.mult))
                settle(dve.tensor_reduce(r_min, rt[5], AX.X, ALU.min))
                settle(dve.tensor_tensor(rt[2], ident8, bcast(r_min), ALU.is_equal))
                settle(dve.tensor_tensor(rt[3], rt[3], rt[2], ALU.add))
                settle(dve.scalar_tensor_tensor(r_den, r_m, 1e-9, r_m2, ALU.add, ALU.add))
                settle(dve.reciprocal(r_den, r_den))
                settle(dve.tensor_tensor(rt[3], rt[3], rt[0], ALU.mult))
                dve.tensor_tensor(rt[6], rt[3], bcast(r_den), ALU.mult).then_inc(rw_ready, 1)

            def scale_y(m):
                k, q = divmod(m, EPAIRS)
                b = k // 2
                dve.wait_ge(y2_ready, m + 1)
                dve.wait_ge(gates_in[b % 2], 16 * EXPERTS * (b // 2 + 1))
                if m >= 2:
                    dve.wait_ge(gy_used, m - 1)
                dve.tensor_tensor(gated_y[:, m % 2, :], ps[:, 4 + m % 2, :],
                                  gates[:, b % 2, q, HALF * (k % 2):HALF * (k % 2 + 1)], ALU.mult).then_inc(gy_ready, 1)

            n = 0
            for m in range(CHUNKS * EPAIRS):
                for i in range(HTILES):
                    dve.wait_ge(silu_ready, n + 1)
                    dve.wait_ge(h3_ready, n + 1)
                    if n >= 2:
                        dve.wait_ge(hid_used, n - 1)
                    dve.tensor_tensor(hid[:, n % 2, :], silu1[:, n % 2, :], ps[:, 2 + n % 2, :], ALU.mult).then_inc(hid_ready, 1)
                    n += 1
                    if i == 1 and m:
                        scale_y(m - 1)
            scale_y(CHUNKS * EPAIRS - 1)

        @block.tensor
        def _(pe):
            pe.wait_ge(tokw_in, 32)
            for o in range(CHAN):
                for half in range(2):
                    mm = pe.matmul(ps[CHAN * half:CHAN * (half + 1), 6 + o // 32, PATCH * (o % 32):PATCH * (o % 32 + 1)],
                                   tokW[:, o, :], dft, start=True, stop=True)
            mm.then_inc(weff_ready, 1)
            pe.wait_ge(params_in, 16)

            def patches(b):
                pe.wait_ge(x_in[b], 64)
                pe.wait_ge(weff_placed, 8)
                xb = xs[b % 3]
                for r in range(STRIDE):
                    first, last = r == 0, r == STRIDE - 1
                    pe.matmul(ps[0:CHAN, b, :], spec[:, 0, r, :], xb[:, 0:NM, r, :], start=first, stop=last)
                    pe.matmul(ps[CHAN:P, b, :], spec[:, 1, r, :], xb[:, 0:NM, r, :], start=first, stop=False)
                    mm = pe.matmul(ps[CHAN:P, b, :], spec[:, 2, r, :], xb[:, 1:NM + 1, r, :], start=False, stop=last)
                mm.then_inc(patches_ready, 1)

            def both(bank, lhsT, rhs, rows=slice(0, P)):
                for c in range(2):
                    mm = pe.matmul(ps[rows, bank + c, :], lhsT, rhs[:, HALF * c:HALF * (c + 1)], start=True, stop=True)
                return mm

            def mixer(p):
                rows = slice(32 * p, 32 * p + 32)
                pe.wait_ge(h_ready, 4 * (p + 1))
                if p:
                    pe.wait_ge(g_ready, p)
                both(4, par("center"), H[:, p, :]).then_inc(centered, 1)
                pe.wait_ge(sq_ready, p + 1)
                if p:
                    pe.wait_ge(o_ready, p)
                both(6, par("chan_mean"), sq).then_inc(var_ready, 1)
                pe.wait_ge(hn_ready, p + 1)
                both(4, par("in_x"), hn).then_inc(xp_ready, 1)
                both(6, par("in_r"), hn).then_inc(res_ready, 1)
                pe.wait_ge(xconv_ready, p + 1)
                both(4, par("ssm_dt"), xconv, rows)
                pe.wait_ge(sres_ready, p + 1)
                both(6, par("ssm_B"), xconv, rows).then_inc(ssm_ready, 1)
                pe.wait_ge(y_ready, p + 1)
                both(4, par("ssm_C", rows), cprod[rows]).then_inc(cy_ready, 1)
                pe.wait_ge(g_ready, p + 1)
                both(6, par("out_w"), gated).then_inc(outw_ready, 1)

            patches(0)
            patches(1)
            mixer(0)
            patches(2)
            patches(3)
            mixer(1)

            pe.wait_ge(tot_ready, 1)
            pe.wait_ge(g_ready, 2)
            pe.matmul(ps[:, 4, 0:1], par("bn_mean"), tot, start=True, stop=True).then_inc(bnmean_ready, 1)
            pe.wait_ge(vtot_ready, 1)
            pe.matmul(ps[:, 5, 0:1], par("bn_mean"), vtot, start=True, stop=True).then_inc(bnvar_ready, 1)

            for p in range(PAIRS):
                pe.wait_ge(h2_ready, p + 1)
                both(4 * p, par("center"), H[:, p, :]).then_inc(centered2, 1)
                pe.wait_ge(sq2_ready, p + 1)
                both(4 * p + 2, par("chan_mean"), wk_tile(4 * p)).then_inc(var2_ready, 1)
            for p in range(PAIRS):
                hr = wk_tile(4 * p + 3)
                krows = slice(64 * p, 64 * p + 64)
                pe.wait_ge(hr_ready, p + 1)
                both(4 * p, par("wq"), hr)
                both(4 * p + 2, par("wq_rot"), hr).then_inc(q_ready, 1)
                pe.wait_ge(q_taken, p + 1)
                both(4 * p, par("wk"), hr, krows)
                both(4 * p + 2, par("wk_rot"), hr, krows).then_inc(k_ready, 1)
                pe.wait_ge(k_taken, p + 1)
                for half in range(2):
                    rows = slice(CHAN * half, CHAN * (half + 1))
                    for j in range(SBLK):
                        mm = pe.matmul(ps[:, 4 * p + half, 32 * j:32 * (j + 1)], hr[rows, P * j:P * (j + 1)], par("wv", rows),
                                       start=True, stop=True)
                mm.then_inc(v_ready, 1)

            pe.wait_ge(masks_in, 16)
            ident_b, mask_ts, mask_st = masks[:, 0, :], masks[:, 1, :], masks[:, 2, :]

            def max_unit(b, i):
                tb, h0, nh = units[i]
                W, slot = P * (tb + 1), b * (NU + 1) + i
                bank = 2 * (slot % 2)
                if i == 0:
                    pe.wait_ge(qk_in[b % 2], 16 * 18 * (b // 2 + 1))
                    if b == 0:
                        pe.wait_ge(v_placed, 1)
                if i >= 2 or b:
                    if i >= 2:
                        pe.wait_ge(maxed, b * NU + i - 1)
                    elif i == 1:
                        pe.wait_ge(negmax_ready, 2 * b)
                    else:
                        pe.wait_ge(maxed, b * NU)
                for h in range(h0, h0 + nh):
                    q = QT[0:96, b % 2, h // 2, P * tb:P * (tb + 1)]
                    at = bank * 512 + ((h - h0) * (W if tb < 2 else 512))
                    for s0 in range(0, W, 512):
                        s1 = min(W, s0 + 512)
                        diag = s1 == W
                        mm = pe.matmul(psf[:, at + s0:at + s1], q, KT[0:96, b % 2, h, s0:s1], start=True, stop=not diag)
                        if diag:
                            mm = pe.matmul(psf[:, at + s1 - P:at + s1], ident_b, mask_ts, start=False, stop=True)
                mm.then_inc(scores_ready, 1)

            def turn_max(b):
                slot = b * (NU + 1) + NU
                pe.wait_ge(maxed, (b + 1) * NU)
                pe.transpose(ps[0:32, 2 * (slot % 2), 0:P], small[:, 8:40], par("ident")).then_inc(max_turned, 1)

            def prob_block(b, j):
                n = NCH * b + HEADS * sum(len(prob_chunks(i)) for i in range(j))
                for h in range(HEADS):
                    for t0, t1 in prob_chunks(j):
                        if n >= 2:
                            pe.wait_ge(probs_ready, n - 1)
                        bank = 4 + n % 2
                        diag = t0 == P * j
                        mm = pe.matmul(ps[:, bank, 0:t1 - t0], KT[0:100, b % 2, h, P * j:P * (j + 1)],
                                       QT[0:100, b % 2, h // 2, t0:t1], start=True, stop=not diag)
                        if diag:
                            mm = pe.matmul(ps[:, bank, 0:P], ident_b, mask_st, start=False, stop=True)
                        mm.then_inc(logits_t, 1)
                        n += 1

            def pv_block(b, j):
                pe.wait_ge(probs_ready, NCH * b + HEADS * sum(len(prob_chunks(i)) for i in range(j + 1)))
                if b == 0 and j == 0:
                    pe.wait_ge(v_placed, 2)
                if b and j == 0:
                    pe.wait_ge(x1_ready, b)
                for t0, t1 in prob_chunks(j):
                    half = t0 // HALF
                    for h in range(HEADS):
                        mm = pe.matmul(ps[32 * h:32 * h + 32, 6 + half, t0 - HALF * half:t1 - HALF * half],
                                       V[:, b, j, h // 2, :], PT[:, j % 2, h, t0:t1],
                                       start=(j == 0), stop=(j == (SBLK // 2 - 1 if half == 0 else SBLK - 1)))
                mm.then_inc(pv_done, 1)

            def denominators(b):
                pe.wait_ge(o_out, b + 1)
                both(6, par("den_sel"), attn_o).then_inc(den_ready, 1)

            def project(b):
                pe.wait_ge(attn_ready, b + 1)
                both(6, par("wo"), attn_n, slice(CHAN * (b % 2), CHAN * (b % 2) + CHAN)).then_inc(wo_ready, 1)

            PER = 4
            for i in range(NU):
                max_unit(0, i)
            turn_max(0)
            for b in range(BATCH):
                nxt = b + 1 < BATCH
                i = 0
                for j in range(SBLK):
                    if j == 0:
                        pe.wait_ge(m_in[b % 2], 16 * 8 * (b // 2 + 1))
                        if b == 0:
                            pe.wait_ge(v_placed, 2)
                    prob_block(b, j)
                    if j == 0 and b:
                        denominators(b - 1)
                    if j == 1 and b:
                        project(b - 1)
                    if nxt:
                        for _ in range(PER):
                            if i < NU:
                                max_unit(b + 1, i)
                                i += 1
                                if i == NU:
                                    turn_max(b + 1)
                    if j:
                        pv_block(b, j - 1)
                pv_block(b, SBLK - 1)
            denominators(BATCH - 1)
            project(BATCH - 1)

            for p in range(PAIRS):
                pe.wait_ge(sq3_ready, p + 1)
                if p:
                    pe.wait_ge(inv3_ready, p)
                both(0, par("chan_mean"), sq3).then_inc(var3_ready, 1)
                pe.wait_ge(flat_ready, p + 1)
                if p:
                    pe.wait_ge(rdiff, p)
                for half in range(2):
                    rows = slice(CHAN * half, CHAN * (half + 1))
                    for j in range(SBLK):
                        mm = pe.matmul(ps[:, 2 + half, EXPERTS * j:EXPERTS * (j + 1)], flat[rows, p, P * j:P * (j + 1)], par("router", rows),
                                       start=True, stop=True)
                mm.then_inc(logit_ready, 1)
                pe.wait_ge(rw_ready, p + 1)
                if p:
                    pe.wait_ge(wT_out, p)
                for k in range(4):
                    mm = pe.transpose(ps[0:32, 4, P * k:P * (k + 1)],
                                      rt[6][:, 4 * k:4 * k + 4, :].rearrange("p b e -> p (b e)"), par("ident"))
                mm.then_inc(wT_ready, 1)

            pe.wait_ge(w_low, 2)
            pe.wait_ge(w_high, 2)
            pe.wait_ge(w2_in, 16)
            pe.wait_ge(wT_out, PAIRS)
            pe.wait_ge(rdiff, PAIRS)

            def up(n):
                m, i = divmod(n, HTILES)
                k, q = divmod(m, EPAIRS)
                if i == 0 and q == 0:
                    pe.wait_ge(tok_in[k // 2], 32)
                toks = tok_parts[:, HALF * k:HALF * (k + 1)]
                if n >= 2:
                    pe.wait_ge(silu_ready, n - 1)
                for part in range(2):
                    mm = pe.matmul(ps[:, n % 2, :], w_parts[part][:, q, i, :], toks, start=(part == 0), stop=(part == 1))
                mm.then_inc(h1_ready, 1)
                if n >= 2:
                    pe.wait_ge(hid_ready, n - 1)
                for part in range(2):
                    mm = pe.matmul(ps[:, 2 + n % 2, :], w_parts[2 + part][:, q, i, :], toks, start=(part == 0), stop=(part == 1))
                mm.then_inc(h3_ready, 1)

            def down(n):
                m, i = divmod(n, HTILES)
                q = m % EPAIRS
                bank = 4 + m % 2
                pe.wait_ge(hid_ready, n + 1)
                if i == 0 and m >= 2:
                    pe.wait_ge(gy_ready, m - 1)
                if i < 2:
                    mm = pe.matmul(ps[0:CHAN, bank, :], w2[:, q, i, :], hid[:, n % 2, :], start=(i == 0), stop=(i == 1))
                if i > 0:
                    mm = pe.matmul(ps[CHAN:P, bank, :], w2[:, q, i + 1, :], hid[:, n % 2, :], start=(i == 1), stop=(i == 2))
                mm.then_inc(hid_used, 1)
                if i == HTILES - 1:
                    pe.wait_ge(hid_used, n + 1)
                    pe.sem_inc(y2_ready, 1)

            def finish(m):
                k, q = divmod(m, EPAIRS)
                bank = 6 + k % 2
                if q == 0:
                    pe.wait_ge(base_ready, k // 4 + 1)
                    if k >= 2:
                        pe.wait_ge(fin_out, k - 1)
                    rows = slice(CHAN * (k // 2 % 2), CHAN * (k // 2 % 2) + CHAN)
                    for blk in range(4):
                        t0 = HALF * (k % 2) + P * blk
                        pe.matmul(ps[:, bank, CHAN * blk:CHAN * (blk + 1)], H[rows, k // 4, t0:t0 + P], par("ident2", rows),
                                  start=(blk == 0), stop=False, skip_group_check=True)
                pe.wait_ge(gy_ready, m + 1)
                for blk in range(4):
                    mm = pe.matmul(ps[:, bank, CHAN * blk:CHAN * (blk + 1)], gated_y[:, m % 2, P * blk:P * (blk + 1)],
                                   par("ident2"), start=False, stop=(q == EPAIRS - 1), skip_group_check=True)
                mm.then_inc(gy_used, 1)
                if q == EPAIRS - 1:
                    pe.wait_ge(gy_used, m + 1)
                    pe.sem_inc(fin_ready, 1)

            total = CHUNKS * EPAIRS * HTILES
            for n in range(total + 1):
                if n < total:
                    up(n)
                if n:
                    down(n - 1)
                if n >= 5 and (n - 5) % HTILES == 0:
                    finish((n - 5) // HTILES)
            finish(CHUNKS * EPAIRS - 1)


def _pair_diag(m):
    r, c = m.shape
    z = np.zeros((2 * r, 2 * c), np.float32)
    z[:r, :c] = m
    z[r:, c:] = m
    return z


def _constants():
    k = np.arange(PATCH)
    f = np.arange(NFREQ)[:, None]
    ang = 2.0 * np.pi * f * k / PATCH
    dft = np.concatenate([np.cos(ang), -np.sin(ang)], 0) / np.sqrt(PATCH)
    inv_freq = 1.0 / 10000.0 ** (np.arange(0, HD, 2, dtype=np.float32) / HD)
    freqs = np.outer(np.arange(TOK, dtype=np.float32), inv_freq)
    emb = np.concatenate([freqs, freqs], axis=-1).astype(np.float32)
    sign = np.where(np.arange(HD) < HD // 2, -1.0, 1.0)[:, None]
    rope = np.stack([np.tile(np.cos(emb).T, (P // HD, 1)), np.tile(sign * np.sin(emb).T, (P // HD, 1))])
    i = np.arange(P)
    masks = np.stack([np.eye(P), np.where(i[None, :] > i[:, None], NEG, 0.0), np.where(i[None, :] < i[:, None], NEG, 0.0)])
    eye64 = np.eye(CHAN)
    chan_mean = _pair_diag(np.full((CHAN, CHAN), 1.0 / CHAN))
    den_sel = np.zeros((P, P))
    for h in range(HEADS):
        den_sel[32 * h + HD, 32 * h:32 * h + 32] = 1.0
    return {"dft": dft, "rope": rope, "masks": masks, "center": np.eye(P) - chan_mean, "chan_mean": chan_mean,
            "bn_mean": np.tile(eye64, (2, 2)) / (BATCH * TOK), "den_sel": den_sel, "ident": np.eye(P),
            "ident2": np.tile(eye64, (2, 1)), "expert_id": np.tile(np.arange(EXPERTS) - float(EXPERTS), (P, 1)),
            "eps5": np.full((P, 1), 1e-5), "eps6": np.full((P, 1), 1e-6)}


def kernel(**inputs):
    import ml_dtypes
    import concourse.bacc as _bacc
    from concourse import mybir as _mybir
    from concourse.bass_utils import run_bass_kernel_spmd as _run

    a = {k: np.asarray(v) for k, v in inputs.items()}
    const = _constants()
    cols, total = param_columns()
    block = np.zeros((P, total), np.float32)

    def put(name, value):
        at, w = cols[name]
        block[:value.shape[0], at:at + w] = value

    def twice(v):
        v = v.reshape(CHAN, -1)
        return np.concatenate([v, v], 0)

    half = HD // 2
    rot = np.concatenate([np.arange(HD * n + half, HD * (n + 1)).tolist() + np.arange(HD * n, HD * n + half).tolist()
                          for n in range(HEADS)]).astype(int)
    in_w, in_b = a["L0_attn_in_w"], a["L0_attn_in_b"]
    put("in_x", _pair_diag(in_w[:CHAN].T))
    put("in_r", _pair_diag(in_w[CHAN:].T))
    put("ssm_dt", _pair_diag(a["L0_attn_dt"]))
    put("ssm_B", _pair_diag(a["L0_attn_B_w"].T))
    put("ssm_C", np.concatenate([_pair_diag(a["L0_attn_C_w"].T)] * 2, 0))
    put("out_w", _pair_diag(a["L0_attn_out_w"].T))
    wq, wk = a["L0_ffn_wq"], a["L0_ffn_wk"]
    put("wq", _pair_diag(wq.T))
    put("wq_rot", _pair_diag(wq[rot].T))
    put("wk", _pair_diag(wk.T))
    put("wk_rot", _pair_diag(wk[rot[:KV * HD]].T))
    put("wv", twice(a["L0_ffn_wv"].T))
    wo = np.zeros((P, CHAN), np.float32)
    for h in range(HEADS):
        wo[32 * h:32 * h + HD] = a["L0_ffn_wo"][:, HD * h:HD * (h + 1)].T
    put("wo", wo)
    put("router", twice(a["L0_ffn_router_w"].T))
    put("conv_w", twice(a["L0_attn_conv_w"]))
    for name, v in (("conv_b", a["L0_attn_conv_b"]), ("in_b_x", in_b[:CHAN]), ("in_b_r", in_b[CHAN:]),
                    ("out_b", a["L0_attn_out_b"]), ("gamma", a["L0_attn_gamma"]), ("beta", a["L0_attn_beta"]),
                    ("ln1", a["L0_ffn_ln1_w"]), ("ln2", a["L0_ffn_ln2_w"])):
        put(name, twice(v))
    for name in ("center", "chan_mean", "bn_mean", "den_sel", "ident", "ident2", "expert_id", "eps5", "eps6"):
        put(name, const[name])

    def hidden(w):
        t = np.zeros((CHAN, EPAIRS, HTILES * P), np.float32)
        for e in range(EXPERTS):
            t[:, e // 2, HID * (e % 2):HID * (e % 2 + 1)] = w[e].T
        return t.reshape(CHAN, -1)

    w2 = a["L0_ffn_w2"]
    w2t = np.zeros((P, EPAIRS, 4, CHAN), np.float32)
    for q in range(EPAIRS):
        even, odd = w2[2 * q].T, w2[2 * q + 1].T
        cut = P - REST
        w2t[:, q, 0] = even[:P]
        w2t[:REST, q, 1] = even[P:]
        w2t[REST:, q, 2] = odd[:cut]
        w2t[:HID - cut, q, 3] = odd[cut:]
    arrays = {
        "x": a["x"], "tok_W": a["L0_tok_W"], "params": block, "dft": const["dft"].astype(np.float32),
        "rope": const["rope"].astype(np.float32), "masks": const["masks"].astype(ml_dtypes.bfloat16),
        "w1": hidden(a["L0_ffn_w1"]), "w3": hidden(a["L0_ffn_w3"]), "w2": w2t.reshape(P, -1),
    }
    nc = _bacc.Bacc("TRN2", target_bir_lowering=False, num_devices=1)
    feed, args = {}, []
    for name, v in arrays.items():
        v = np.ascontiguousarray(v)
        feed[f"in_{name}"] = v
        args.append(nc.dram_tensor(f"in_{name}", v.shape, _mybir.dt.from_np(v.dtype), kind="ExternalInput").ap())
    args.append(nc.dram_tensor("out_0", (BATCH, TOK, CHAN), F32, kind="ExternalOutput").ap())
    vit_tower(nc, *args)
    r = _run(nc, [feed], core_ids=[0])
    return r.results[0]["out_0"]
```

```python
from contextlib import ExitStack

import numpy as np

import concourse.bass as bass
from concourse import mybir

ALU = mybir.AluOpType
ACT = mybir.ActivationFunctionType
AX = mybir.AxisListType
F32 = mybir.dt.float32
F32R = mybir.dt.float32r
BF16 = mybir.dt.bfloat16

P = 128
BATCH, CHAN, TIME, VARS = 4, 64, 128, 64
PATCH, STRIDE = 16, 8
NPATCH = TIME // STRIDE
TOK = VARS * NPATCH
PAIRS = BATCH // 2
HALF = TOK // 2
NM = NPATCH // 2
NFREQ = PATCH // 2 + 1
STATE = 16
TAPS = 4
HEADS, KV, HD = 4, 2, 16
SBLK = TOK // P
EXPERTS, HID = 8, 170
EPAIRS = EXPERTS // 2
HTILES = 3
REST = HID - P
CHUNKS = BATCH * 2
NEG = -1e30

PARAMS = [("in_x", 128), ("in_r", 128), ("ssm_dt", 32), ("ssm_B", 32), ("ssm_C", 128), ("out_w", 128),
          ("wq", 128), ("wq_rot", 128), ("wk", 64), ("wk_rot", 64), ("wv", 32), ("wo", 64), ("router", 16),
          ("conv_w", 4), ("conv_b", 1), ("in_b_x", 1), ("in_b_r", 1), ("out_b", 1), ("gamma", 1), ("beta", 1),
          ("ln1", 1), ("ln2", 1),
          ("center", 128), ("chan_mean", 128), ("bn_mean", 128), ("den_sel", 128), ("ident", 128),
          ("ident2", 64), ("pick0", 64), ("pick1", 64), ("expert_id", 8), ("eps5", 1), ("eps6", 1)]


def param_columns():
    at, out = 0, {}
    for name, width in PARAMS:
        out[name] = (at, width)
        at += width
    return out, at


HEAD_ORDER = [0, 2, 1, 3]


def max_units():
    units = []
    for tb in range(SBLK):
        first = min(tb + 1, 4)
        for h in range(0, HEADS, 4 // first if first < 3 else 1):
            units.append((tb, 0, first, h, 4 // first if first < 3 else 1))
    for tb in range(4, SBLK):
        n = tb - 3
        for h in range(0, HEADS, 4 // n if n < 3 else 1):
            units.append((tb, 4, n, h, 4 // n if n < 3 else 1))
    return units


def prob_groups():
    return [(1, j) for j in range(SBLK)] + [(0, j) for j in range(SBLK // 2)]


def vit_tower(nc, x, tok_W, params_d, dft_d, rope_d, masks_d, w1_d, w3_d, w2_d, out):
    cols, NPARAM = param_columns()
    units, groups = max_units(), prob_groups()
    NU, NG = len(units), len(groups)
    SLOTS = NU + 1
    UNITS = 2 * PAIRS

    with ExitStack() as ctx:
        def sb(name, shape, dt=F32):
            return ctx.enter_context(nc.sbuf_tensor(name, shape, dt))

        def sem(name):
            return ctx.enter_context(nc.semaphore(name))

        ps = ctx.enter_context(nc.psum_tensor("ps", [P, 8, HALF], F32))

        XSLOT = (NM + 1) * STRIDE * VARS
        early = sb("early", [P, 3 * XSLOT])
        work = sb("work", [P, 12 * TOK + 4])
        params = sb("params", [P, NPARAM])
        masks = sb("masks", [P, 3, P], BF16)
        spec = sb("spec", [P, 3, STRIDE, CHAN])
        H = sb("H", [P, PAIRS, TOK])
        mix = sb("mix", [P, PAIRS, TOK])
        high = sb("high", [P, PAIRS, TOK], F32R)
        low = sb("low", [P, PAIRS, TOK], F32R)
        khigh = sb("khigh", [P, TOK], F32R)
        klow = sb("klow", [P, TOK], F32R)
        QT = sb("QT", [P, 2, KV, TOK], F32R)
        KT = sb("KT", [P, 2, HEADS, TOK], F32R)
        small = sb("small", [P, 72])
        negmax = sb("negmax", [32, 2, P], F32R)
        w_dram = nc.dram_tensor("routing_weights", [EXPERTS, BATCH * TOK], F32, kind="Internal").ap()

        def par(name, rows=slice(0, P)):
            a, w = cols[name]
            return params[rows, a:a + w]

        def tile(i):
            return work[:, i * TOK:(i + 1) * TOK]

        def cut(t, c):
            return t[:, HALF * c:HALF * (c + 1)]

        xs = [early[:, XSLOT * i:XSLOT * (i + 1)].rearrange("p (m r v) -> p m r v", r=STRIDE, v=VARS) for i in range(3)]
        normed = early[:, 0:2 * TOK].rearrange("p (a t) -> p a t", a=PAIRS)
        V = early[:, 2 * TOK:4 * TOK].rearrange("p (b j g d) -> p b j g d", b=BATCH, j=SBLK, g=KV)
        PT = early[:, 4 * TOK:12 * TOK].rearrange("p (i h t) -> p i h t", i=4, h=HEADS)
        gates = early[:, 4 * TOK:12 * TOK].rearrange("p (i q t) -> p i q t", i=2, q=EPAIRS)
        w2 = early[:, 12 * TOK:13 * TOK].rearrange("p (q s o) -> p q s o", q=EPAIRS, s=4)
        wT = early[:, 13 * TOK:13 * TOK + P]

        gated, hn, sres, xconv, rstd = tile(0), tile(1), tile(2), tile(3), tile(4)
        sq = gated
        dA, cprod, csum, zeros, z, y = tile(5), tile(6), tile(7), tile(8), tile(9), tile(10)
        xpad = work[:, 11 * TOK:12 * TOK + TAPS - 1]
        tokW = work[0:2 * NFREQ, 3 * TOK:7 * TOK].rearrange("k (o c) -> k o c", o=CHAN)
        dft = work[0:2 * NFREQ, 7 * TOK:7 * TOK + PATCH]
        sq2 = [tile(0), tile(1)]
        inv2 = [tile(2), tile(3)]
        ms = [tile(4), tile(5)]
        hr = [tile(6), tile(7)]
        prod_cos, prod_sin = tile(8), tile(9)
        cos_t, sin_t = tile(10), tile(11)
        attn_o = [tile(b) for b in range(BATCH)]
        attn_n = work[:, 4 * TOK:6 * TOK].rearrange("p (i t) -> p i t", i=4)
        w1_raw = work[:, 6 * TOK:6 * TOK + 1536]
        w3_raw = work[:, 6 * TOK + 1536:9 * TOK]
        rden, sq3, inv3, flat = tile(9), tile(10), tile(10), tile(11)
        rt_flat = spec[:].rearrange("p a r o -> p (a r o)")
        rt = [rt_flat[:, P * i:P * (i + 1)].rearrange("p (n e) -> p n e", e=EXPERTS) for i in range(7)]
        r_m, r_min, r_m2, r_den = (rt_flat[:, 7 * P + 16 * i:7 * P + 16 * (i + 1)] for i in range(4))
        silu1 = early[:, 2 * TOK:4 * TOK].rearrange("p (i t) -> p i t", i=4)
        hid = work[:, 6 * TOK:8 * TOK].rearrange("p (i t) -> p i t", i=4)
        gated_y = tile(8).rearrange("p (i t) -> p i t", i=2)
        acc = tile(0).rearrange("p (i t) -> p i t", i=2)
        final = tile(1)[:, 0:512].rearrange("p (i b o) -> p i b o", i=2, b=4)
        kt_flat = KT[:].rearrange("p i h t -> p (i h t)")
        qt_flat = QT[:].rearrange("p i g t -> p (i g t)")
        NW = EPAIRS * HTILES * P
        w1_high, w1_low, w3_high = kt_flat[:, 0:NW], kt_flat[:, NW:2 * NW], qt_flat[:, 0:NW]
        w3_low = [khigh[:, 0:NW // 2], klow[:, 0:NW // 2]]
        toks = [kt_flat[:, 3 * TOK:4 * TOK], low[:, 1, :], kt_flat[:, 4 * TOK:5 * TOK], kt_flat[:, 5 * TOK:6 * TOK]]
        part_high = [high[:, 0, :], high[:, 1, :]]
        part_low = [low[:, 0, :], kt_flat[:, 6 * TOK:7 * TOK]]

        sums, sqs, tot, vtot = small[:, 0:4], small[:, 4:6], small[:, 6:7], small[:, 7:8]
        negmean, bnscale = small[:, 8:9], small[:, 9:10]
        maxima = small[:, 16:48].rearrange("p (h b) -> p h b", h=HEADS)
        maxima_far = small[:, 48:64].rearrange("p (h b) -> p h b", h=HEADS)

        params_in = sem("params_in"); tokw_in = sem("tokw_in"); rope_in = sem("rope_in"); masks_in = sem("masks_in")
        x_in = [sem(f"x_in{b}") for b in range(BATCH)]
        weff_ready = sem("weff_ready"); weff_placed = sem("weff_placed"); spec_blank = sem("spec_blank")
        patches_ready = sem("patches_ready"); h_ready = sem("h_ready")
        centered = sem("centered"); sq_ready = sem("sq_ready"); var_ready = sem("var_ready")
        rstd_ready = sem("rstd_ready"); hn_ready = sem("hn_ready"); xp_ready = sem("xp_ready")
        res_ready = sem("res_ready"); sres_ready = sem("sres_ready"); xconv_ready = sem("xconv_ready")
        ssm_ready = sem("ssm_ready"); dA_ready = sem("dA_ready"); y_ready = sem("y_ready")
        cy_ready = sem("cy_ready"); g_ready = sem("g_ready"); outw_ready = sem("outw_ready"); o_ready = sem("o_ready")
        tot_ready = sem("tot_ready"); bnmean_ready = sem("bnmean_ready"); negmean_ready = sem("negmean_ready")
        sqs_ready = sem("sqs_ready"); vtot_ready = sem("vtot_ready"); bnvar_ready = sem("bnvar_ready")
        bnrstd_ready = sem("bnrstd_ready"); h2_ready = sem("h2_ready")
        centered2 = sem("centered2"); sq2_ready = sem("sq2_ready"); var2_ready = sem("var2_ready")
        s2_ready = sem("s2_ready"); ms_ready = sem("ms_ready"); r_ready = sem("r_ready"); hr_ready = sem("hr_ready")
        rot_ready = sem("rot_ready"); rot_taken = sem("rot_taken"); rot_sum = sem("rot_sum")
        rot_high = sem("rot_high"); rot_split = sem("rot_split")
        v_ready = sem("v_ready"); v_placed = sem("v_placed"); v_blank = sem("v_blank"); kt_blank = sem("kt_blank")
        pads_blank = sem("pads_blank")
        qk_in = [sem(f"qk_in{i}") for i in range(2)]; m_in = [sem(f"m_in{i}") for i in range(2)]
        scores_ready = sem("scores_ready"); maxed = sem("maxed"); maxima_ready = sem("maxima_ready")
        max_turned = sem("max_turned"); negmax_ready = sem("negmax_ready")
        logits_t = sem("logits_t"); probs_ready = sem("probs_ready"); pv_done = sem("pv_done"); o_out = sem("o_out")
        den_ready = sem("den_ready"); rden_ready = sem("rden_ready"); attn_ready = sem("attn_ready")
        wo_ready = sem("wo_ready"); x1_ready = sem("x1_ready"); sq3_ready = sem("sq3_ready")
        var3_ready = sem("var3_ready"); inv3_ready = sem("inv3_ready"); flat_ready = sem("flat_ready")
        high3 = sem("high3"); split3 = sem("split3"); base_ready = sem("base_ready")
        tok_in = [sem(f"tok_in{b}") for b in range(BATCH)]
        logit_ready = sem("logit_ready"); rdiff = sem("rdiff"); rexp = sem("rexp"); rw_ready = sem("rw_ready")
        wT_ready = sem("wT_ready"); wT_out = sem("wT_out"); w_stored = sem("w_stored")
        moe_w_in = sem("moe_w_in"); w2_in = sem("w2_in"); w_high = sem("w_high"); w_split = sem("w_split")
        gates_in = [sem(f"gates_in{b}") for b in range(BATCH)]
        h1_ready = sem("h1_ready"); h3_ready = sem("h3_ready"); silu_ready = sem("silu_ready"); hid_ready = sem("hid_ready")
        hid_used = sem("hid_used"); y2_ready = sem("y2_ready"); gy_ready = sem("gy_ready"); acc_step = sem("acc_step")
        fin_ready = sem("fin_ready"); fin_out = sem("fin_out")
        stored = [sem(f"stored{i}") for i in range(2)]
        dve_step = sem("dve_step"); act_step = sem("act_step"); pool_step = sem("pool_step")

        block = ctx.enter_context(nc.Block())

        rot_items = [(kind, p, c) for p in range(PAIRS) for kind in "qk" for c in range(2)]
        NB = 2 * NG
        A_FROM, A_TO = 4, 21

        def a_until(k):
            return min(SLOTS, max(0, -(-SLOTS * (k + 1 - A_FROM) // (A_TO - A_FROM))))

        def beats(p, batches_den):
            return [("den", b, c) for b in batches_den for c in range(2)]

        def tail(p):
            return ([("wo", p, c) for c in range(2)] + [("var", p, c) for c in range(2)]
                    + [("route", p, 0), ("pick", p, 0), ("turn", p, 0)])

        side_attn = beats(0, (0, 1)) + tail(0) + beats(1, (2,))
        side_moe = beats(1, (3,)) + tail(1)
        side_order = side_attn + side_moe
        NSA = len(side_attn)
        attn_at = {(3, 1 + (22 * i) // NSA): [] for i in range(NSA)}
        for i, beat in enumerate(side_attn):
            attn_at[(3, 1 + (22 * i) // NSA)].append(i)
        moe_at = {1 + 3 * i: [NSA + i] for i in range(len(side_moe))}

        def side_bank(i):
            return i % 3 if i < NSA else 7

        def den_index(b, c):
            return 2 * b + c

        def used_after(t):
            m, i = divmod(t, HTILES)
            return 2 * m + 1 + i

        @block.sync
        def _(sp):
            def load_x(b):
                v = x[b].rearrange("c (m s r) v -> s c m (r v)", s=2, r=STRIDE)
                for s in range(2):
                    rows = slice(CHAN * s, CHAN * (s + 1))
                    sp.dma_start(xs[b % 3][rows, 0:NM].rearrange("p m r v -> p m (r v)"), v[s]).then_inc(x_in[b], 16)
                    sp.dma_start(xs[b % 3][rows, NM],
                                 x[b, :, TIME - 1:TIME, :].broadcast_to([CHAN, STRIDE, VARS])).then_inc(x_in[b], 16)

            for b in range(3):
                load_x(b)
            sp.dma_start(masks[:], masks_d.rearrange("m p s -> p m s")).then_inc(masks_in, 16)
            sp.wait_ge(patches_ready, 1)
            load_x(3)
            sp.wait_ge(cy_ready, UNITS)
            sp.dma_start(cos_t, rope_d[0]).then_inc(rope_in, 16)
            sp.dma_start(sin_t, rope_d[1]).then_inc(rope_in, 16)

            def stack(b):
                p, h0, buf = b // 2, CHAN * (b % 2), b % 2
                sp.wait_ge(rot_split, 4 * (p + 1))
                if b == 0:
                    sp.wait_ge(kt_blank, 1)
                if b >= 2:
                    sp.wait_ge(logits_t, NB * (b - 1))
                for grp, part in enumerate((khigh, klow, khigh)):
                    for h in range(HEADS):
                        src = 64 * p + 32 * (b % 2) + HD * (h // 2)
                        dst = 32 * grp + HD * (h % 2)
                        sp.dma_start(KT[dst:dst + HD, buf, h, :].bitcast(F32),
                                     part[src:src + HD, :].bitcast(F32)).then_inc(qk_in[buf], 16)
                for grp, part in enumerate((high, high, low)):
                    for g in range(KV):
                        src = h0 + 32 * g
                        sp.dma_start(QT[32 * grp:32 * grp + 32, buf, g, :].bitcast(F32),
                                     part[src:src + 32, p, :].bitcast(F32)).then_inc(qk_in[buf], 16)

            def place_maxima(b):
                sp.wait_ge(negmax_ready, 2 * (b + 1))
                for part in range(2):
                    for a in range(2):
                        at = 96 + 2 * a + part
                        sp.dma_start(QT[at:at + 1, b % 2, :, :].bitcast(F32).rearrange("p g (j s) -> p (g j) s", s=P),
                                     negmax[16 * a:16 * (a + 1), part, :].bitcast(F32)).then_inc(m_in[b % 2], 16)

            stack(0)
            stack(1)
            place_maxima(0)
            for rows in (slice(0, CHAN), slice(CHAN, P)):
                sp.dma_start(w1_raw[rows], w1_d).then_inc(moe_w_in, 16)
                sp.dma_start(w3_raw[rows], w3_d).then_inc(moe_w_in, 16)
            sp.dma_start(w2.rearrange("p q s o -> p (q s o)"), w2_d).then_inc(w2_in, 16)
            place_maxima(1)
            for b in (2, 3):
                stack(b)
                place_maxima(b)

            for p in range(PAIRS):
                sp.wait_ge(split3, 2 * (p + 1))
                for b in (2 * p, 2 * p + 1):
                    rows = slice(CHAN * (b % 2), CHAN * (b % 2) + CHAN)
                    sp.dma_start(toks[b][0:CHAN].bitcast(F32), part_high[p][rows].bitcast(F32)).then_inc(tok_in[b], 16)
                    sp.dma_start(toks[b][CHAN:P].bitcast(F32), part_low[p][rows].bitcast(F32)).then_inc(tok_in[b], 16)
                sp.wait_ge(wT_out, p + 1)
                for j in range(SBLK):
                    sp.dma_start(w_dram[:, 2 * TOK * p:2 * TOK * (p + 1)].rearrange(
                        "e (b j s) -> j b e s", b=2, j=SBLK)[j], wT[16 * j:16 * (j + 1)]).then_inc(w_stored, 16)
                sp.wait_ge(w_stored, 16 * SBLK * (p + 1))
                for b in (2 * p, 2 * p + 1):
                    if b == 0:
                        sp.wait_ge(pv_done, NG * BATCH)
                    if b >= 2:
                        sp.wait_ge(gy_ready, 2 * EPAIRS * (b - 1))
                    for e in range(EXPERTS):
                        sp.dma_start(gates[CHAN * (e % 2):CHAN * (e % 2 + 1), b % 2, e // 2, :],
                                     w_dram[e:e + 1, TOK * b:TOK * (b + 1)].broadcast_to([CHAN, TOK])
                                     ).then_inc(gates_in[b], 16)

        @block.gpsimd
        def _(pool):
            done = [0]

            def settle(ins):
                done[0] += 1
                ins.then_inc(pool_step, 1)
                pool.wait_ge(pool_step, done[0])

            pool.memset(spec[:], 0.0).then_inc(spec_blank, 1)
            pool.memset(xpad[:, 0:TAPS - 1], 0.0).then_inc(pads_blank, 1)
            pool.wait_ge(weff_ready, 1)
            pool.memset(zeros, 0.0).then_inc(pads_blank, 1)
            settle(pool.memset(kt_flat.bitcast(F32), 0.0))
            for h in range(HEADS):
                ins = pool.memset(KT[96:98 if h % 2 == 0 else 100, :, h, :].bitcast(F32), 1.0)
            settle(ins)
            for h in (1, 3):
                ins = pool.memset(KT[96:98, :, h, :].bitcast(F32), 0.0)
            ins.then_inc(kt_blank, 1)
            pool.wait_ge(kt_blank, 1)
            pool.wait_ge(patches_ready, BATCH)
            flatV = V.rearrange("p b j g d -> p (b j g) d")
            settle(pool.memset(flatV[:, :, HD:32], 0.0))
            pool.memset(flatV[:, :, HD:HD + 1], 1.0).then_inc(v_blank, 1)
            for i, (kind, p, c) in enumerate(rot_items):
                rows = slice(0, P) if kind == "q" else slice(64 * p, 64 * p + 64)
                pool.wait_ge(rot_taken, i + 1)
                if i:
                    pool.wait_ge(rot_sum, i)
                a, b = cut(prod_cos, i % 2)[rows], cut(prod_sin, i % 2)[rows]
                pool.tensor_tensor(a, a, b, ALU.add).then_inc(rot_sum, 1)

            pool.wait_ge(moe_w_in, 64)
            pool.wait_ge(logits_t, NB * 3)
            pool.wait_ge(qk_in[1], 2 * 18 * 16)
            pool.wait_ge(scores_ready, NU * BATCH)
            pool.tensor_copy(w1_high, w1_raw).then_inc(w_high, 1)
            pool.tensor_copy(w3_high, w3_raw).then_inc(w_high, 1)
            pool.wait_ge(w_high, 2)
            pool.tensor_tensor(w1_low, w1_raw, w1_high.bitcast(F32), ALU.subtract).then_inc(w_split, 1)
            for i in range(2):
                a, b = NW // 2 * i, NW // 2 * (i + 1)
                pool.tensor_tensor(w3_low[i], w3_raw[:, a:b], w3_high[:, a:b].bitcast(F32),
                                   ALU.subtract).then_inc(w_split, 1)

            for k in range(CHUNKS):
                for q in range(1, EPAIRS):
                    m = EPAIRS * k + q
                    pool.wait_ge(gy_ready, m + 1)
                    if q == 1 and k >= 2:
                        pool.wait_ge(fin_ready, k - 1)
                    a = gated_y[:, 0, :] if q == 1 else acc[:, k % 2, :]
                    if q > 1:
                        pool.wait_ge(acc_step, 3 * k + q - 1)
                    pool.tensor_tensor(acc[:, k % 2, :], a, gated_y[:, m % 2, :], ALU.add).then_inc(acc_step, 1)

        @block.scalar
        def _(act):
            done = [0]

            def settle(ins):
                done[0] += 1
                ins.then_inc(act_step, 1)
                act.wait_ge(act_step, done[0])

            act.dma_start(tokW, tok_W.rearrange("o (k c) -> k o c", c=CHAN)).then_inc(tokw_in, 16)
            act.dma_start(dft, dft_d).then_inc(tokw_in, 16)
            act.dma_start(params[:], params_d).then_inc(params_in, 16)
            act.preload_act_table_set("natural_log_exp_and_others")
            act.wait_ge(params_in, 16)

            def patches_out(b):
                act.wait_ge(patches_ready, b + 1)
                dst = H[CHAN * (b % 2):CHAN * (b % 2 + 1), b // 2, :].rearrange("c (v m two) -> c two m v", m=NM, two=2)
                for two in range(2):
                    act.activation(dst[:, two], ps[CHAN * two:CHAN * (two + 1), b, :].rearrange("c (m v) -> c m v", v=VARS),
                                   ACT.Copy).then_inc(h_ready, 1)

            def mixer_norm(p):
                for c in range(2):
                    act.wait_ge(centered, 2 * p + c + 1)
                    if p:
                        act.wait_ge(outw_ready, c + 1)
                    act.activation(cut(sq, c), ps[:, 4 + c, :], ACT.Square).then_inc(sq_ready, 1)
                for c in range(2):
                    act.wait_ge(var_ready, 2 * p + c + 1)
                    settle(act.activation(cut(rstd, c), ps[:, 6 + c, :], ACT.Ln, bias=par("eps5")))
                    act.activation(cut(rstd, c), cut(rstd, c), ACT.Exp, scale=-0.5).then_inc(rstd_ready, 1)
                for c in range(2):
                    act.wait_ge(res_ready, 2 * p + c + 1)
                    act.activation(cut(sres, c), ps[:, 6 + c, :], ACT.Silu, bias=par("in_b_r")).then_inc(sres_ready, 1)
                act.preload_act_table_set("natural_log_exp_and_others")

            def mixer_decay(p):
                rows = slice(32 * p, 32 * p + 32)
                for c in range(2):
                    act.wait_ge(ssm_ready, 2 * p + c + 1)
                    act.activation(cut(dA, c)[rows], ps[rows, 4 + c, :], ACT.Exp).then_inc(dA_ready, 1)

            patches_out(0)
            patches_out(1)
            mixer_norm(0)
            patches_out(2)
            mixer_decay(0)
            patches_out(3)
            mixer_norm(1)
            mixer_decay(1)

            act.wait_ge(negmean_ready, 1)
            for p in range(PAIRS):
                act.activation(tile(1 + p), mix[:, p, :], ACT.Square, bias=negmean,
                               accum_out=sqs[:, p:p + 1]).then_inc(sqs_ready, 1)
            act.wait_ge(bnvar_ready, 1)
            settle(act.activation(bnscale, ps[:, 5, 0:1], ACT.Ln, bias=par("eps5")))
            act.activation(bnscale, bnscale, ACT.Exp, scale=-0.5).then_inc(bnrstd_ready, 1)

            act.wait_ge(sqs_ready, 2)
            for u in range(UNITS):
                act.wait_ge(centered2, u + 1)
                act.activation(cut(sq2[u // 2], u % 2), ps[:, u, :], ACT.Square).then_inc(sq2_ready, 1)
            for u in range(UNITS):
                s, m = cut(inv2[u // 2], u % 2), cut(ms[u // 2], u % 2)
                act.wait_ge(var2_ready, u + 1)
                settle(act.activation(s, ps[:, 4 + u, :], ACT.Ln, bias=par("eps5")))
                settle(act.activation(m, s, ACT.Exp, scale=-1.0))
                act.activation(s, s, ACT.Exp, scale=-0.5).then_inc(s2_ready, 1)
            for u in range(UNITS):
                m = cut(ms[u // 2], u % 2)
                act.wait_ge(ms_ready, u + 1)
                settle(act.activation(m, m, ACT.Ln, bias=par("eps6")))
                act.activation(m, m, ACT.Exp, scale=-0.5).then_inc(r_ready, 1)

            def high_part(i):
                kind, p, c = rot_items[i]
                act.wait_ge(rot_sum, i + 1)
                if kind == "q":
                    dst, rows = cut(high[:, p, :], c), slice(0, P)
                else:
                    rows = slice(64 * p, 64 * p + 64)
                    dst = cut(khigh, c)[rows]
                act.activation(dst, cut(prod_cos, i % 2)[rows], ACT.Copy).then_inc(rot_high, 1)

            def place_values(u):
                p, c = divmod(u, 2)
                act.wait_ge(v_ready, 2 * u + 2)
                act.wait_ge(v_blank, 1)
                for b in range(2):
                    act.activation(V[:, 2 * p + b, 4 * c:4 * c + 4, :, 0:HD].rearrange("p j g d -> p (j g) d"),
                                   ps[:, u + 4 * b, 0:P].rearrange("p (n d) -> p n d", d=HD), ACT.Copy).then_inc(v_placed, 1)

            for p in range(PAIRS):
                for i in range(4 * p, 4 * p + 4):
                    high_part(i)
                for c in range(2):
                    place_values(2 * p + c)

            def side(i):
                name, a, c = side_order[i]
                bank = side_bank(i)
                if name == "den":
                    n = den_index(a, c)
                    act.wait_ge(den_ready, n + 1)
                    if n >= 2:
                        act.wait_ge(attn_ready, n - 1)
                    settle(act.activation(cut(rden, n % 2), ps[:, bank, :], ACT.Ln))
                    act.activation(cut(rden, n % 2), cut(rden, n % 2), ACT.Exp, scale=-1.0).then_inc(rden_ready, 1)
                elif name == "var":
                    act.wait_ge(var3_ready, 2 * a + c + 1)
                    settle(act.activation(cut(inv3, c), ps[:, bank, :], ACT.Ln, bias=par("eps6")))
                    act.activation(cut(inv3, c), cut(inv3, c), ACT.Exp, scale=-0.5).then_inc(inv3_ready, 1)
                elif name == "pick":
                    act.wait_ge(rdiff, a + 1)
                    act.activation(rt[1], rt[1], ACT.Exp).then_inc(rexp, 1)
                elif name == "turn":
                    act.wait_ge(wT_ready, a + 1)
                    if a:
                        act.wait_ge(w_stored, 16 * SBLK * a)
                    act.activation(wT, ps[:, bank, 0:P], ACT.Copy).then_inc(wT_out, 1)

            def output_half(b, half):
                act.wait_ge(pv_done, NG * b + (SBLK if half else NG))
                act.activation(cut(attn_o[b], half), ps[:, 7, :], ACT.Copy).then_inc(o_out, 1)

            for b in range(BATCH):
                for gi, (half, j) in enumerate(groups):
                    w = HALF * (half + 1) - max(HALF * half, P * j)
                    G = NG * b + gi
                    if G >= 4:
                        act.wait_ge(pv_done, G - 3)
                    for g in range(KV):
                        n = 2 * G + g
                        bank = 3 + 2 * (n % 2)
                        act.wait_ge(logits_t, n + 1)
                        act.activation(PT[:, G % 4, 2 * g:2 * g + 2, 0:w], ps[:, bank:bank + 2, 0:w], ACT.Exp,
                                       scale=float(HD) ** -0.5).then_inc(probs_ready, 1)
                        for i in attn_at.get((b, 2 * gi + g), []):
                            side(i)
                    if b and gi == 1:
                        output_half(b - 1, 0)
                    if gi == SBLK + 1:
                        output_half(b, 1)
            output_half(BATCH - 1, 0)

            def rows_out(k):
                act.wait_ge(fin_ready, k + 1)
                if k >= 2:
                    act.wait_ge(stored[k % 2], 16 * (k // 2))
                act.activation(final[:, k % 2], ps[:, 6, 0:256].rearrange("p (b o) -> p b o", b=4),
                               ACT.Copy).then_inc(fin_out, 1)
                act.wait_ge(fin_out, k + 1)
                act.dma_start(out[k // 2, HALF * (k % 2):HALF * (k % 2 + 1), :].rearrange("(b s) o -> s b o", b=4),
                              final[:, k % 2]).then_inc(stored[k % 2], 16)

            act.wait_ge(pv_done, NG * BATCH)
            per_chunk = EPAIRS * HTILES
            for n in range(CHUNKS * per_chunk):
                act.wait_ge(h1_ready, n + 1)
                if n >= 4:
                    act.wait_ge(hid_ready, n - 3)
                act.activation(silu1[:, n % 4, :], ps[:, n % 2, :], ACT.Silu).then_inc(silu_ready, 1)
                if n > per_chunk and n % per_chunk == 9:
                    rows_out(n // per_chunk - 1)
                for i in moe_at.get(n, []):
                    side(i)
            rows_out(CHUNKS - 1)
            for i in range(2):
                act.wait_ge(stored[i], 8 * CHUNKS)

        @block.vector
        def _(dve):
            done = [0]

            def settle(ins):
                done[0] += 1
                ins.then_inc(dve_step, 1)
                dve.wait_ge(dve_step, done[0])

            dve.wait_ge(spec_blank, 1)
            dve.wait_ge(weff_ready, 1)
            lo, hi = slice(0, CHAN), slice(CHAN, P)
            src = ps[:, 7, :].rearrange("p (o r) -> p r o", r=PATCH)
            for odd, rows in enumerate((lo, hi)):
                outs = slice(odd, CHAN, 2)
                dve.tensor_copy(spec[lo, 0, :, outs], src[rows, 0:STRIDE]).then_inc(weff_placed, 1)
                dve.tensor_copy(spec[hi, 0, :, outs], src[rows, STRIDE:PATCH]).then_inc(weff_placed, 1)
                dve.tensor_copy(spec[hi, 1, :, outs], src[rows, 0:STRIDE]).then_inc(weff_placed, 1)
                dve.tensor_copy(spec[lo, 2, :, outs], src[rows, STRIDE:PATCH]).then_inc(weff_placed, 1)
            dve.wait_ge(params_in, 16)
            dve.wait_ge(pads_blank, 2)
            cw = par("conv_w")

            def mixer_conv(p):
                for c in range(2):
                    dve.wait_ge(rstd_ready, 2 * p + c + 1)
                    dve.tensor_tensor(cut(hn, c), ps[:, 4 + c, :], cut(rstd, c), ALU.mult).then_inc(hn_ready, 1)
                for c in range(2):
                    at = HALF * c
                    dve.wait_ge(xp_ready, 2 * p + c + 1)
                    settle(dve.tensor_scalar(xpad[:, TAPS - 1 + at:TAPS - 1 + at + HALF], ps[:, 4 + c, :], par("in_b_x"),
                                             None, ALU.add))
                    xc = cut(xconv, c)
                    settle(dve.tensor_scalar(xc, xpad[:, at:at + HALF], cw[:, 0:1], par("conv_b"), ALU.mult, ALU.add))
                    for k in range(1, TAPS):
                        ins = dve.scalar_tensor_tensor(xc, xpad[:, at + k:at + k + HALF], cw[:, k:k + 1], xc,
                                                       ALU.mult, ALU.add)
                        if k < TAPS - 1:
                            settle(ins)
                    ins.then_inc(xconv_ready, 1)

            def mixer_scan(p):
                rows = slice(32 * p, 32 * p + 32)
                for c in range(2):
                    h, first = HALF * c, 1 if c == 0 else 0
                    dve.wait_ge(dA_ready, 2 * p + c + 1)
                    start = 1.0 if c == 0 else cprod[rows, h - 1:h]
                    settle(dve.tensor_tensor_scan(cut(cprod, c)[rows], cut(dA, c)[rows], cut(zeros, c)[rows], start,
                                                  ALU.mult, ALU.add))
                    settle(dve.tensor_tensor(cut(z, c)[rows], cut(cprod, c)[rows], ps[rows, 6 + c, :], ALU.mult))
                    start = 0.0 if c == 0 else csum[rows, h - 1:h]
                    settle(dve.tensor_tensor_scan(cut(csum, c)[rows], cut(z, c)[rows], cut(zeros, c)[rows], start,
                                                  ALU.add, ALU.add))
                    if c == 0:
                        settle(dve.tensor_copy(y[rows, 0:1], ps[rows, 6, 0:1]))
                    settle(dve.tensor_tensor(z[rows, h + first:h + HALF], csum[rows, h + first - 1:h + HALF - 1],
                                             dA[rows, h + first:h + HALF], ALU.mult))
                    dve.tensor_tensor(y[rows, h + first:h + HALF], csum[rows, h + first:h + HALF],
                                      z[rows, h + first:h + HALF], ALU.subtract).then_inc(y_ready, 1)
                for c in range(2):
                    dve.wait_ge(cy_ready, 2 * p + c + 1)
                    dve.wait_ge(sres_ready, 2 * p + c + 1)
                    dve.tensor_tensor(cut(gated, c), ps[:, 4 + c, :], cut(sres, c), ALU.mult).then_inc(g_ready, 1)
                for c in range(2):
                    dve.wait_ge(outw_ready, 2 * p + c + 1)
                    dve.wait_ge(xconv_ready, 2 * p + c + 1)
                    dve.scalar_tensor_tensor(cut(mix[:, p, :], c), ps[:, 6 + c, :], par("out_b"), cut(xconv, c), ALU.add,
                                             ALU.add, accum_out=sums[:, 2 * p + c:2 * p + c + 1]).then_inc(o_ready, 1)

            for p in range(PAIRS):
                mixer_conv(p)
                mixer_scan(p)

            dve.wait_ge(o_ready, UNITS)
            dve.tensor_reduce(tot, sums, AX.X, ALU.add).then_inc(tot_ready, 1)
            dve.wait_ge(bnmean_ready, 1)
            dve.tensor_scalar(negmean, ps[:, 4, 0:1], -1.0, None, ALU.mult).then_inc(negmean_ready, 1)
            dve.wait_ge(sqs_ready, 2)
            dve.tensor_tensor(vtot, sqs[:, 0:1], sqs[:, 1:2], ALU.add).then_inc(vtot_ready, 1)
            dve.wait_ge(bnrstd_ready, 1)
            dve.wait_ge(negmean_ready, 1)
            settle(dve.tensor_tensor(bnscale, bnscale, par("gamma"), ALU.mult))
            for u in range(UNITS):
                m, h = cut(mix[:, u // 2, :], u % 2), cut(H[:, u // 2, :], u % 2)
                settle(dve.tensor_scalar(m, m, negmean, bnscale, ALU.add, ALU.mult))
                dve.scalar_tensor_tensor(h, m, par("beta"), h, ALU.add, ALU.add).then_inc(h2_ready, 1)

            dve.wait_ge(patches_ready, BATCH)
            for u in range(UNITS):
                m = cut(ms[u // 2], u % 2)
                dve.wait_ge(s2_ready, u + 1)
                dve.tensor_tensor(m, m, ps[:, 4 + u, :], ALU.mult).then_inc(ms_ready, 1)
                settle(dve.tensor_tensor(cut(normed[:, u // 2, :], u % 2), ps[:, u, :], cut(inv2[u // 2], u % 2), ALU.mult))
            for u in range(UNITS):
                dve.wait_ge(r_ready, u + 1)
                dve.scalar_tensor_tensor(cut(hr[u // 2], u % 2), cut(normed[:, u // 2, :], u % 2), par("ln1"),
                                         cut(ms[u // 2], u % 2), ALU.mult, ALU.mult).then_inc(hr_ready, 1)

            dve.wait_ge(rope_in, 32)

            def rotate(i):
                kind, p, c = rot_items[i]
                rows = slice(0, P) if kind == "q" else slice(64 * p, 64 * p + 64)
                u = 2 * p + c
                dve.wait_ge(rot_ready, i + 1)
                dve.tensor_tensor(cut(prod_cos, i % 2)[rows], ps[rows, u, :], cut(cos_t, c)[rows],
                                  ALU.mult).then_inc(dve_step, 1)
                done[0] += 1
                dve.wait_ge(dve_step, done[0])
                dve.tensor_tensor(cut(prod_sin, i % 2)[rows], ps[rows, 4 + u, :], cut(sin_t, c)[rows],
                                  ALU.mult).then_inc(rot_taken, 1)

            def low_part(i):
                kind, p, c = rot_items[i]
                rows = slice(0, P) if kind == "q" else slice(64 * p, 64 * p + 64)
                hi, lo = (high[:, p, :], low[:, p, :]) if kind == "q" else (khigh, klow)
                dve.wait_ge(rot_high, i + 1)
                dve.tensor_tensor(cut(lo, c)[rows], cut(prod_cos, i % 2)[rows], cut(hi, c)[rows].bitcast(F32),
                                  ALU.subtract).then_inc(rot_split, 1)

            for i in range(len(rot_items) + 1):
                if i < len(rot_items):
                    if i >= 2:
                        dve.wait_ge(rot_split, i - 1)
                    rotate(i)
                if i:
                    low_part(i - 1)

            def find_max(b, i):
                tb, s0, ns, h, nh = units[i]
                bank = (SLOTS * b + i) % 3
                dve.wait_ge(scores_ready, NU * b + i + 1)
                if b and i == 0:
                    dve.wait_ge(max_turned, b)
                src = ps[:, bank, 0:nh * ns * P].rearrange("p (h s) -> p h s", h=nh)
                dst = maxima[:, h:h + nh, tb] if s0 == 0 else maxima_far[:, h:h + nh, tb - 4]
                dve.tensor_reduce(dst, src, AX.X, ALU.max).then_inc(maxed, 1)

            def finish_max(b):
                dve.wait_ge(maxed, NU * (b + 1))
                dve.tensor_tensor(maxima[:, :, 4:8], maxima[:, :, 4:8], maxima_far, ALU.max).then_inc(maxima_ready, 1)
                bank = (SLOTS * b + NU) % 3
                dve.wait_ge(max_turned, b + 1)
                if b:
                    dve.wait_ge(m_in[(b - 1) % 2], 16 * 4 * ((b - 1) // 2 + 1))
                dve.tensor_scalar(negmax[:, 0, :], ps[0:32, bank, 0:P], -1.0, None, ALU.mult).then_inc(negmax_ready, 1)
                dve.wait_ge(negmax_ready, 2 * b + 1)
                dve.scalar_tensor_tensor(negmax[:, 1, :], ps[0:32, bank, 0:P], -1.0, negmax[:, 0, :].bitcast(F32),
                                         ALU.mult, ALU.subtract).then_inc(negmax_ready, 1)

            def bcast(col):
                return col.rearrange("p (n e) -> p n e", e=1).broadcast_to([P, 16, EXPERTS])

            ident8 = par("expert_id").rearrange("p (n e) -> p n e", n=1).broadcast_to([P, 16, EXPERTS])

            def side(i):
                name, p, c = side_order[i]
                bank = side_bank(i)
                if name == "den":
                    n = den_index(p, c)
                    dve.wait_ge(rden_ready, n + 1)
                    dve.wait_ge(o_out, 2 * p + 2)
                    if n >= 4:
                        dve.wait_ge(wo_ready, n % 2 + 1)
                    dve.tensor_tensor(attn_n[:, n % 4, :], cut(attn_o[p], c), cut(rden, n % 2), ALU.mult).then_inc(attn_ready, 1)
                elif name == "wo":
                    x1 = cut(mix[:, p, :], c)
                    dve.wait_ge(wo_ready, 2 * p + c + 1)
                    dve.tensor_tensor(x1, ps[:, bank, :], cut(normed[:, p, :], c), ALU.add).then_inc(x1_ready, 1)
                    dve.wait_ge(x1_ready, 2 * p + c + 1)
                    if p:
                        dve.wait_ge(flat_ready, c + 1)
                    dve.tensor_tensor(cut(sq3, c), x1, x1, ALU.mult).then_inc(sq3_ready, 1)
                elif name == "var":
                    x1 = cut(mix[:, p, :], c)
                    dve.wait_ge(inv3_ready, 2 * p + c + 1)
                    if p:
                        dve.wait_ge(logit_ready, 1)
                    dve.scalar_tensor_tensor(cut(flat, c), x1, par("ln2"), cut(inv3, c), ALU.mult, ALU.mult).then_inc(flat_ready, 1)
                    dve.wait_ge(flat_ready, 2 * p + c + 1)
                    hi, lo = cut(part_high[p], c), cut(part_low[p], c)
                    dve.tensor_copy(hi, cut(flat, c)).then_inc(high3, 1)
                    dve.wait_ge(high3, 2 * p + c + 1)
                    dve.tensor_tensor(lo, cut(flat, c), hi.bitcast(F32), ALU.subtract).then_inc(split3, 1)
                    h = cut(H[:, p, :], c)
                    dve.tensor_tensor(h, h, x1, ALU.add).then_inc(base_ready, 1)
                elif name == "route":
                    lg = ps[:, bank, 0:P].rearrange("p (n e) -> p n e", e=EXPERTS)
                    dve.wait_ge(logit_ready, p + 1)
                    if p:
                        dve.wait_ge(wT_ready, p)
                    settle(dve.tensor_reduce(r_m, lg, AX.X, ALU.max))
                    dve.tensor_tensor(rt[1], lg, bcast(r_m), ALU.subtract).then_inc(rdiff, 1)
                elif name == "pick":
                    dve.wait_ge(rexp, p + 1)
                    settle(dve.tensor_reduce(r_den, rt[1], AX.X, ALU.add))
                    settle(dve.reciprocal(r_den, r_den))
                    settle(dve.tensor_tensor(rt[0], rt[1], bcast(r_den), ALU.mult))
                    settle(dve.tensor_reduce(r_m, rt[0], AX.X, ALU.max))
                    settle(dve.tensor_tensor(rt[2], rt[0], bcast(r_m), ALU.is_equal))
                    settle(dve.tensor_tensor(rt[2], rt[2], ident8, ALU.mult))
                    settle(dve.tensor_reduce(r_min, rt[2], AX.X, ALU.min))
                    settle(dve.tensor_tensor(rt[3], ident8, bcast(r_min), ALU.is_equal))
                    settle(dve.scalar_tensor_tensor(rt[4], rt[3], -2.0, rt[0], ALU.mult, ALU.add))
                    settle(dve.tensor_reduce(r_m2, rt[4], AX.X, ALU.max))
                    settle(dve.tensor_tensor(rt[5], rt[4], bcast(r_m2), ALU.is_equal))
                    settle(dve.tensor_tensor(rt[5], rt[5], ident8, ALU.mult))
                    settle(dve.tensor_reduce(r_min, rt[5], AX.X, ALU.min))
                    settle(dve.tensor_tensor(rt[2], ident8, bcast(r_min), ALU.is_equal))
                    settle(dve.tensor_tensor(rt[3], rt[3], rt[2], ALU.add))
                    settle(dve.scalar_tensor_tensor(r_den, r_m, 1e-9, r_m2, ALU.add, ALU.add))
                    settle(dve.reciprocal(r_den, r_den))
                    settle(dve.tensor_tensor(rt[3], rt[3], rt[0], ALU.mult))
                    dve.tensor_tensor(rt[6], rt[3], bcast(r_den), ALU.mult).then_inc(rw_ready, 1)

            for i in range(NU):
                find_max(0, i)
            finish_max(0)
            for b in range(BATCH):
                if b + 1 < BATCH:
                    for i in range(NU):
                        find_max(b + 1, i)
                    finish_max(b + 1)
                else:
                    for k in range(NB):
                        for i in attn_at.get((b, k), []):
                            side(i)

            def scale_y(m):
                k, q = divmod(m, EPAIRS)
                b = k // 2
                dve.wait_ge(y2_ready, m + 1)
                if q == 0 and k % 2 == 0:
                    dve.wait_ge(gates_in[b], 16 * EXPERTS)
                if m >= 2:
                    kk, qq = divmod(m - 2, EPAIRS)
                    dve.wait_ge(acc_step, 3 * kk + max(qq, 1))
                dve.tensor_tensor(gated_y[:, m % 2, :], ps[:, 4 + m % 2, :],
                                  gates[:, b % 2, q, HALF * (k % 2):HALF * (k % 2 + 1)], ALU.mult).then_inc(gy_ready, 1)

            dve.wait_ge(w_split, 3)
            total = CHUNKS * EPAIRS * HTILES
            for n in range(total):
                dve.wait_ge(silu_ready, n + 1)
                dve.wait_ge(h3_ready, n + 1)
                if n >= 4:
                    dve.wait_ge(hid_used, used_after(n - 4))
                dve.tensor_tensor(hid[:, n % 4, :], silu1[:, n % 4, :], ps[:, 2 + n % 2, :], ALU.mult).then_inc(hid_ready, 1)
                if n >= 5 and n % 3 == 2:
                    scale_y((n - 5) // 3)
                for i in moe_at.get(n, []):
                    side(i)
            scale_y(CHUNKS * EPAIRS - 1)

        @block.tensor
        def _(pe):
            pe.wait_ge(tokw_in, 32)
            for o in range(CHAN // 2):
                mm = pe.matmul(ps[:, 7, PATCH * o:PATCH * (o + 1)],
                               tokW[:, 2 * o:2 * o + 2, :].rearrange("k o c -> k (o c)"), dft, start=True, stop=True)
            mm.then_inc(weff_ready, 1)

            def patches(b):
                pe.wait_ge(x_in[b], 64)
                pe.wait_ge(weff_placed, 8)
                xb = xs[b % 3]
                for r in range(STRIDE):
                    first, last = r == 0, r == STRIDE - 1
                    pe.matmul(ps[0:CHAN, b, :], spec[:, 0, r, :], xb[:, 0:NM, r, :], start=first, stop=last)
                    pe.matmul(ps[CHAN:P, b, :], spec[:, 1, r, :], xb[:, 0:NM, r, :], start=first, stop=False)
                    mm = pe.matmul(ps[CHAN:P, b, :], spec[:, 2, r, :], xb[:, 1:NM + 1, r, :], start=False, stop=last)
                mm.then_inc(patches_ready, 1)

            def one(bank, lhsT, rhs, rows=slice(0, P)):
                return pe.matmul(ps[rows, bank, :], lhsT, rhs, start=True, stop=True)

            def mixer_norm(p):
                pe.wait_ge(h_ready, 4 * (p + 1))
                for c in range(2):
                    if p:
                        pe.wait_ge(g_ready, c + 1)
                    one(4 + c, par("center"), cut(H[:, p, :], c)).then_inc(centered, 1)
                for c in range(2):
                    pe.wait_ge(sq_ready, 2 * p + c + 1)
                    if p:
                        pe.wait_ge(o_ready, c + 1)
                    one(6 + c, par("chan_mean"), cut(sq, c)).then_inc(var_ready, 1)
                for c in range(2):
                    pe.wait_ge(hn_ready, 2 * p + c + 1)
                    one(4 + c, par("in_x"), cut(hn, c)).then_inc(xp_ready, 1)
                    one(6 + c, par("in_r"), cut(hn, c)).then_inc(res_ready, 1)

            def mixer_out(p):
                rows = slice(32 * p, 32 * p + 32)
                for c in range(2):
                    pe.wait_ge(xconv_ready, 2 * p + c + 1)
                    one(4 + c, par("ssm_dt"), cut(xconv, c), rows)
                    pe.wait_ge(sres_ready, 2 * p + c + 1)
                    one(6 + c, par("ssm_B"), cut(xconv, c), rows).then_inc(ssm_ready, 1)
                for c in range(2):
                    pe.wait_ge(y_ready, 2 * p + c + 1)
                    one(4 + c, par("ssm_C", rows), cut(y, c)[rows]).then_inc(cy_ready, 1)
                for c in range(2):
                    pe.wait_ge(g_ready, 2 * p + c + 1)
                    one(6 + c, par("out_w"), cut(gated, c)).then_inc(outw_ready, 1)

            patches(0)
            patches(1)
            pe.wait_ge(params_in, 16)
            mixer_norm(0)
            patches(2)
            mixer_out(0)
            patches(3)
            mixer_norm(1)
            mixer_out(1)

            pe.wait_ge(tot_ready, 1)
            pe.matmul(ps[:, 4, 0:1], par("bn_mean"), tot, start=True, stop=True).then_inc(bnmean_ready, 1)
            pe.wait_ge(vtot_ready, 1)
            pe.matmul(ps[:, 5, 0:1], par("bn_mean"), vtot, start=True, stop=True).then_inc(bnvar_ready, 1)

            for u in range(UNITS):
                pe.wait_ge(h2_ready, u + 1)
                one(u, par("center"), cut(H[:, u // 2, :], u % 2)).then_inc(centered2, 1)
            for u in range(UNITS):
                pe.wait_ge(sq2_ready, u + 1)
                one(4 + u, par("chan_mean"), cut(sq2[u // 2], u % 2)).then_inc(var2_ready, 1)
            taken = 0
            for i, (kind, p, c) in enumerate(rot_items):
                u = 2 * p + c
                src = cut(hr[p], c)
                if kind == "q":
                    pe.wait_ge(hr_ready, u + 1)
                    one(u, par("wq"), src)
                    one(4 + u, par("wq_rot"), src).then_inc(rot_ready, 1)
                else:
                    rows = slice(64 * p, 64 * p + 64)
                    pe.wait_ge(rot_taken, i - 1)
                    one(u, par("wk"), src, rows)
                    one(4 + u, par("wk_rot"), src, rows).then_inc(rot_ready, 1)
                if kind == "k" and c == 1:
                    for cc in range(2):
                        uu = 2 * p + cc
                        pe.wait_ge(rot_taken, i + cc)
                        for half in range(2):
                            hrows = slice(CHAN * half, CHAN * (half + 1))
                            for j in range(4):
                                t0 = HALF * cc + P * j
                                mm = pe.matmul(ps[:, uu + 4 * half, 32 * j:32 * (j + 1)], hr[p][hrows, t0:t0 + P],
                                               par("wv", hrows), start=True, stop=True)
                            mm.then_inc(v_ready, 1)

            pe.wait_ge(masks_in, 16)
            pe.wait_ge(v_placed, 2 * UNITS)
            ident_b, mask_ts, mask_st = masks[:, 0, :], masks[:, 1, :], masks[:, 2, :]

            def max_slot(b, i):
                slot = SLOTS * b + i
                bank = slot % 3
                if slot >= 3:
                    bb, ii = divmod(slot - 3, SLOTS)
                    if ii == NU:
                        pe.wait_ge(negmax_ready, 2 * (bb + 1))
                    else:
                        pe.wait_ge(maxed, NU * bb + ii + 1)
                if i == NU:
                    pe.wait_ge(maxima_ready, b + 1)
                    pe.transpose(ps[0:32, bank, 0:P], small[:, 16:48], par("ident")).then_inc(max_turned, 1)
                    return
                if i == 0:
                    pe.wait_ge(qk_in[b % 2], 16 * 18 * (b // 2 + 1))
                tb, s0, ns, h0, nh = units[i]
                for n in range(nh):
                    h = HEAD_ORDER[h0 + n]
                    at = n * ns * P
                    diag = s0 + ns == tb + 1
                    kt = KT[0:96, b % 2, h, P * s0:P * (s0 + ns)]
                    mm = pe.matmul(ps[:, bank, at:at + ns * P], QT[0:96, b % 2, h // 2, P * tb:P * (tb + 1)], kt,
                                   start=True, stop=not diag)
                    if diag:
                        mm = pe.matmul(ps[:, bank, at + (ns - 1) * P:at + ns * P], ident_b, mask_ts, start=False, stop=True)
                mm.then_inc(scores_ready, 1)

            def prob_unit(b, gi, g):
                half, j = groups[gi]
                n = 2 * (NG * b + gi) + g
                bank = 3 + 2 * (n % 2)
                t0, t1 = max(HALF * half, P * j), HALF * (half + 1)
                if n >= 2:
                    pe.wait_ge(probs_ready, n - 1)
                diag = t0 == P * j
                for a in range(2):
                    mm = pe.matmul(ps[:, bank + a, 0:t1 - t0], KT[0:100, b % 2, 2 * g + a, P * j:P * (j + 1)],
                                   QT[0:100, b % 2, g, t0:t1], start=True, stop=not diag)
                    if diag:
                        mm = pe.matmul(ps[:, bank + a, 0:P], ident_b, mask_st, start=False, stop=True)
                mm.then_inc(logits_t, 1)

            def pv_group(G):
                b, gi = divmod(G, NG)
                half, j = groups[gi]
                t0, t1 = max(HALF * half, P * j), HALF * (half + 1)
                pe.wait_ge(probs_ready, 2 * G + 2)
                if j == 0 and G:
                    pe.wait_ge(o_out, 2 * b + (1 - half))
                for h in range(HEADS):
                    mm = pe.matmul(ps[32 * h:32 * h + 32, 7, t0 - HALF * half:HALF], V[:, b, j, h // 2, :],
                                   PT[:, G % 4, h, 0:t1 - t0], start=(j == 0), stop=(j == (SBLK - 1 if half else SBLK // 2 - 1)))
                mm.then_inc(pv_done, 1)

            def side_free(i):
                j = i - 3 if i < NSA else i - 1
                if i == NSA:
                    pe.wait_ge(o_out, 2 * BATCH)
                    return
                if j < 0:
                    return
                name, p, c = side_order[j]
                if name == "den":
                    pe.wait_ge(rden_ready, den_index(p, c) + 1)
                elif name == "wo":
                    pe.wait_ge(x1_ready, 2 * p + c + 1)
                elif name == "var":
                    pe.wait_ge(inv3_ready, 2 * p + c + 1)
                elif name == "route":
                    pe.wait_ge(rdiff, p + 1)
                elif name == "turn":
                    pe.wait_ge(wT_out, p + 1)

            def side(i):
                name, p, c = side_order[i]
                bank = side_bank(i)
                if name == "pick":
                    return
                side_free(i)
                if name == "turn":
                    side_free(i - 1 if i < NSA else i)
                if name == "den":
                    pe.wait_ge(o_out, 2 * p + 2)
                    one(bank, par("den_sel"), cut(attn_o[p], c)).then_inc(den_ready, 1)
                elif name == "wo":
                    for half in range(2):
                        n = den_index(2 * p + half, c)
                        pe.wait_ge(attn_ready, n + 1)
                        mm = one(bank, par("wo"), attn_n[:, n % 4, :], slice(CHAN * half, CHAN * (half + 1)))
                    mm.then_inc(wo_ready, 1)
                elif name == "var":
                    pe.wait_ge(sq3_ready, 2 * p + c + 1)
                    one(bank, par("chan_mean"), cut(sq3, c)).then_inc(var3_ready, 1)
                elif name == "route":
                    pe.wait_ge(flat_ready, 2 * p + 2)
                    for j in range(SBLK):
                        mm = pe.matmul(ps[:, bank, 16 * j:16 * (j + 1)], flat[:, P * j:P * (j + 1)], par("router"),
                                       start=True, stop=True)
                    mm.then_inc(logit_ready, 1)
                elif name == "turn":
                    pe.wait_ge(rw_ready, p + 1)
                    pe.transpose(ps[:, bank, 0:P], rt[6].rearrange("p n e -> p (n e)"), par("ident")).then_inc(wT_ready, 1)

            for i in range(SLOTS):
                max_slot(0, i)
            for b in range(BATCH):
                at = 0
                pe.wait_ge(m_in[b % 2], 16 * 4 * (b // 2 + 1))
                for gi in range(NG):
                    for g in range(KV):
                        k = 2 * gi + g
                        prob_unit(b, gi, g)
                        if b + 1 < BATCH:
                            while at < a_until(k):
                                max_slot(b + 1, at)
                                at += 1
                        for i in attn_at.get((b, k), []):
                            side(i)
                    G = NG * b + gi
                    if G:
                        pv_group(G - 1)
            pv_group(NG * BATCH - 1)

            pe.wait_ge(w_split, 3)
            pe.wait_ge(w2_in, 16)
            w1h, w1l, w3h = (w.rearrange("p (q i c) -> p q i c", q=EPAIRS, i=HTILES) for w in (w1_high, w1_low, w3_high))
            w3l = [w.rearrange("p (q i c) -> p q i c", q=EPAIRS // 2, i=HTILES) for w in w3_low]

            def up(n):
                m, i = divmod(n, HTILES)
                k, q = divmod(m, EPAIRS)
                if i == 0 and q == 0 and k % 2 == 0:
                    pe.wait_ge(tok_in[k // 2], 32)
                tk = cut(toks[k // 2], k % 2)
                if n >= 2:
                    pe.wait_ge(silu_ready, n - 1)
                pe.matmul(ps[:, n % 2, :], w1h[:, q, i, :], tk, start=True, stop=False)
                pe.matmul(ps[:, n % 2, :], w1l[:, q, i, :], tk, start=False, stop=True).then_inc(h1_ready, 1)
                if n >= 2:
                    pe.wait_ge(hid_ready, n - 1)
                pe.matmul(ps[:, 2 + n % 2, :], w3h[:, q, i, :], tk, start=True, stop=False)
                pe.matmul(ps[:, 2 + n % 2, :], w3l[q // 2][:, q % 2, i, :], tk, start=False, stop=True).then_inc(h3_ready, 1)

            def down(t, i, odd, start, stop):
                m = t // HTILES
                rows = slice(CHAN, P) if odd else slice(0, CHAN)
                return pe.matmul(ps[rows, 4 + m % 2, :], w2[:, m % EPAIRS, i + odd, :], hid[:, t % 4, :], start=start, stop=stop)

            total = CHUNKS * EPAIRS * HTILES

            def downs(t):
                m, i = divmod(t, HTILES)
                if i == 2 and t < total - 1:
                    return
                pe.wait_ge(hid_ready, t + 1)
                if i == 0:
                    if m:
                        down(t - 1, 2, 1, False, True).then_inc(y2_ready, 1)
                    if m >= 2:
                        pe.wait_ge(gy_ready, m - 1)
                    down(t, 0, 0, True, False).then_inc(hid_used, 1)
                elif i == 1:
                    down(t, 1, 0, False, True)
                    down(t, 1, 1, True, False).then_inc(hid_used, 1)
                else:
                    down(t, 2, 1, False, True).then_inc(y2_ready, 1)

            def finish(k):
                pe.wait_ge(base_ready, 2 * (k // 4) + k % 2 + 1)
                pe.wait_ge(acc_step, 3 * (k + 1))
                if k:
                    pe.wait_ge(fin_out, k)
                b = k // 2
                for blk in range(4):
                    t0 = HALF * (k % 2) + P * blk
                    pe.matmul(ps[:, 6, CHAN * blk:CHAN * (blk + 1)], H[:, b // 2, t0:t0 + P], par("pick%d" % (b % 2)),
                              start=(blk == 0), stop=False, skip_group_check=True)
                for blk in range(4):
                    mm = pe.matmul(ps[:, 6, CHAN * blk:CHAN * (blk + 1)], acc[:, k % 2, P * blk:P * (blk + 1)],
                                   par("ident2"), start=False, stop=True, skip_group_check=True)
                mm.then_inc(fin_ready, 1)

            per_chunk = EPAIRS * HTILES
            for n in range(total + 2):
                if n < total:
                    up(n)
                if n >= 2:
                    downs(n - 2)
                if n > per_chunk and n % per_chunk == 8:
                    finish(n // per_chunk - 1)
                for i in moe_at.get(n, []):
                    side(i)
            finish(CHUNKS - 1)


def _pair_diag(m):
    r, c = m.shape
    z = np.zeros((2 * r, 2 * c), np.float32)
    z[:r, :c] = m
    z[r:, c:] = m
    return z


def _constants():
    k = np.arange(PATCH)
    f = np.arange(NFREQ)[:, None]
    ang = 2.0 * np.pi * f * k / PATCH
    dft = np.concatenate([np.cos(ang), -np.sin(ang)], 0) / np.sqrt(PATCH)
    inv_freq = 1.0 / 10000.0 ** (np.arange(0, HD, 2, dtype=np.float32) / HD)
    freqs = np.outer(np.arange(TOK, dtype=np.float32), inv_freq)
    emb = np.concatenate([freqs, freqs], axis=-1).astype(np.float32)
    sign = np.where(np.arange(HD) < HD // 2, -1.0, 1.0)[:, None]
    rope = np.stack([np.tile(np.cos(emb).T, (P // HD, 1)), np.tile(sign * np.sin(emb).T, (P // HD, 1))])
    i = np.arange(P)
    masks = np.stack([np.eye(P), np.where(i[None, :] > i[:, None], NEG, 0.0), np.where(i[None, :] < i[:, None], NEG, 0.0)])
    eye64 = np.eye(CHAN)
    chan_mean = _pair_diag(np.full((CHAN, CHAN), 1.0 / CHAN))
    den_sel = np.zeros((P, P))
    for h in range(HEADS):
        den_sel[32 * h + HD, 32 * h:32 * h + 32] = 1.0
    return {"dft": dft, "rope": rope, "masks": masks, "center": np.eye(P) - chan_mean, "chan_mean": chan_mean,
            "bn_mean": np.tile(eye64, (2, 2)) / (BATCH * TOK), "den_sel": den_sel, "ident": np.eye(P),
            "ident2": np.tile(eye64, (2, 1)),
            "pick0": np.eye(P)[:, :CHAN], "pick1": np.eye(P)[:, CHAN:], "expert_id": np.tile(np.arange(EXPERTS) - float(EXPERTS), (P, 1)),
            "eps5": np.full((P, 1), 1e-5), "eps6": np.full((P, 1), 1e-6)}


def kernel(**inputs):
    import ml_dtypes
    import concourse.bacc as _bacc
    from concourse import mybir as _mybir
    from concourse.bass_utils import run_bass_kernel_spmd as _run

    a = {k: np.asarray(v) for k, v in inputs.items()}
    const = _constants()
    cols, total = param_columns()
    block = np.zeros((P, total), np.float32)

    def put(name, value):
        at, w = cols[name]
        block[:value.shape[0], at:at + w] = value

    def twice(v):
        v = v.reshape(CHAN, -1)
        return np.concatenate([v, v], 0)

    half = HD // 2
    rot = np.concatenate([np.arange(HD * n + half, HD * (n + 1)).tolist() + np.arange(HD * n, HD * n + half).tolist()
                          for n in range(HEADS)]).astype(int)
    in_w, in_b = a["L0_attn_in_w"], a["L0_attn_in_b"]
    put("in_x", _pair_diag(in_w[:CHAN].T))
    put("in_r", _pair_diag(in_w[CHAN:].T))
    put("ssm_dt", _pair_diag(a["L0_attn_dt"]))
    put("ssm_B", _pair_diag(a["L0_attn_B_w"].T))
    put("ssm_C", np.concatenate([_pair_diag(a["L0_attn_C_w"].T)] * 2, 0))
    put("out_w", _pair_diag(a["L0_attn_out_w"].T))
    wq, wk = a["L0_ffn_wq"], a["L0_ffn_wk"]
    put("wq", _pair_diag(wq.T))
    put("wq_rot", _pair_diag(wq[rot].T))
    put("wk", _pair_diag(wk.T))
    put("wk_rot", _pair_diag(wk[rot[:KV * HD]].T))
    put("wv", twice(a["L0_ffn_wv"].T))
    wo = np.zeros((P, CHAN), np.float32)
    for h in range(HEADS):
        wo[32 * h:32 * h + HD] = a["L0_ffn_wo"][:, HD * h:HD * (h + 1)].T
    put("wo", wo)
    put("router", _pair_diag(a["L0_ffn_router_w"].T))
    put("conv_w", twice(a["L0_attn_conv_w"]))
    for name, v in (("conv_b", a["L0_attn_conv_b"]), ("in_b_x", in_b[:CHAN]), ("in_b_r", in_b[CHAN:]),
                    ("out_b", a["L0_attn_out_b"]), ("gamma", a["L0_attn_gamma"]), ("beta", a["L0_attn_beta"]),
                    ("ln1", a["L0_ffn_ln1_w"]), ("ln2", a["L0_ffn_ln2_w"])):
        put(name, twice(v))
    for name in ("center", "chan_mean", "bn_mean", "den_sel", "ident", "ident2", "pick0", "pick1", "expert_id", "eps5", "eps6"):
        put(name, const[name])

    def hidden(w):
        t = np.zeros((CHAN, EPAIRS, HTILES * P), np.float32)
        for e in range(EXPERTS):
            t[:, e // 2, HID * (e % 2):HID * (e % 2 + 1)] = w[e].T
        return t.reshape(CHAN, -1)

    w2 = a["L0_ffn_w2"]
    w2t = np.zeros((P, EPAIRS, 4, CHAN), np.float32)
    for q in range(EPAIRS):
        even, odd = w2[2 * q].T, w2[2 * q + 1].T
        cut = P - REST
        w2t[:, q, 0] = even[:P]
        w2t[:REST, q, 1] = even[P:]
        w2t[REST:, q, 2] = odd[:cut]
        w2t[:HID - cut, q, 3] = odd[cut:]
    arrays = {
        "x": a["x"], "tok_W": a["L0_tok_W"], "params": block, "dft": const["dft"].astype(np.float32),
        "rope": const["rope"].astype(np.float32), "masks": const["masks"].astype(ml_dtypes.bfloat16),
        "w1": hidden(a["L0_ffn_w1"]), "w3": hidden(a["L0_ffn_w3"]), "w2": w2t.reshape(P, -1),
    }
    nc = _bacc.Bacc("TRN2", target_bir_lowering=False, num_devices=1)
    feed, args = {}, []
    for name, v in arrays.items():
        v = np.ascontiguousarray(v)
        feed[f"in_{name}"] = v
        args.append(nc.dram_tensor(f"in_{name}", v.shape, _mybir.dt.from_np(v.dtype), kind="ExternalInput").ap())
    args.append(nc.dram_tensor("out_0", (BATCH, TOK, CHAN), F32, kind="ExternalOutput").ap())
    vit_tower(nc, *args)
    r = _run(nc, [feed], core_ids=[0])
    return r.results[0]["out_0"]
```

```python
from contextlib import ExitStack

import numpy as np

import concourse.bass as bass
from concourse import mybir

ALU = mybir.AluOpType
ACT = mybir.ActivationFunctionType
AX = mybir.AxisListType
F32 = mybir.dt.float32
F32R = mybir.dt.float32r
BF16 = mybir.dt.bfloat16

P = 128
BATCH, CHAN, TIME, VARS = 4, 64, 128, 64
PATCH, STRIDE = 16, 8
NPATCH = TIME // STRIDE
TOK = VARS * NPATCH
PAIRS = BATCH // 2
HALF = TOK // 2
NM = NPATCH // 2
NFREQ = PATCH // 2 + 1
OGRP = 4
TAPS = 4
HEADS, KV, HD = 4, 2, 16
SBLK = TOK // P
EXPERTS, HID = 8, 170
EPAIRS = EXPERTS // 2
HTILES = 3
REST = HID - P
CHUNKS = BATCH * 2
NEG = -1e30
EPS_LN, EPS_RMS = 1e-5, 1e-6

PARAMS = [("in_x", 128), ("in_r", 128), ("ssm_dt", 32), ("ssm_B", 32), ("ssm_C", 128), ("out_w", 128),
          ("wq", 128), ("wq_rot", 128), ("wk", 64), ("wk_rot", 64), ("wv", 32), ("wo", 64), ("router", 16),
          ("conv_w", 4), ("conv_b", 1), ("in_b_x", 1), ("in_b_r", 1), ("out_b", 1), ("gamma", 1), ("beta", 1),
          ("ln1", 1), ("ln2", 1),
          ("center", 128), ("chan_mean", 128), ("bn_mean", 128), ("den_sel", 128), ("ident", 128),
          ("ident2", 64), ("expert_id", 8), ("eps5", 1), ("eps6", 1), ("eps56", 1), ("head_rows", 4)]


def param_columns():
    at, out = 0, {}
    for name, width in PARAMS:
        out[name] = (at, width)
        at += width
    return out, at


HEAD_ORDER = [0, 2, 1, 3]


def max_units():
    units = []
    for tb, s0 in [(tb, 0) for tb in range(SBLK)] + [(tb, 4) for tb in range(4, SBLK)]:
        n = min(tb + 1 - s0, 4)
        heads = 4 // n if n < 3 else 1
        for h in range(0, HEADS, heads):
            units.append((tb, s0, n, h, heads))
    return units


def ring_slots(units):
    first = sum(u[0] < 4 for u in units)
    slots, begin = [], []
    for b in range(BATCH):
        begin.append(len(slots))
        own = [("unit", b, i) for i in range(len(units))]
        own.insert(first + 2, ("turn", b, 0))
        if b >= 2:
            own.insert(9, ("den", b - 2, 1))
            own.insert(5, ("den", b - 2, 0))
        slots += own + [("turn", b, 1)]
    return slots, begin + [len(slots)], first


def prob_groups():
    return [(0, j) for j in range(SBLK // 2)] + [(1, j) for j in range(SBLK)]


def vit_tower(nc, x, tok_W, params_d, dft_d, rope_d, masks_d, w1_d, w3_d, w2_d, out):
    cols, NPARAM = param_columns()
    units, groups = max_units(), prob_groups()
    NU, NG = len(units), len(groups)
    slots, begin, FIRST = ring_slots(units)
    ready_at = slots.index(("turn", 0, 0)) + 1
    UNITS = 2 * PAIRS

    with ExitStack() as ctx:
        def sb(name, shape, dt=F32):
            return ctx.enter_context(nc.sbuf_tensor(name, shape, dt))

        def sem(name):
            return ctx.enter_context(nc.semaphore(name))

        ps = ctx.enter_context(nc.psum_tensor("ps", [P, 8, HALF], F32))

        XSLOT = (NM + 1) * STRIDE * VARS
        early = sb("early", [P, 3 * XSLOT])
        work = sb("work", [P, 12 * TOK + 4])
        params = sb("params", [P, NPARAM])
        masks = sb("masks", [P, 3, P], BF16)
        spec = sb("spec", [P, 3, STRIDE, CHAN])
        H = sb("H", [P, PAIRS, TOK])
        mix = sb("mix", [P, PAIRS, TOK])
        high = sb("high", [P, PAIRS, TOK], F32R)
        low = sb("low", [P, PAIRS, TOK], F32R)
        khigh = sb("khigh", [P, TOK], F32R)
        klow = sb("klow", [P, TOK], F32R)
        QT = sb("QT", [P, 2, KV, TOK], F32R)
        KT = sb("KT", [P, 2, HEADS, TOK], F32R)
        small = sb("small", [P, 72])
        negmax = sb("negmax", [P, 2, 4, HEADS, 2], F32R)
        w_dram = nc.dram_tensor("routing_weights", [EXPERTS, BATCH * TOK], F32, kind="Internal").ap()

        def par(name, rows=slice(0, P)):
            a, w = cols[name]
            return params[rows, a:a + w]

        def tile(i):
            return work[:, i * TOK:(i + 1) * TOK]

        def cut(t, c):
            return t[:, HALF * c:HALF * (c + 1)]

        xs = [early[:, XSLOT * i:XSLOT * (i + 1)].rearrange("p (m r v) -> p m r v", r=STRIDE, v=VARS) for i in range(3)]
        normed = early[:, 0:2 * TOK].rearrange("p (a t) -> p a t", a=PAIRS)
        V = early[:, 2 * TOK:4 * TOK].rearrange("p (b j g d) -> p b j g d", b=BATCH, j=SBLK, g=KV)
        PT = early[:, 4 * TOK:12 * TOK].rearrange("p (i h t) -> p i h t", i=4, h=HEADS)
        gates = early[:, 4 * TOK:12 * TOK].rearrange("p (i q t) -> p i q t", i=2, q=EPAIRS)
        w2 = early[:, 12 * TOK:13 * TOK].rearrange("p (q s o) -> p q s o", q=EPAIRS, s=4)
        wT = early[:, 13 * TOK:13 * TOK + P]

        gated, hn, sres, xconv, rstd = tile(0), tile(1), tile(2), tile(3), tile(4)
        sq = gated
        dA, cprod, csum, zeros, z, y = tile(5), tile(6), tile(7), tile(8), tile(9), tile(10)
        xpad = work[:, 11 * TOK:12 * TOK + TAPS - 1]
        KDFT = 2 * NFREQ * OGRP
        tokW = work[0:KDFT, 3 * TOK:4 * TOK].rearrange("k (i m) -> k i m", m=P)
        dft = work[0:KDFT, 7 * TOK:7 * TOK + OGRP * PATCH]
        sq2 = [tile(0), tile(1)]
        inv2 = [tile(2), tile(3)]
        ms = [tile(4), tile(5)]
        hr = [tile(6), tile(7)]
        prod_cos, prod_sin = tile(8), tile(9)
        cos_t, sin_t = tile(10), tile(11)
        attn_o = [tile(b) for b in range(BATCH)]
        w1_raw = work[:, 6 * TOK:6 * TOK + 1536]
        w3_raw = work[:, 6 * TOK + 1536:9 * TOK]
        rden, sq3, inv3, flat = tile(9), tile(10), tile(10), tile(11)
        rt_flat = spec[:].rearrange("p a r o -> p (a r o)")
        rt = [rt_flat[:, P * i:P * (i + 1)].rearrange("p (n e) -> p n e", e=EXPERTS) for i in range(7)]
        r_m, r_min, r_m2, r_den = (rt_flat[:, 7 * P + 16 * i:7 * P + 16 * (i + 1)] for i in range(4))
        silu1 = early[:, 2 * TOK:4 * TOK].rearrange("p (i t) -> p i t", i=4)
        hid = work[:, 6 * TOK:8 * TOK].rearrange("p (i t) -> p i t", i=4)
        gated_y = tile(8).rearrange("p (i t) -> p i t", i=2)
        acc = tile(0).rearrange("p (i t) -> p i t", i=2)
        final = tile(1)[:, 0:512].rearrange("p (i b o) -> p i b o", i=2, b=4)
        kt_flat = KT[:].rearrange("p i h t -> p (i h t)")
        qt_flat = QT[:].rearrange("p i g t -> p (i g t)")
        NW = EPAIRS * HTILES * P
        w1_high, w1_low, w3_high = kt_flat[:, 0:NW], kt_flat[:, NW:2 * NW], qt_flat[:, 0:NW]
        w3_low = [khigh[:, 0:NW // 2], klow[:, 0:NW // 2]]
        toks = [kt_flat[:, 3 * TOK:4 * TOK], low[:, 1, :], kt_flat[:, 4 * TOK:5 * TOK], kt_flat[:, 5 * TOK:6 * TOK]]
        part_high = [high[:, 0, :], high[:, 1, :]]
        part_low = [low[:, 0, :], kt_flat[:, 6 * TOK:7 * TOK]]

        sums, sqs, tot, vtot = small[:, 0:4], small[:, 4:6], small[:, 6:7], small[:, 7:8]
        negmean, bnscale, bnshift = small[:, 8:9], small[:, 9:10], small[:, 10:11]
        maxima = small[:, 16:48].rearrange("p (c j h) -> p c h j", c=2, j=4)
        maxima_far = small[:, 48:64].rearrange("p (j h) -> p h j", j=4)

        params_in = sem("params_in"); tokw_in = sem("tokw_in"); rope_in = sem("rope_in"); masks_in = sem("masks_in")
        x_in = [sem(f"x_in{b}") for b in range(BATCH)]
        weff_ready = sem("weff_ready"); weff_placed = sem("weff_placed"); spec_blank = sem("spec_blank")
        patches_ready = sem("patches_ready"); h_ready = sem("h_ready")
        centered = sem("centered"); sq_ready = sem("sq_ready"); var_ready = sem("var_ready")
        rstd_ready = sem("rstd_ready"); hn_ready = sem("hn_ready"); xp_ready = sem("xp_ready")
        res_ready = sem("res_ready"); sres_ready = sem("sres_ready"); xconv_ready = sem("xconv_ready")
        tap_ready = sem("tap_ready"); csum_ready = sem("csum_ready")
        ssm_ready = sem("ssm_ready"); dA_ready = sem("dA_ready"); y_ready = sem("y_ready")
        cy_ready = sem("cy_ready"); g_ready = sem("g_ready"); outw_ready = sem("outw_ready"); o_ready = sem("o_ready")
        tot_ready = sem("tot_ready"); bnmean_ready = sem("bnmean_ready"); negmean_ready = sem("negmean_ready")
        sqs_ready = sem("sqs_ready"); vtot_ready = sem("vtot_ready"); bnvar_ready = sem("bnvar_ready")
        bnrstd_ready = sem("bnrstd_ready"); h2_ready = sem("h2_ready")
        affine_ready = sem("affine_ready"); bn_ready = sem("bn_ready")
        centered2 = sem("centered2"); sq2_ready = sem("sq2_ready"); var2_ready = sem("var2_ready")
        s2_ready = sem("s2_ready"); logs_ready = sem("logs_ready"); normed_ready = sem("normed_ready"); r_ready = sem("r_ready"); hr_ready = sem("hr_ready")
        rot_ready = sem("rot_ready"); rot_taken = sem("rot_taken"); rot_sum = sem("rot_sum")
        rot_high = sem("rot_high"); rot_split = sem("rot_split")
        v_ready = sem("v_ready"); v_placed = sem("v_placed"); v_blank = sem("v_blank"); kt_blank = sem("kt_blank")
        pads_blank = sem("pads_blank")
        keys_in = [sem(f"keys_in{i}") for i in range(2)]; queries_in = [sem(f"queries_in{b}") for b in range(BATCH)]; maxima_placed = sem("maxima_placed")
        scores_ready = sem("scores_ready"); maxed = sem("maxed")
        max_turned = sem("max_turned"); negmax_ready = sem("negmax_ready")
        logits_t = sem("logits_t"); probs_ready = sem("probs_ready"); pv_done = sem("pv_done"); o_out = sem("o_out")
        den_ready = sem("den_ready"); den_log = sem("den_log"); rden_ready = sem("rden_ready"); attn_ready = sem("attn_ready")
        wo_ready = sem("wo_ready"); x1_ready = sem("x1_ready"); sq3_ready = sem("sq3_ready")
        var3_ready = sem("var3_ready"); inv3_ready = sem("inv3_ready"); flat_ready = sem("flat_ready")
        high3 = sem("high3"); split3 = sem("split3"); base_ready = sem("base_ready")
        tok_in = [sem(f"tok_in{b}") for b in range(BATCH)]
        logit_ready = sem("logit_ready"); rdiff = sem("rdiff"); rexp = sem("rexp"); rw_ready = sem("rw_ready")
        wT_ready = sem("wT_ready"); wT_out = sem("wT_out"); w_stored = sem("w_stored")
        moe_w_in = sem("moe_w_in"); w2_in = sem("w2_in"); w_high = sem("w_high"); w_split = sem("w_split")
        gates_in = [[sem(f"gates_in{b}{q}") for q in range(EPAIRS)] for b in range(BATCH)]
        h1_ready = sem("h1_ready"); h3_ready = sem("h3_ready"); silu_ready = sem("silu_ready"); hid_ready = sem("hid_ready")
        hid_used = sem("hid_used"); y2_ready = sem("y2_ready"); gy_ready = sem("gy_ready"); acc_step = sem("acc_step")
        fin_ready = sem("fin_ready"); fin_out = sem("fin_out")
        stored = [sem(f"stored{i}") for i in range(2)]
        dve_step = sem("dve_step"); act_step = sem("act_step"); pool_step = sem("pool_step")

        block = ctx.enter_context(nc.Block())

        rot_items = [("q", 0, 0), ("q", 0, 1), ("k", 0, 0), ("k", 0, 1), ("q", 1, 0), ("q", 1, 1)]

        def rot_bank(i):
            return (4, 6, 0, 2)[i % 4]

        NB = 2 * NG
        NHALF = NB // 3
        UNITS_BY, TURN_AT = 5, 6
        AHEAD = 29

        def slots_until(b, k):
            if k < NHALF:
                start = ready_at if b == 0 else begin[b] + ahead(b)
                if k < TURN_AT:
                    left = begin[b + 1] - 1 - start
                    return start + min(left, -(-left * (k + 1) // UNITS_BY))
                return begin[b + 1]
            if b == BATCH - 1:
                return begin[BATCH]
            return begin[b + 1] + -(-ahead(b + 1) * (k + 1 - NHALF) // (NB - NHALF))

        def ahead(b):
            return AHEAD + (2 if b >= 2 else 0)

        def slot_bank(*slot):
            return slots.index(slot) % 3

        ring_after = {}
        for i, slot in enumerate(slots):
            if slot[0] != "unit" and i >= ready_at:
                n = next(n for n in range(BATCH * NB) if slots_until(*divmod(n, NB)) > i)
                ring_after.setdefault(n, []).append(slot)

        side_attn = [("wo", 0, 0, 7), ("wo", 0, 1, 8), ("var", 0, 0, 10), ("var", 0, 1, 11), ("den", 2, 0, 12),
                     ("route", 0, 0, 13), ("pick", 0, 0, 14), ("den", 2, 1, 15), ("pick", 0, 1, 15), ("pick", 0, 2, 16),
                     ("pick", 0, 3, 17), ("pick", 0, 4, 18), ("den", 3, 0, 19), ("turn", 0, 0, 20)]
        side_moe = [("den", 3, 1), ("wo", 1, 0), ("wo", 1, 1), ("var", 1, 0), ("var", 1, 1), ("route", 1, 0),
                    ("pick", 1, 0), ("pick", 1, 1), ("pick", 1, 2), ("pick", 1, 3), ("pick", 1, 4), ("turn", 1, 0)]
        side_order = [beat[:3] for beat in side_attn] + side_moe
        NSA = len(side_attn)
        attn_at = {}
        for i, beat in enumerate(side_attn):
            attn_at.setdefault((BATCH - 1, beat[3]), []).append(i)
        moe_when = {"den1": (2, 3, 4), "wo0": (5, 5, 6), "wo1": (7, 7, 8), "var0": (10, 11, 12), "var1": (10, 11, 13),
                    "route0": (15, 15, 16), "pick0": (17, 17, 18), "pick1": (19, 19, 20), "pick2": (21, 21, 22),
                    "pick3": (23, 23, 24), "pick4": (25, 25, 26), "turn0": (28, 29, 29)}
        moe_at = [{}, {}, {}]
        for i in range(NSA, len(side_order)):
            name, _, c = side_order[i]
            for e, n in enumerate(moe_when[name + str(c)]):
                moe_at[e].setdefault(n, []).append(i)
        side_bank, side_before, last_on = [], [], {}
        for i, (name, _, c) in enumerate(side_order):
            if name == "pick":
                side_bank.append(None)
                side_before.append(None)
                continue
            bank = (len(side_bank) % 3) if i < NSA else 7 if name == "turn" else 6 + c
            side_before.append(last_on.get(bank))
            side_bank.append(bank)
            last_on[bank] = i

        def den_index(b, c):
            return 2 * b + c

        def used_after(t):
            m, i = divmod(t, HTILES)
            return 2 * m + 1 + i

        def stack_queries(queue, b):
            p, buf, h0 = b // 2, b % 2, CHAN * (b % 2)
            for grp, part in enumerate((high, high, low)):
                for g in range(KV):
                    src = h0 + 32 * g
                    queue.dma_start(QT[32 * grp:32 * grp + 32, buf, g, :].bitcast(F32),
                                    part[src:src + 32, p, :].bitcast(F32)).then_inc(queries_in[b], 16)

        @block.sync
        def _(sp):
            def load_x(b):
                v = x[b].rearrange("c (m s r) v -> s c m (r v)", s=2, r=STRIDE)
                for s in range(2):
                    rows = slice(CHAN * s, CHAN * (s + 1))
                    sp.dma_start(xs[b % 3][rows, 0:NM].rearrange("p m r v -> p m (r v)"), v[s]).then_inc(x_in[b], 16)
                    sp.dma_start(xs[b % 3][rows, NM],
                                 x[b, :, TIME - 1:TIME, :].broadcast_to([CHAN, STRIDE, VARS])).then_inc(x_in[b], 16)

            for b in range(3):
                load_x(b)
            sp.dma_start(masks[:], masks_d.rearrange("m p s -> p m s")).then_inc(masks_in, 16)
            sp.wait_ge(patches_ready, 1)
            load_x(3)
            sp.wait_ge(cy_ready, UNITS)
            sp.dma_start(cos_t, rope_d[0]).then_inc(rope_in, 16)
            sp.dma_start(sin_t, rope_d[1]).then_inc(rope_in, 16)

            def stack_keys(b):
                p, buf = b // 2, b % 2
                sp.wait_ge(rot_split, 4)
                if b == 0:
                    sp.wait_ge(kt_blank, 2 * HEADS)
                if b >= 2:
                    sp.wait_ge(logits_t, NB * (b - 1))
                for grp, part in enumerate((khigh, klow, khigh)):
                    for h in range(HEADS):
                        src = 64 * p + 32 * (b % 2) + HD * (h // 2)
                        dst = 32 * grp + HD * (h % 2)
                        sp.dma_start(KT[dst:dst + HD, buf, h, :].bitcast(F32),
                                     part[src:src + HD, :].bitcast(F32)).then_inc(keys_in[buf], 16)

            sp.wait_ge(rot_split, 2)
            stack_queries(sp, 0)
            stack_keys(0)
            stack_queries(sp, 1)
            stack_keys(1)
            sp.wait_ge(v_ready, 2)
            sp.wait_ge(rot_split, len(rot_items))
            for rows in (slice(0, CHAN), slice(CHAN, P)):
                sp.dma_start(w1_raw[rows], w1_d).then_inc(moe_w_in, 16)
                sp.dma_start(w3_raw[rows], w3_d).then_inc(moe_w_in, 16)
            sp.dma_start(w2.rearrange("p q s o -> p (q s o)"), w2_d).then_inc(w2_in, 16)
            for b in (2, 3):
                stack_keys(b)

            for p in range(PAIRS):
                sp.wait_ge(split3, 2 * (p + 1))
                for b in (2 * p, 2 * p + 1):
                    rows = slice(CHAN * (b % 2), CHAN * (b % 2) + CHAN)
                    sp.dma_start(toks[b][0:CHAN].bitcast(F32), part_high[p][rows].bitcast(F32)).then_inc(tok_in[b], 16)
                    sp.dma_start(toks[b][CHAN:P].bitcast(F32), part_low[p][rows].bitcast(F32)).then_inc(tok_in[b], 16)
                sp.wait_ge(wT_out, p + 1)
                for j in range(SBLK):
                    sp.dma_start(w_dram[:, 2 * TOK * p:2 * TOK * (p + 1)].rearrange(
                        "e (b j s) -> j b e s", b=2, j=SBLK)[j], wT[16 * j:16 * (j + 1)]).then_inc(w_stored, 16)
                sp.wait_ge(w_stored, 16 * SBLK * (p + 1))
                for b in (2 * p, 2 * p + 1):
                    if b == 0:
                        sp.wait_ge(pv_done, NG * BATCH - 2)
                    if b == 1:
                        sp.wait_ge(pv_done, NG * BATCH)
                    if b >= 2:
                        sp.wait_ge(gy_ready, 2 * EPAIRS * (b - 1))
                    for e in range(EXPERTS):
                        sp.dma_start(gates[CHAN * (e % 2):CHAN * (e % 2 + 1), b % 2, e // 2, :],
                                     w_dram[e:e + 1, TOK * b:TOK * (b + 1)].broadcast_to([CHAN, TOK])
                                     ).then_inc(gates_in[b][e // 2], 16)

        @block.gpsimd
        def _(pool):
            done = [0]

            def settle(ins):
                done[0] += 1
                ins.then_inc(pool_step, 1)
                pool.wait_ge(pool_step, done[0])

            pool.memset(spec[:], 0.0).then_inc(spec_blank, 1)
            pool.memset(xpad[:, 0:TAPS - 1], 0.0).then_inc(pads_blank, 1)
            pool.memset(zeros, 0.0).then_inc(pads_blank, 1)
            pool.wait_ge(pads_blank, 2)
            pool.memset(kt_flat.bitcast(F32), 0.0).then_inc(pads_blank, 1)

            pool.wait_ge(patches_ready, BATCH)
            flatV = V.rearrange("p b j g d -> p (b j g) d")
            settle(pool.memset(flatV[:, :, HD:32], 0.0))
            pool.memset(flatV[:, :, HD:HD + 1], 1.0).then_inc(v_blank, 1)
            for i in range(len(rot_items)):
                pool.wait_ge(rot_taken, 2 * i + 2)
                a, b = cut(prod_cos, i % 2), cut(prod_sin, i % 2)
                pool.tensor_tensor(a, a, b, ALU.add).then_inc(rot_sum, 1)

            pool.wait_ge(rot_split, len(rot_items))
            for b in (2, 3):
                pool.wait_ge(logits_t, NB * (b - 1))
                stack_queries(pool, b)

            def parts_and_base(p):
                for c in range(2):
                    pool.wait_ge(high3, 2 * p + c + 1)
                    pool.tensor_tensor(cut(part_low[p], c), cut(flat, c), cut(part_high[p], c).bitcast(F32),
                                       ALU.subtract).then_inc(split3, 1)
                    h = cut(H[:, p, :], c)
                    pool.tensor_tensor(h, h, cut(mix[:, p, :], c), ALU.add).then_inc(base_ready, 1)

            pool.wait_ge(moe_w_in, 64)
            pool.wait_ge(logits_t, NB * 3)
            pool.wait_ge(keys_in[1], 2 * 12 * 16)
            pool.wait_ge(scores_ready, NU * BATCH)
            pool.tensor_copy(w1_high, w1_raw).then_inc(w_high, 1)
            pool.tensor_copy(w3_high, w3_raw).then_inc(w_high, 1)
            pool.wait_ge(w_high, 2)
            pool.tensor_tensor(w1_low, w1_raw, w1_high.bitcast(F32), ALU.subtract).then_inc(w_split, 1)
            for i in range(2):
                a, b = NW // 2 * i, NW // 2 * (i + 1)
                pool.tensor_tensor(w3_low[i], w3_raw[:, a:b], w3_high[:, a:b].bitcast(F32),
                                   ALU.subtract).then_inc(w_split, 1)

            parts_and_base(0)
            for k in range(CHUNKS):
                if k == 1:
                    parts_and_base(1)
                for q in range(1, EPAIRS):
                    m = EPAIRS * k + q
                    pool.wait_ge(gy_ready, m + 1)
                    if q == 1 and k >= 2:
                        pool.wait_ge(fin_ready, k - 1)
                    a = gated_y[:, 0, :] if q == 1 else acc[:, k % 2, :]
                    if q > 1:
                        pool.wait_ge(acc_step, 4 * k + q)
                    pool.tensor_tensor(acc[:, k % 2, :], a, gated_y[:, m % 2, :], ALU.add).then_inc(acc_step, 1)
                    if q == 1:
                        rows = slice(CHAN * (k // 2 % 2), CHAN * (k // 2 % 2 + 1))
                        pool.wait_ge(base_ready, 2 * (k // 4) + k % 2 + 1)
                        pool.wait_ge(acc_step, 4 * k + 1)
                        pool.tensor_tensor(acc[rows, k % 2, :], acc[rows, k % 2, :], cut(H[rows, k // 4, :], k % 2),
                                           ALU.add).then_inc(acc_step, 1)

        @block.scalar
        def _(act):
            done = [0]

            def settle(ins):
                done[0] += 1
                ins.then_inc(act_step, 1)
                act.wait_ge(act_step, done[0])

            act.dma_start(dft, dft_d).then_inc(tokw_in, 16)
            act.dma_start(tokW.rearrange("k i m -> k (i m)"), tok_W).then_inc(tokw_in, 16)
            act.dma_start(params[:], params_d).then_inc(params_in, 16)
            act.preload_act_table_set("natural_log_exp_and_others")
            act.wait_ge(params_in, 16)

            def patches_out(b):
                act.wait_ge(patches_ready, b + 1)
                dst = H[CHAN * (b % 2):CHAN * (b % 2 + 1), b // 2, :].rearrange("c (v m two) -> c two m v", m=NM, two=2)
                for two in range(2):
                    act.activation(dst[:, two], ps[CHAN * two:CHAN * (two + 1), b, :].rearrange("c (m v) -> c m v", v=VARS),
                                   ACT.Copy).then_inc(h_ready, 1)

            def mixer_norm(p):
                for c in range(2):
                    act.wait_ge(centered, 2 * p + c + 1)
                    if p:
                        act.wait_ge(outw_ready, c + 1)
                    act.activation(cut(sq, c), ps[:, 4 + c, :], ACT.Square).then_inc(sq_ready, 1)
                for c in range(2):
                    act.wait_ge(var_ready, 2 * p + c + 1)
                    settle(act.activation(cut(rstd, c), ps[:, 6 + c, :], ACT.Ln, bias=par("eps5")))
                    act.activation(cut(rstd, c), cut(rstd, c), ACT.Exp, scale=-0.5).then_inc(rstd_ready, 1)
                for c in range(2):
                    at = HALF * c
                    act.wait_ge(xp_ready, 2 * p + c + 1)
                    act.wait_ge(pads_blank, 1)
                    if p:
                        act.wait_ge(xconv_ready, 2)
                        act.wait_ge(o_ready, c + 1)
                    settle(act.activation(xpad[:, TAPS - 1 + at:TAPS - 1 + at + HALF], ps[:, 4 + c, :], ACT.Identity,
                                          bias=par("in_b_x")))
                    act.activation(cut(xconv, c), xpad[:, at:at + HALF], ACT.Identity, bias=par("conv_b"),
                                   scale=par("conv_w")[:, 0:1]).then_inc(tap_ready, 1)
                for c in range(2):
                    act.wait_ge(res_ready, 2 * p + c + 1)
                    act.activation(cut(sres, c), ps[:, 6 + c, :], ACT.Silu, bias=par("in_b_r")).then_inc(sres_ready, 1)
                act.preload_act_table_set("natural_log_exp_and_others")

            def mixer_decay(p):
                rows = slice(32 * p, 32 * p + 32)
                for c in range(2):
                    act.wait_ge(ssm_ready, 2 * p + c + 1)
                    act.activation(cut(dA, c)[rows], ps[rows, 4 + c, :], ACT.Exp).then_inc(dA_ready, 1)

            patches_out(0)
            patches_out(1)
            mixer_norm(0)
            mixer_decay(0)
            patches_out(2)
            patches_out(3)
            mixer_norm(1)
            mixer_decay(1)

            act.wait_ge(negmean_ready, 1)
            for p in range(PAIRS):
                act.activation(tile(1 + p), mix[:, p, :], ACT.Square, bias=negmean,
                               accum_out=sqs[:, p:p + 1]).then_inc(sqs_ready, 1)
            act.wait_ge(bnvar_ready, 1)
            settle(act.activation(bnscale, ps[:, 5, 0:1], ACT.Ln, bias=par("eps5")))
            act.activation(bnscale, bnscale, ACT.Exp, scale=-0.5).then_inc(bnrstd_ready, 1)

            for u in range(UNITS):
                m = cut(mix[:, u // 2, :], u % 2)
                act.wait_ge(affine_ready, 1)
                act.activation(m, m, ACT.Identity, bias=bnshift, scale=bnscale).then_inc(bn_ready, 1)

            act.wait_ge(sqs_ready, 2)
            for u in range(UNITS):
                act.wait_ge(centered2, u + 1)
                act.activation(cut(sq2[u // 2], u % 2), ps[:, u, :], ACT.Square).then_inc(sq2_ready, 1)
            for u in range(UNITS):
                s, m = cut(inv2[u // 2], u % 2), cut(ms[u // 2], u % 2)
                act.wait_ge(var2_ready, u + 1)
                act.activation(m, ps[:, 4 + u, :], ACT.Ln, bias=par("eps56"), scale=1.0 + EPS_RMS).then_inc(logs_ready, 1)
                act.activation(s, ps[:, 4 + u, :], ACT.Ln, bias=par("eps5")).then_inc(logs_ready, 1)
                act.wait_ge(logs_ready, 2 * u + 1)
                act.activation(m, m, ACT.Exp, scale=-0.5).then_inc(r_ready, 1)

            def layer_deviation(u):
                s = cut(inv2[u // 2], u % 2)
                act.wait_ge(logs_ready, 2 * u + 2)
                act.activation(s, s, ACT.Exp, scale=-0.5).then_inc(s2_ready, 1)

            def high_part(i):
                kind, p, c = rot_items[i]
                act.wait_ge(rot_sum, i + 1)
                act.activation(cut(high[:, p, :] if kind == "q" else khigh, c), cut(prod_cos, i % 2),
                               ACT.Copy).then_inc(rot_high, 1)

            def place_values(b):
                act.wait_ge(v_ready, b % 2 + 1)
                act.wait_ge(v_blank, 1)
                p = b // 2
                act.activation(V[:, b, :, :, 0:HD].rearrange("p j g d -> p (j g) d"),
                               ps[:, 3 + b % 2, 2 * P * p:2 * P * (p + 1)].rearrange("p (n d) -> p n d", d=HD),
                               ACT.Copy).then_inc(v_placed, 1)

            layer_deviation(0)
            layer_deviation(1)
            for i in range(len(rot_items)):
                high_part(i)
                if i == 0:
                    layer_deviation(2)
                    layer_deviation(3)
            for b in range(BATCH):
                place_values(b)

            def denominators_log(b, c, bank):
                n = den_index(b, c)
                act.wait_ge(den_ready, n + 1)
                if n >= 2:
                    act.wait_ge(attn_ready, n - 1)
                act.activation(cut(rden, n % 2), ps[:, bank, :], ACT.Ln).then_inc(den_log, 1)

            def denominators_inverse(b, c):
                n = den_index(b, c)
                act.wait_ge(den_log, n + 1)
                act.activation(cut(rden, n % 2), cut(rden, n % 2), ACT.Exp, scale=-1.0).then_inc(rden_ready, 1)

            def side(i):
                name, a, c = side_order[i]
                bank = side_bank[i]
                if name == "den":
                    denominators_log(a, c, bank)
                    denominators_inverse(a, c)
                elif name == "var":
                    act.wait_ge(var3_ready, 2 * a + c + 1)
                    settle(act.activation(cut(inv3, c), ps[:, bank, :], ACT.Ln, bias=par("eps6")))
                    act.activation(cut(inv3, c), cut(inv3, c), ACT.Exp, scale=-0.5).then_inc(inv3_ready, 1)
                elif name == "pick" and c == 0:
                    act.wait_ge(rdiff, a + 1)
                    act.activation(rt[1], rt[1], ACT.Exp).then_inc(rexp, 1)
                elif name == "turn":
                    act.wait_ge(wT_ready, a + 1)
                    if a:
                        act.wait_ge(w_stored, 16 * SBLK * a)
                    act.activation(wT, ps[:, bank, 0:P], ACT.Copy).then_inc(wT_out, 1)

            def output_half(b, half):
                act.wait_ge(pv_done, NG * b + (NG if half else SBLK // 2))
                act.activation(cut(attn_o[b], half), ps[:, 7, :], ACT.Copy).then_inc(o_out, 1)

            def place_max(b, half):
                act.wait_ge(max_turned, 2 * b + half + 1)
                if b >= 2:
                    act.wait_ge(logits_t, NB * (b - 1))
                bank = slot_bank("turn", b, half)
                for g in range(KV):
                    act.activation(cut(QT[96:104, b % 2, g, :], half), ps[96:104, bank, :],
                                   ACT.Copy).then_inc(maxima_placed, 1)

            place_max(0, 0)
            for b in range(BATCH):
                for gi, (half, j) in enumerate(groups):
                    w = HALF * (half + 1) - max(HALF * half, P * j)
                    G = NG * b + gi
                    if G >= 4:
                        act.wait_ge(pv_done, G - 3)
                    for g in range(KV):
                        n = 2 * G + g
                        bank = 3 + 2 * (n % 2)
                        act.wait_ge(logits_t, n + 1)
                        act.activation(PT[:, G % 4, 2 * g:2 * g + 2, 0:w], ps[:, bank:bank + 2, 0:w], ACT.Exp,
                                       scale=float(HD) ** -0.5).then_inc(probs_ready, 1)
                        for kind, bb, i in ring_after.get(n, []):
                            if kind == "turn":
                                place_max(bb, i)
                            else:
                                denominators_log(bb, i, slot_bank(kind, bb, i))
                        for kind, bb, i in ring_after.get(n - 1, []):
                            if kind == "den":
                                denominators_inverse(bb, i)
                        for i in attn_at.get((b, 2 * gi + g), []):
                            side(i)
                        if b and gi == 1 and g == 0:
                            output_half(b - 1, 1)
                        if gi == SBLK // 2 + 1 and g == 0:
                            output_half(b, 0)
            output_half(BATCH - 1, 1)

            def rows_out(k):
                act.wait_ge(fin_ready, k + 1)
                if k >= 2:
                    act.wait_ge(stored[k % 2], 16 * (k // 2))
                act.activation(final[:, k % 2], ps[:, 6, 0:256].rearrange("p (b o) -> p b o", b=4),
                               ACT.Copy).then_inc(fin_out, 1)
                act.wait_ge(fin_out, k + 1)
                act.dma_start(out[k // 2, HALF * (k % 2):HALF * (k % 2 + 1), :].rearrange("(b s) o -> s b o", b=4),
                              final[:, k % 2]).then_inc(stored[k % 2], 16)

            act.wait_ge(pv_done, NG * BATCH)
            per_chunk = EPAIRS * HTILES
            for n in range(CHUNKS * per_chunk):
                act.wait_ge(h1_ready, n + 1)
                if n >= 4:
                    act.wait_ge(hid_ready, n - 3)
                act.activation(silu1[:, n % 4, :], ps[:, n % 2, :], ACT.Silu).then_inc(silu_ready, 1)
                if n > per_chunk and n % per_chunk == 9:
                    rows_out(n // per_chunk - 1)
                if n in moe_at[1]:
                    if side_order[moe_at[1][n][0]][0] in ("den", "var") or side_order[moe_at[1][n][0]][::2] == ("pick", 0):
                        act.preload_act_table_set("natural_log_exp_and_others")
                    for i in moe_at[1][n]:
                        side(i)
            rows_out(CHUNKS - 1)
            for i in range(2):
                act.wait_ge(stored[i], 8 * CHUNKS)

        @block.vector
        def _(dve):
            done = [0]

            def settle(ins):
                done[0] += 1
                ins.then_inc(dve_step, 1)
                dve.wait_ge(dve_step, done[0])

            dve.wait_ge(spec_blank, 1)
            dve.wait_ge(weff_ready, 1)
            lo, hi = slice(0, CHAN), slice(CHAN, P)
            src = ps[:, 7, :].rearrange("p (i o r) -> p r i o", o=OGRP, r=PATCH)
            dst = spec[:].rearrange("p a r (i h o) -> p a h r i o", h=2, o=OGRP)
            for h, rows in enumerate((lo, hi)):
                dve.tensor_copy(dst[lo, 0, h], src[rows, 0:STRIDE]).then_inc(weff_placed, 1)
                dve.tensor_copy(dst[hi, 0, h], src[rows, STRIDE:PATCH]).then_inc(weff_placed, 1)
                dve.tensor_copy(dst[hi, 1, h], src[rows, 0:STRIDE]).then_inc(weff_placed, 1)
                dve.tensor_copy(dst[lo, 2, h], src[rows, STRIDE:PATCH]).then_inc(weff_placed, 1)
            dve.wait_ge(params_in, 16)
            dve.wait_ge(pads_blank, 3)
            for h in range(HEADS):
                for buf in range(2):
                    dve.tensor_scalar(KT[96:104, buf, h, :], zeros[96:104], par("head_rows", slice(96, 104))[:, h:h + 1],
                                      None, ALU.add).then_inc(kt_blank, 1)
            cw = par("conv_w")

            def mixer_conv(p):
                for c in range(2):
                    dve.wait_ge(rstd_ready, 2 * p + c + 1)
                    dve.tensor_tensor(cut(hn, c), ps[:, 4 + c, :], cut(rstd, c), ALU.mult).then_inc(hn_ready, 1)
                for c in range(2):
                    at = HALF * c
                    dve.wait_ge(tap_ready, 2 * p + c + 1)
                    xc = cut(xconv, c)
                    for k in range(1, TAPS):
                        ins = dve.scalar_tensor_tensor(xc, xpad[:, at + k:at + k + HALF], cw[:, k:k + 1], xc,
                                                       ALU.mult, ALU.add)
                        if k < TAPS - 1:
                            settle(ins)
                    ins.then_inc(xconv_ready, 1)

            def mixer_scan(p):
                rows = slice(32 * p, 32 * p + 32)
                for c in range(2):
                    h, first = HALF * c, 1 if c == 0 else 0
                    dve.wait_ge(dA_ready, 2 * p + c + 1)
                    start = 1.0 if c == 0 else cprod[rows, h - 1:h]
                    settle(dve.tensor_tensor_scan(cut(cprod, c)[rows], cut(dA, c)[rows], cut(zeros, c)[rows], start,
                                                  ALU.mult, ALU.add))
                    settle(dve.tensor_tensor(cut(z, c)[rows], cut(cprod, c)[rows], ps[rows, 6 + c, :], ALU.mult))
                    start = 0.0 if c == 0 else csum[rows, h - 1:h]
                    dve.tensor_tensor_scan(cut(csum, c)[rows], cut(z, c)[rows], cut(zeros, c)[rows], start,
                                           ALU.add, ALU.add).then_inc(csum_ready, 1)
                    dve.wait_ge(csum_ready, 2 * p + c + 1)
                    if c == 0:
                        settle(dve.tensor_copy(y[rows, 0:1], ps[rows, 6, 0:1]))
                    settle(dve.tensor_tensor(z[rows, h + first:h + HALF], csum[rows, h + first - 1:h + HALF - 1],
                                             dA[rows, h + first:h + HALF], ALU.mult))
                    dve.tensor_tensor(y[rows, h + first:h + HALF], csum[rows, h + first:h + HALF],
                                      z[rows, h + first:h + HALF], ALU.subtract).then_inc(y_ready, 1)
                for c in range(2):
                    dve.wait_ge(cy_ready, 2 * p + c + 1)
                    dve.wait_ge(sres_ready, 2 * p + c + 1)
                    dve.tensor_tensor(cut(gated, c), ps[:, 4 + c, :], cut(sres, c), ALU.mult).then_inc(g_ready, 1)
                for c in range(2):
                    dve.wait_ge(outw_ready, 2 * p + c + 1)
                    dve.wait_ge(xconv_ready, 2 * p + c + 1)
                    dve.scalar_tensor_tensor(cut(mix[:, p, :], c), ps[:, 6 + c, :], par("out_b"), cut(xconv, c), ALU.add,
                                             ALU.add, accum_out=sums[:, 2 * p + c:2 * p + c + 1]).then_inc(o_ready, 1)

            for p in range(PAIRS):
                mixer_conv(p)
                mixer_scan(p)

            dve.wait_ge(o_ready, UNITS)
            dve.tensor_reduce(tot, sums, AX.X, ALU.add).then_inc(tot_ready, 1)
            dve.wait_ge(bnmean_ready, 1)
            dve.tensor_scalar(negmean, ps[:, 4, 0:1], -1.0, None, ALU.mult).then_inc(negmean_ready, 1)
            dve.wait_ge(sqs_ready, 2)
            dve.tensor_tensor(vtot, sqs[:, 0:1], sqs[:, 1:2], ALU.add).then_inc(vtot_ready, 1)
            dve.wait_ge(bnrstd_ready, 1)
            dve.wait_ge(negmean_ready, 1)
            settle(dve.tensor_tensor(bnscale, bnscale, par("gamma"), ALU.mult))
            dve.scalar_tensor_tensor(bnshift, negmean, bnscale, par("beta"), ALU.mult, ALU.add).then_inc(affine_ready, 1)
            for u in range(UNITS):
                m, h = cut(mix[:, u // 2, :], u % 2), cut(H[:, u // 2, :], u % 2)
                dve.wait_ge(bn_ready, u + 1)
                dve.tensor_tensor(h, h, m, ALU.add).then_inc(h2_ready, 1)

            dve.wait_ge(patches_ready, BATCH)
            def both_norms(u):
                dve.wait_ge(r_ready, u + 1)
                dve.scalar_tensor_tensor(cut(hr[u // 2], u % 2), ps[:, u, :], par("ln1"), cut(ms[u // 2], u % 2),
                                         ALU.mult, ALU.mult).then_inc(hr_ready, 1)

            def layer_norm(u):
                dve.wait_ge(s2_ready, u + 1)
                dve.tensor_tensor(cut(normed[:, u // 2, :], u % 2), ps[:, u, :], cut(inv2[u // 2], u % 2),
                                  ALU.mult).then_inc(normed_ready, 1)

            for u in range(3):
                both_norms(u)

            dve.wait_ge(rope_in, 32)
            dve.wait_ge(kt_blank, 2 * HEADS)

            def rotate(i):
                kind, p, c = rot_items[i]
                bank = rot_bank(i)
                dve.wait_ge(rot_ready, i + 1)
                dve.tensor_tensor(cut(prod_cos, i % 2), ps[:, bank, :], cut(cos_t, c), ALU.mult).then_inc(rot_taken, 1)
                dve.tensor_tensor(cut(prod_sin, i % 2), ps[:, bank + 1, :], cut(sin_t, c), ALU.mult).then_inc(rot_taken, 1)

            def low_part(i):
                kind, p, c = rot_items[i]
                hi, lo = (high[:, p, :], low[:, p, :]) if kind == "q" else (khigh, klow)
                dve.wait_ge(rot_high, i + 1)
                dve.tensor_tensor(cut(lo, c), cut(prod_cos, i % 2), cut(hi, c).bitcast(F32),
                                  ALU.subtract).then_inc(rot_split, 1)

            for i in range(len(rot_items) + 1):
                if i < len(rot_items):
                    if i >= 2:
                        dve.wait_ge(rot_split, i - 1)
                    rotate(i)
                if i:
                    low_part(i - 1)
                if i == 0:
                    both_norms(3)
                if i < 2:
                    layer_norm(2 * i)
                    layer_norm(2 * i + 1)

            def find_max(b, i):
                tb, s0, ns, h, nh = units[i]
                dve.wait_ge(scores_ready, NU * b + i + 1)
                if b and i == 0:
                    dve.wait_ge(negmax_ready, 4 * b)
                src = ps[:, slot_bank("unit", b, i), 0:nh * ns * P].rearrange("p (h s) -> p h s", h=nh)
                dst = maxima[:, tb // 4, h:h + nh, tb % 4] if s0 == 0 else maxima_far[:, h:h + nh, tb - 4]
                dve.tensor_reduce(dst, src, AX.X, ALU.max).then_inc(maxed, 1)

            def split_max(b, half):
                dve.wait_ge(maxed, NU * b + (NU if half else FIRST))
                if half:
                    settle(dve.tensor_tensor(maxima[:, 1], maxima[:, 1], maxima_far, ALU.max))
                if b:
                    dve.wait_ge(max_turned, 2 * b - 1 + half)
                parts = negmax[:, half].rearrange("p j h part -> p part h j")
                dve.tensor_scalar(parts[:, 0], maxima[:, half], -1.0, None, ALU.mult).then_inc(negmax_ready, 1)
                dve.wait_ge(negmax_ready, 4 * b + 2 * half + 1)
                dve.scalar_tensor_tensor(parts[:, 1], maxima[:, half], -1.0, parts[:, 0].bitcast(F32),
                                         ALU.mult, ALU.subtract).then_inc(negmax_ready, 1)

            def over_denominators(b, c):
                n = den_index(b, c)
                dve.wait_ge(rden_ready, n + 1)
                dve.wait_ge(o_out, 2 * b + c + 1)
                o = cut(attn_o[b], c)
                dve.tensor_tensor(o, o, cut(rden, n % 2), ALU.mult).then_inc(attn_ready, 1)

            def bcast(col):
                return col.rearrange("p (n e) -> p n e", e=1).broadcast_to([P, 16, EXPERTS])

            ident8 = par("expert_id").rearrange("p (n e) -> p n e", n=1).broadcast_to([P, 16, EXPERTS])

            def side(i):
                name, p, c = side_order[i]
                bank = side_bank[i]
                if name == "den":
                    over_denominators(p, c)
                elif name == "wo":
                    x1 = cut(mix[:, p, :], c)
                    dve.wait_ge(wo_ready, 2 * p + c + 1)
                    dve.tensor_tensor(x1, ps[:, bank, :], cut(normed[:, p, :], c), ALU.add).then_inc(x1_ready, 1)
                    dve.wait_ge(x1_ready, 2 * p + c + 1)
                    if p:
                        dve.wait_ge(flat_ready, c + 1)
                    dve.tensor_tensor(cut(sq3, c), x1, x1, ALU.mult).then_inc(sq3_ready, 1)
                elif name == "var":
                    x1 = cut(mix[:, p, :], c)
                    dve.wait_ge(inv3_ready, 2 * p + c + 1)
                    if p:
                        dve.wait_ge(logit_ready, 1)
                        dve.wait_ge(split3, c + 1)
                    dve.scalar_tensor_tensor(cut(flat, c), x1, par("ln2"), cut(inv3, c), ALU.mult, ALU.mult).then_inc(flat_ready, 1)
                    dve.wait_ge(flat_ready, 2 * p + c + 1)
                    dve.tensor_copy(cut(part_high[p], c), cut(flat, c)).then_inc(high3, 1)
                elif name == "route":
                    lg = ps[:, bank, 0:P].rearrange("p (n e) -> p n e", e=EXPERTS)
                    dve.wait_ge(logit_ready, p + 1)
                    if p:
                        dve.wait_ge(wT_ready, p)
                    settle(dve.tensor_reduce(r_m, lg, AX.X, ALU.max))
                    dve.tensor_tensor(rt[1], lg, bcast(r_m), ALU.subtract).then_inc(rdiff, 1)
                elif name == "pick" and c == 0:
                    dve.wait_ge(rexp, p + 1)
                    settle(dve.tensor_reduce(r_den, rt[1], AX.X, ALU.add))
                    settle(dve.reciprocal(r_den, r_den))
                    settle(dve.tensor_tensor(rt[0], rt[1], bcast(r_den), ALU.mult))
                elif name == "pick" and c == 1:
                    settle(dve.tensor_reduce(r_m, rt[0], AX.X, ALU.max))
                    settle(dve.tensor_tensor(rt[2], rt[0], bcast(r_m), ALU.is_equal))
                    settle(dve.tensor_tensor(rt[2], rt[2], ident8, ALU.mult))
                    settle(dve.tensor_reduce(r_min, rt[2], AX.X, ALU.min))
                elif name == "pick" and c == 2:
                    settle(dve.tensor_tensor(rt[3], ident8, bcast(r_min), ALU.is_equal))
                    settle(dve.scalar_tensor_tensor(rt[4], rt[3], -2.0, rt[0], ALU.mult, ALU.add))
                    settle(dve.tensor_reduce(r_m2, rt[4], AX.X, ALU.max))
                    settle(dve.tensor_tensor(rt[5], rt[4], bcast(r_m2), ALU.is_equal))
                elif name == "pick" and c == 3:
                    settle(dve.tensor_tensor(rt[5], rt[5], ident8, ALU.mult))
                    settle(dve.tensor_reduce(r_min, rt[5], AX.X, ALU.min))
                    settle(dve.tensor_tensor(rt[2], ident8, bcast(r_min), ALU.is_equal))
                elif name == "pick":
                    settle(dve.tensor_tensor(rt[3], rt[3], rt[2], ALU.add))
                    settle(dve.scalar_tensor_tensor(r_den, r_m, 1e-9, r_m2, ALU.add, ALU.add))
                    settle(dve.reciprocal(r_den, r_den))
                    settle(dve.tensor_tensor(rt[3], rt[3], rt[0], ALU.mult))
                    dve.tensor_tensor(rt[6], rt[3], bcast(r_den), ALU.mult).then_inc(rw_ready, 1)

            for at, (kind, b, i) in enumerate(slots):
                if kind == "unit":
                    find_max(b, i)
                    if i in (FIRST - 1, NU - 1):
                        split_max(b, 0 if i < FIRST else 1)
                if at >= 4 and slots[at - 4][0] == "den":
                    over_denominators(*slots[at - 4][1:])
            for k in range(NB):
                for i in attn_at.get((BATCH - 1, k), []):
                    side(i)

            def scale_y(m):
                k, q = divmod(m, EPAIRS)
                b = k // 2
                dve.wait_ge(y2_ready, m + 1)
                if k % 2 == 0:
                    dve.wait_ge(gates_in[b][q], 32)
                if m >= 2:
                    kk, qq = divmod(m - 2, EPAIRS)
                    dve.wait_ge(acc_step, 4 * kk + (qq + 1 if qq > 1 else 1))
                dve.tensor_tensor(gated_y[:, m % 2, :], ps[:, 4 + m % 2, :],
                                  gates[:, b % 2, q, HALF * (k % 2):HALF * (k % 2 + 1)], ALU.mult).then_inc(gy_ready, 1)

            dve.wait_ge(w_split, 3)
            total = CHUNKS * EPAIRS * HTILES
            for n in range(total):
                dve.wait_ge(silu_ready, n + 1)
                dve.wait_ge(h3_ready, n + 1)
                if n >= 4:
                    dve.wait_ge(hid_used, used_after(n - 4))
                dve.tensor_tensor(hid[:, n % 4, :], silu1[:, n % 4, :], ps[:, 2 + n % 2, :], ALU.mult).then_inc(hid_ready, 1)
                if n >= 5 and n % 3 == 2:
                    scale_y((n - 5) // 3)
                for i in moe_at[2].get(n, []):
                    side(i)
            scale_y(CHUNKS * EPAIRS - 1)

        @block.tensor
        def _(pe):
            pe.wait_ge(tokw_in, 32)
            W = OGRP * PATCH
            for i in range(CHAN // (2 * OGRP)):
                mm = pe.matmul(ps[:, 7, W * i:W * (i + 1)], tokW[:, i, :], dft, start=True, stop=True)
            mm.then_inc(weff_ready, 1)

            def patches(b, steps=range(STRIDE)):
                pe.wait_ge(x_in[b], 64)
                pe.wait_ge(weff_placed, 8)
                xb = xs[b % 3]
                for r in steps:
                    first, last = r == 0, r == STRIDE - 1
                    pe.matmul(ps[0:CHAN, b, :], spec[:, 0, r, :], xb[:, 0:NM, r, :], start=first, stop=last)
                    pe.matmul(ps[CHAN:P, b, :], spec[:, 1, r, :], xb[:, 0:NM, r, :], start=first, stop=False)
                    mm = pe.matmul(ps[CHAN:P, b, :], spec[:, 2, r, :], xb[:, 1:NM + 1, r, :], start=False, stop=last)
                if last:
                    mm.then_inc(patches_ready, 1)

            def one(bank, lhsT, rhs, rows=slice(0, P)):
                return pe.matmul(ps[rows, bank, :], lhsT, rhs, start=True, stop=True)

            def mixer_norm(p):
                pe.wait_ge(h_ready, 4 * (p + 1))
                for c in range(2):
                    if p:
                        pe.wait_ge(g_ready, c + 1)
                    one(4 + c, par("center"), cut(H[:, p, :], c)).then_inc(centered, 1)
                for c in range(2):
                    pe.wait_ge(sq_ready, 2 * p + c + 1)
                    if p:
                        pe.wait_ge(o_ready, c + 1)
                    one(6 + c, par("chan_mean"), cut(sq, c)).then_inc(var_ready, 1)
                for c in range(2):
                    pe.wait_ge(hn_ready, 2 * p + c + 1)
                    one(4 + c, par("in_x"), cut(hn, c)).then_inc(xp_ready, 1)
                    one(6 + c, par("in_r"), cut(hn, c)).then_inc(res_ready, 1)

            def mixer_out(p):
                rows = slice(32 * p, 32 * p + 32)
                for c in range(2):
                    pe.wait_ge(xconv_ready, 2 * p + c + 1)
                    one(4 + c, par("ssm_dt"), cut(xconv, c), rows)
                    pe.wait_ge(sres_ready, 2 * p + c + 1)
                    one(6 + c, par("ssm_B"), cut(xconv, c), rows).then_inc(ssm_ready, 1)
                if p == 0:
                    patches(2, later)
                    patches(3)
                for c in range(2):
                    pe.wait_ge(y_ready, 2 * p + c + 1)
                    one(4 + c, par("ssm_C", rows), cut(y, c)[rows]).then_inc(cy_ready, 1)
                for c in range(2):
                    pe.wait_ge(g_ready, 2 * p + c + 1)
                    one(6 + c, par("out_w"), cut(gated, c)).then_inc(outw_ready, 1)

            patches(0)
            patches(1)
            pe.wait_ge(params_in, 16)
            sooner, later = range(STRIDE // 2), range(STRIDE // 2, STRIDE)
            mixer_norm(0)
            patches(2, sooner)
            mixer_out(0)
            mixer_norm(1)
            mixer_out(1)

            pe.wait_ge(tot_ready, 1)
            pe.matmul(ps[:, 4, 0:1], par("bn_mean"), tot, start=True, stop=True).then_inc(bnmean_ready, 1)
            pe.wait_ge(vtot_ready, 1)
            pe.matmul(ps[:, 5, 0:1], par("bn_mean"), vtot, start=True, stop=True).then_inc(bnvar_ready, 1)

            for u in range(UNITS):
                pe.wait_ge(h2_ready, u + 1)
                one(u, par("center"), cut(H[:, u // 2, :], u % 2)).then_inc(centered2, 1)
            for u in range(UNITS):
                pe.wait_ge(sq2_ready, u + 1)
                one(4 + u, par("chan_mean"), cut(sq2[u // 2], u % 2)).then_inc(var2_ready, 1)
            def values():
                pe.wait_ge(hr_ready, UNITS)
                pe.wait_ge(rot_taken, 10)
                for half in range(2):
                    hrows = slice(CHAN * half, CHAN * (half + 1))
                    for u in range(UNITS):
                        for j in range(4):
                            t0 = HALF * (u % 2) + P * j
                            mm = pe.matmul(ps[:, 3 + half, P * u + 32 * j:P * u + 32 * (j + 1)],
                                           hr[u // 2][hrows, t0:t0 + P], par("wv", hrows), start=True, stop=True)
                    mm.then_inc(v_ready, 1)

            for i, (kind, p, c) in enumerate(rot_items):
                bank = rot_bank(i)
                if i < 2:
                    pe.wait_ge(logs_ready, 4 * i + 4)
                elif i < 4:
                    pe.wait_ge(normed_ready, 2 * i - 2)
                else:
                    pe.wait_ge(rot_taken, 2 * (i - 4) + 2)
                if kind == "q":
                    pe.wait_ge(hr_ready, 2 * p + c + 1)
                    one(bank, par("wq"), cut(hr[p], c))
                    one(bank + 1, par("wq_rot"), cut(hr[p], c)).then_inc(rot_ready, 1)
                else:
                    pe.wait_ge(hr_ready, UNITS - 1 + c)
                    for at, name in ((bank, "wk"), (bank + 1, "wk_rot")):
                        for pair in range(PAIRS):
                            mm = one(at, par(name), cut(hr[pair], c), slice(64 * pair, 64 * pair + 64))
                    mm.then_inc(rot_ready, 1)
            values()

            pe.wait_ge(masks_in, 16)
            pe.wait_ge(rot_taken, 2 * len(rot_items))
            ident_b, mask_ts, mask_st = masks[:, 0, :], masks[:, 1, :], masks[:, 2, :]

            def max_slot(slot):
                kind, b, i = slots[slot]
                bank = slot % 3
                if slot >= 3:
                    last_kind, last_b, last_i = slots[slot - 3]
                    if last_kind == "turn":
                        pe.wait_ge(maxima_placed, 4 * last_b + 2 * last_i + 2)
                    elif last_kind == "den":
                        pe.wait_ge(den_log, den_index(last_b, last_i) + 1)
                    else:
                        pe.wait_ge(maxed, NU * last_b + last_i + 1)
                if kind == "den":
                    pe.wait_ge(o_out, 2 * b + i + 1)
                    one(bank, par("den_sel"), cut(attn_o[b], i)).then_inc(den_ready, 1)
                    return
                if kind == "turn":
                    pe.wait_ge(negmax_ready, 4 * b + 2 * i + 2)
                    for j in range(4):
                        mm = pe.matmul(ps[96:104, bank, P * j:P * (j + 1)],
                                       negmax[:, i, j].rearrange("p h part -> p (h part)").bitcast(F32), par("ident"),
                                       start=True, stop=True)
                    mm.then_inc(max_turned, 1)
                    return
                if i == 0:
                    pe.wait_ge(keys_in[b % 2], 16 * 12 * (b // 2 + 1))
                    pe.wait_ge(queries_in[b], 16 * 3 * KV)
                tb, s0, ns, h0, nh = units[i]
                diag = s0 + ns == tb + 1
                if diag:
                    pe.matmul(ps[:, bank, 0:nh * ns * P].rearrange("p (h s) -> p h s", h=nh)[:, :, (ns - 1) * P:],
                              ident_b, mask_ts.rearrange("p (h s) -> p h s", h=1).broadcast_to([P, nh, P]),
                              start=True, stop=False, skip_group_check=True)
                for n in range(nh):
                    h = HEAD_ORDER[h0 + n]
                    at = n * ns * P
                    kt = KT[0:96, b % 2, h, P * s0:P * (s0 + ns)]
                    mm = pe.matmul(ps[:, bank, at:at + ns * P], QT[0:96, b % 2, h // 2, P * tb:P * (tb + 1)], kt,
                                   start=not diag, stop=True, skip_group_check=diag)
                mm.then_inc(scores_ready, 1)

            def prob_unit(b, gi, g):
                half, j = groups[gi]
                n = 2 * (NG * b + gi) + g
                bank = 3 + 2 * (n % 2)
                t0, t1 = max(HALF * half, P * j), HALF * (half + 1)
                if n == 0:
                    pe.wait_ge(v_placed, 4)
                if g == 0 and j == 0:
                    pe.wait_ge(maxima_placed, 4 * b + 2 * half + 2)
                if n >= 2:
                    pe.wait_ge(probs_ready, n - 1)
                diag = t0 == P * j
                if diag:
                    for a in range(2):
                        pe.matmul(ps[:, bank + a, 0:P], ident_b, mask_st, start=True, stop=False, skip_group_check=True)
                for a in range(2):
                    mm = pe.matmul(ps[:, bank + a, 0:t1 - t0], KT[0:104, b % 2, 2 * g + a, P * j:P * (j + 1)],
                                   QT[0:104, b % 2, g, t0:t1], start=not diag, stop=True, skip_group_check=diag)
                mm.then_inc(logits_t, 1)

            def pv_group(G):
                b, gi = divmod(G, NG)
                half, j = groups[gi]
                t0, t1 = max(HALF * half, P * j), HALF * (half + 1)
                pe.wait_ge(probs_ready, 2 * G + 2)
                if j == 0 and G:
                    pe.wait_ge(o_out, 2 * b + half)
                for h in range(HEADS):
                    mm = pe.matmul(ps[32 * h:32 * h + 32, 7, t0 - HALF * half:HALF], V[:, b, j, h // 2, :],
                                   PT[:, G % 4, h, 0:t1 - t0], start=(j == 0), stop=(j == (SBLK - 1 if half else SBLK // 2 - 1)))
                mm.then_inc(pv_done, 1)

            def side_free(i):
                if side_before[i] is None:
                    if i < NSA:
                        pe.wait_ge(maxed, NU * BATCH)
                        pe.wait_ge(maxima_placed, 4 * BATCH)
                    return
                name, p, c = side_order[side_before[i]]
                if name == "den":
                    pe.wait_ge(rden_ready, den_index(p, c) + 1)
                elif name == "wo":
                    pe.wait_ge(x1_ready, 2 * p + c + 1)
                elif name == "var":
                    pe.wait_ge(inv3_ready, 2 * p + c + 1)
                elif name == "route":
                    pe.wait_ge(rdiff, p + 1)
                elif name == "turn":
                    pe.wait_ge(wT_out, p + 1)

            def side(i):
                name, p, c = side_order[i]
                bank = side_bank[i]
                if name == "pick":
                    return
                side_free(i)
                if name == "den":
                    pe.wait_ge(o_out, 2 * p + c + 1)
                    one(bank, par("den_sel"), cut(attn_o[p], c)).then_inc(den_ready, 1)
                elif name == "wo":
                    for half in range(2):
                        n = den_index(2 * p + half, c)
                        pe.wait_ge(attn_ready, n + 1)
                        mm = one(bank, par("wo"), cut(attn_o[2 * p + half], c), slice(CHAN * half, CHAN * (half + 1)))
                    mm.then_inc(wo_ready, 1)
                elif name == "var":
                    pe.wait_ge(sq3_ready, 2 * p + c + 1)
                    one(bank, par("chan_mean"), cut(sq3, c)).then_inc(var3_ready, 1)
                elif name == "route":
                    pe.wait_ge(flat_ready, 2 * p + 2)
                    for j in range(SBLK):
                        mm = pe.matmul(ps[:, bank, 16 * j:16 * (j + 1)], flat[:, P * j:P * (j + 1)], par("router"),
                                       start=True, stop=True)
                    mm.then_inc(logit_ready, 1)
                elif name == "turn":
                    pe.wait_ge(rw_ready, p + 1)
                    pe.transpose(ps[:, bank, 0:P], rt[6].rearrange("p n e -> p (n e)"), par("ident")).then_inc(wT_ready, 1)

            at = 0
            while at < ready_at:
                max_slot(at)
                at += 1
            for b in range(BATCH):
                for gi in range(NG):
                    for g in range(KV):
                        k = 2 * gi + g
                        prob_unit(b, gi, g)
                        while at < slots_until(b, k):
                            max_slot(at)
                            at += 1
                        for i in attn_at.get((b, k), []):
                            side(i)
                    G = NG * b + gi
                    if G:
                        pv_group(G - 1)
            pv_group(NG * BATCH - 1)

            pe.wait_ge(w_split, 3)
            pe.wait_ge(w2_in, 16)
            pe.wait_ge(wT_out, 1)
            pe.wait_ge(rden_ready, 7)
            w1h, w1l, w3h = (w.rearrange("p (q i c) -> p q i c", q=EPAIRS, i=HTILES) for w in (w1_high, w1_low, w3_high))
            w3l = [w.rearrange("p (q i c) -> p q i c", q=EPAIRS // 2, i=HTILES) for w in w3_low]

            def up(n):
                m, i = divmod(n, HTILES)
                k, q = divmod(m, EPAIRS)
                if i == 0 and q == 0 and k % 2 == 0:
                    pe.wait_ge(tok_in[k // 2], 32)
                tk = cut(toks[k // 2], k % 2)
                if n >= 2:
                    pe.wait_ge(silu_ready, n - 1)
                pe.matmul(ps[:, n % 2, :], w1h[:, q, i, :], tk, start=True, stop=False)
                pe.matmul(ps[:, n % 2, :], w1l[:, q, i, :], tk, start=False, stop=True).then_inc(h1_ready, 1)
                if n >= 2:
                    pe.wait_ge(hid_ready, n - 1)
                pe.matmul(ps[:, 2 + n % 2, :], w3h[:, q, i, :], tk, start=True, stop=False)
                pe.matmul(ps[:, 2 + n % 2, :], w3l[q // 2][:, q % 2, i, :], tk, start=False, stop=True).then_inc(h3_ready, 1)

            def down(t, i, odd, start, stop):
                m = t // HTILES
                rows = slice(CHAN, P) if odd else slice(0, CHAN)
                return pe.matmul(ps[rows, 4 + m % 2, :], w2[:, m % EPAIRS, i + odd, :], hid[:, t % 4, :], start=start, stop=stop)

            total = CHUNKS * EPAIRS * HTILES

            def downs(t):
                m, i = divmod(t, HTILES)
                if i == 2 and t < total - 1:
                    return
                pe.wait_ge(hid_ready, t + 1)
                if i == 0:
                    if m:
                        down(t - 1, 2, 1, False, True).then_inc(y2_ready, 1)
                    if m >= 2:
                        pe.wait_ge(gy_ready, m - 1)
                    down(t, 0, 0, True, False).then_inc(hid_used, 1)
                elif i == 1:
                    down(t, 1, 0, False, True)
                    down(t, 1, 1, True, False).then_inc(hid_used, 1)
                else:
                    down(t, 2, 1, False, True).then_inc(y2_ready, 1)

            def finish(k):
                pe.wait_ge(acc_step, 4 * (k + 1))
                if k:
                    pe.wait_ge(fin_out, k)
                else:
                    pe.wait_ge(rdiff, PAIRS)
                for blk in range(4):
                    mm = pe.matmul(ps[:, 6, CHAN * blk:CHAN * (blk + 1)], acc[:, k % 2, P * blk:P * (blk + 1)],
                                   par("ident2"), start=True, stop=True)
                mm.then_inc(fin_ready, 1)

            per_chunk = EPAIRS * HTILES
            for n in range(total + 2):
                if n < total:
                    up(n)
                if n >= 2:
                    downs(n - 2)
                if n > per_chunk and n % per_chunk == 8:
                    finish(n // per_chunk - 1)
                for i in moe_at[0].get(n, []):
                    side(i)
            finish(CHUNKS - 1)


def _pair_diag(m):
    r, c = m.shape
    z = np.zeros((2 * r, 2 * c), np.float32)
    z[:r, :c] = m
    z[r:, c:] = m
    return z


def _constants():
    k = np.arange(PATCH)
    f = np.arange(NFREQ)[:, None]
    ang = 2.0 * np.pi * f * k / PATCH
    dft = np.concatenate([np.cos(ang), -np.sin(ang)], 0) / np.sqrt(PATCH)
    dft = np.kron(np.eye(OGRP), dft)
    inv_freq = 1.0 / 10000.0 ** (np.arange(0, HD, 2, dtype=np.float32) / HD)
    freqs = np.outer(np.arange(TOK, dtype=np.float32), inv_freq)
    emb = np.concatenate([freqs, freqs], axis=-1).astype(np.float32)
    sign = np.where(np.arange(HD) < HD // 2, -1.0, 1.0)[:, None]
    rope = np.stack([np.tile(np.cos(emb).T, (P // HD, 1)), np.tile(sign * np.sin(emb).T, (P // HD, 1))])
    i = np.arange(P)
    masks = np.stack([np.eye(P), np.where(i[None, :] > i[:, None], NEG, 0.0), np.where(i[None, :] < i[:, None], NEG, 0.0)])
    eye64 = np.eye(CHAN)
    chan_mean = _pair_diag(np.full((CHAN, CHAN), 1.0 / CHAN))
    den_sel = np.zeros((P, P))
    for h in range(HEADS):
        den_sel[32 * h + HD, 32 * h:32 * h + 32] = 1.0
    head_rows = np.zeros((P, HEADS))
    for o, h in enumerate(HEAD_ORDER):
        head_rows[96 + 2 * o:98 + 2 * o, h] = 1.0
    return {"head_rows": head_rows, "dft": dft, "rope": rope, "masks": masks, "center": np.eye(P) - chan_mean, "chan_mean": chan_mean,
            "bn_mean": np.tile(eye64, (2, 2)) / (BATCH * TOK), "den_sel": den_sel, "ident": np.eye(P),
            "ident2": np.tile(eye64, (2, 1)),
            "expert_id": np.tile(np.arange(EXPERTS) - float(EXPERTS), (P, 1)),
            "eps5": np.full((P, 1), EPS_LN), "eps6": np.full((P, 1), EPS_RMS), "eps56": np.full((P, 1), EPS_LN * EPS_RMS)}


def kernel(**inputs):
    import ml_dtypes
    import concourse.bacc as _bacc
    from concourse import mybir as _mybir
    from concourse.bass_utils import run_bass_kernel_spmd as _run

    a = {k: np.asarray(v) for k, v in inputs.items()}
    const = _constants()
    cols, total = param_columns()
    block = np.zeros((P, total), np.float32)

    def put(name, value):
        at, w = cols[name]
        block[:value.shape[0], at:at + w] = value

    def twice(v):
        v = v.reshape(CHAN, -1)
        return np.concatenate([v, v], 0)

    half = HD // 2
    rot = np.concatenate([np.arange(HD * n + half, HD * (n + 1)).tolist() + np.arange(HD * n, HD * n + half).tolist()
                          for n in range(HEADS)]).astype(int)
    in_w, in_b = a["L0_attn_in_w"], a["L0_attn_in_b"]
    put("in_x", _pair_diag(in_w[:CHAN].T))
    put("in_r", _pair_diag(in_w[CHAN:].T))
    put("ssm_dt", _pair_diag(a["L0_attn_dt"]))
    put("ssm_B", _pair_diag(a["L0_attn_B_w"].T))
    put("ssm_C", np.concatenate([_pair_diag(a["L0_attn_C_w"].T)] * 2, 0))
    put("out_w", _pair_diag(a["L0_attn_out_w"].T))
    wq, wk = a["L0_ffn_wq"], a["L0_ffn_wk"]
    put("wq", _pair_diag(wq.T))
    put("wq_rot", _pair_diag(wq[rot].T))
    put("wk", _pair_diag(wk.T))
    put("wk_rot", _pair_diag(wk[rot[:KV * HD]].T))
    put("wv", twice(a["L0_ffn_wv"].T))
    wo = np.zeros((P, CHAN), np.float32)
    for h in range(HEADS):
        wo[32 * h:32 * h + HD] = a["L0_ffn_wo"][:, HD * h:HD * (h + 1)].T
    put("wo", wo)
    put("router", _pair_diag(a["L0_ffn_router_w"].T))
    put("conv_w", twice(a["L0_attn_conv_w"]))
    for name, v in (("conv_b", a["L0_attn_conv_b"]), ("in_b_x", in_b[:CHAN]), ("in_b_r", in_b[CHAN:]),
                    ("out_b", a["L0_attn_out_b"]), ("gamma", a["L0_attn_gamma"]), ("beta", a["L0_attn_beta"]),
                    ("ln1", a["L0_ffn_ln1_w"]), ("ln2", a["L0_ffn_ln2_w"])):
        put(name, twice(v))
    for name in ("center", "chan_mean", "bn_mean", "den_sel", "ident", "ident2", "expert_id", "eps5", "eps6", "eps56", "head_rows"):
        put(name, const[name])

    def hidden(w):
        t = np.zeros((CHAN, EPAIRS, HTILES * P), np.float32)
        for e in range(EXPERTS):
            t[:, e // 2, HID * (e % 2):HID * (e % 2 + 1)] = w[e].T
        return t.reshape(CHAN, -1)

    w2 = a["L0_ffn_w2"]
    w2t = np.zeros((P, EPAIRS, 4, CHAN), np.float32)
    for q in range(EPAIRS):
        even, odd = w2[2 * q].T, w2[2 * q + 1].T
        cut = P - REST
        w2t[:, q, 0] = even[:P]
        w2t[:REST, q, 1] = even[P:]
        w2t[REST:, q, 2] = odd[:cut]
        w2t[:HID - cut, q, 3] = odd[cut:]
    arrays = {
        "x": a["x"],
        "tok_W": a["L0_tok_W"].reshape(-1, 2, OGRP, 2 * NFREQ, CHAN).transpose(2, 3, 0, 1, 4).reshape(2 * NFREQ * OGRP, -1), "params": block, "dft": const["dft"].astype(np.float32),
        "rope": const["rope"].astype(np.float32), "masks": const["masks"].astype(ml_dtypes.bfloat16),
        "w1": hidden(a["L0_ffn_w1"]), "w3": hidden(a["L0_ffn_w3"]), "w2": w2t.reshape(P, -1),
    }
    nc = _bacc.Bacc("TRN2", target_bir_lowering=False, num_devices=1)
    feed, args = {}, []
    for name, v in arrays.items():
        v = np.ascontiguousarray(v)
        feed[f"in_{name}"] = v
        args.append(nc.dram_tensor(f"in_{name}", v.shape, _mybir.dt.from_np(v.dtype), kind="ExternalInput").ap())
    args.append(nc.dram_tensor("out_0", (BATCH, TOK, CHAN), F32, kind="ExternalOutput").ap())
    vit_tower(nc, *args)
    r = _run(nc, [feed], core_ids=[0])
    return r.results[0]["out_0"]
```
